# Optimizing a Trainium2 kernel written in Bass

```python
import numpy as np
import jax
import jax.numpy as jnp

def _softmax(x, axis=-1):
    return jax.nn.softmax(x, axis=axis)

def _gelu(x):
    return jax.nn.gelu(x, approximate=True)

def _silu(x):
    return jax.nn.silu(x)

def _sigmoid(x):
    return jax.nn.sigmoid(x)

def _layernorm(x, axis=-1, eps=1e-05):
    m = jnp.mean(x, axis=axis, keepdims=True)
    v = jnp.var(x, axis=axis, keepdims=True)
    return (x - m) / jnp.sqrt(v + eps)

def _scatter_add(tgt, idx, src, axis=0):
    return tgt.at[idx].add(src)

def _segment_sum(src, seg, n):
    return jax.ops.segment_sum(src, seg, n)
kernel_name = 'mk_macaron_d2_jaxref_r8_fa707e'

def setup_inputs(seed: int=0):
    np.random.seed(seed)
    _w = jnp.asarray

    def _L0_attn_setup():
        import jax, jax.numpy as jnp
        import numpy as np
        B, L, E, D, H = (2, 256, 128, 128, 8)

        def _ln(x, g, b, eps=1e-05):
            m = jnp.mean(x, axis=-1, keepdims=True)
            v = jnp.mean((x - m) ** 2, axis=-1, keepdims=True)
            return (x - m) * jax.lax.rsqrt(v + eps) * g + b
        key = jax.random.key(seed)
        ks = jax.random.split(key, 10)
        s = 0.02

        def n(k, shape):
            return jax.random.normal(k, shape, jnp.float32) * s
        return {'emb': jax.random.normal(ks[0], (B, L, E), jnp.float32), 'Wa_w': n(ks[1], (H, D, E)), 'Wa_b': jnp.zeros((H, D), jnp.float32), 'Wb_w': n(ks[2], (H, D, E)), 'Wb_b': jnp.zeros((H, D), jnp.float32), 'C_w': n(ks[3], (H, D, D)), 'C_b': jnp.zeros((H, D), jnp.float32), 'D_w': n(ks[4], (D, E)), 'D_b': jnp.zeros((D,), jnp.float32), 'Wout_w': n(ks[5], (E, D)), 'Wout_b': jnp.zeros((E,), jnp.float32), 'hn_g': jnp.ones((H, D), jnp.float32), 'hn_b': jnp.zeros((H, D), jnp.float32), 'head_w': jnp.ones((H,), jnp.float32), 'ffn1_w': n(ks[6], (4 * E, E)), 'ffn1_b': jnp.zeros((4 * E,), jnp.float32), 'ffn2_w': n(ks[7], (E, 4 * E)), 'ffn2_b': jnp.zeros((E,), jnp.float32), 'proj_w': n(ks[8], (E, E)), 'proj_b': jnp.zeros((E,), jnp.float32), 'norm_g': jnp.ones((E,), jnp.float32), 'norm_b': jnp.zeros((E,), jnp.float32)}
    _L0_attn_in = _L0_attn_setup()

    def _L0_ffn_setup():
        import jax, jax.numpy as jnp
        import numpy as np
        import math
        N_EMBD = 128
        HIDDEN = 4 * N_EMBD
        N_EXPERTS = 8
        TOP_K = 2
        B, T = (4, 256)

        def new_gelu(x):
            c = math.sqrt(2.0 / math.pi)
            return 0.5 * x * (1.0 + jnp.tanh(c * (x + 0.044715 * x * x * x)))

        def _moe_forward(x, Wfc_s, bfc_s, Wproj_s, bproj_s, Wr, Wfc, bfc, Wproj, bproj):
            Bb, Tt, C = x.shape
            xf = x.reshape(Bb * Tt, C)
            N = Bb * Tt
            shared = new_gelu(xf @ Wfc_s + bfc_s) @ Wproj_s + bproj_s
            logits = xf @ Wr
            probs = jax.nn.softmax(logits, axis=-1)
            topk_p, topk_i = jax.lax.top_k(probs, TOP_K)
            topk_p = topk_p / jnp.sum(topk_p, axis=-1, keepdims=True)
            gate = jnp.zeros((N, N_EXPERTS), dtype=xf.dtype)
            gate = gate.at[jnp.arange(N)[:, None], topk_i].add(topk_p)
            routed = jnp.zeros_like(xf)
            for e in range(N_EXPERTS):
                h = new_gelu(xf @ Wfc[e] + bfc[e]) @ Wproj[e] + bproj[e]
                routed = routed + h * gate[:, e:e + 1]
            return (shared + routed).reshape(Bb, Tt, C)
        key = jax.random.key(seed)
        ks = jax.random.split(key, 10)
        s = 0.02
        return {'x': jax.random.normal(ks[0], (B, T, N_EMBD), dtype=jnp.float32), 'Wfc_s': jax.random.normal(ks[1], (N_EMBD, HIDDEN), dtype=jnp.float32) * s, 'bfc_s': jnp.zeros((HIDDEN,), dtype=jnp.float32), 'Wproj_s': jax.random.normal(ks[2], (HIDDEN, N_EMBD), dtype=jnp.float32) * s, 'bproj_s': jnp.zeros((N_EMBD,), dtype=jnp.float32), 'Wr': jax.random.normal(ks[3], (N_EMBD, N_EXPERTS), dtype=jnp.float32) * s, 'Wfc': jax.random.normal(ks[4], (N_EXPERTS, N_EMBD, HIDDEN), dtype=jnp.float32) * s, 'bfc': jnp.zeros((N_EXPERTS, HIDDEN), dtype=jnp.float32), 'Wproj': jax.random.normal(ks[5], (N_EXPERTS, HIDDEN, N_EMBD), dtype=jnp.float32) * s, 'bproj': jnp.zeros((N_EXPERTS, N_EMBD), dtype=jnp.float32)}
    _L0_ffn_in = _L0_ffn_setup()

    def _L1_attn_setup():
        import jax, jax.numpy as jnp
        import numpy as np
        B, T, D, H = (2, 256, 128, 16)
        HD = D // H
        key = jax.random.key(seed)
        ks = jax.random.split(key, 9)
        s = 1.0 / np.sqrt(D)
        return {'x': jax.random.normal(ks[0], (B, T, D), dtype=jnp.float32), 'Wq': jax.random.uniform(ks[1], (D, D), minval=-s, maxval=s, dtype=jnp.float32), 'bq': jax.random.uniform(ks[2], (D,), minval=-s, maxval=s, dtype=jnp.float32), 'Wk': jax.random.uniform(ks[3], (D, D), minval=-s, maxval=s, dtype=jnp.float32), 'bk': jax.random.uniform(ks[4], (D,), minval=-s, maxval=s, dtype=jnp.float32), 'Wv': jax.random.uniform(ks[5], (D, D), minval=-s, maxval=s, dtype=jnp.float32), 'bv': jax.random.uniform(ks[6], (D,), minval=-s, maxval=s, dtype=jnp.float32), 'Wo': jax.random.uniform(ks[7], (D, D), minval=-s, maxval=s, dtype=jnp.float32), 'bo': jax.random.uniform(ks[8], (D,), minval=-s, maxval=s, dtype=jnp.float32)}
    _L1_attn_in = _L1_attn_setup()

    def _L1_ffn_setup():
        import jax, jax.numpy as jnp
        import numpy as np
        EPS = 1e-05

        def _quantize(W):
            gamma = jnp.mean(jnp.abs(W))
            return jnp.clip(jnp.round(W / (gamma + EPS)), -1.0, 1.0)
        key = jax.random.key(seed)
        k_x, k_w1, k_b1, k_w2, k_b2 = jax.random.split(key, 5)
        n_embd = 128
        d_ff = 4 * n_embd
        B, S = (4, 512)
        bound1 = 1.0 / np.sqrt(n_embd)
        bound2 = 1.0 / np.sqrt(d_ff)
        x = jax.random.normal(k_x, (B, S, n_embd), dtype=jnp.float32)
        W1 = jax.random.uniform(k_w1, (d_ff, n_embd), jnp.float32, -bound1, bound1)
        b1 = jax.random.uniform(k_b1, (d_ff,), jnp.float32, -bound1, bound1)
        W2 = jax.random.uniform(k_w2, (n_embd, d_ff), jnp.float32, -bound2, bound2)
        b2 = jax.random.uniform(k_b2, (n_embd,), jnp.float32, -bound2, bound2)
        return {'x': x, 'W1': W1, 'b1': b1, 'W2': W2, 'b2': b2}
    _L1_ffn_in = _L1_ffn_setup()
    _d = {'L0_attn_emb': _L0_attn_in['emb'], 'L0_attn_Wa_w': _L0_attn_in['Wa_w'], 'L0_attn_Wa_b': _L0_attn_in['Wa_b'], 'L0_attn_Wb_w': _L0_attn_in['Wb_w'], 'L0_attn_Wb_b': _L0_attn_in['Wb_b'], 'L0_attn_C_w': _L0_attn_in['C_w'], 'L0_attn_C_b': _L0_attn_in['C_b'], 'L0_attn_D_w': _L0_attn_in['D_w'], 'L0_attn_D_b': _L0_attn_in['D_b'], 'L0_attn_Wout_w': _L0_attn_in['Wout_w'], 'L0_attn_Wout_b': _L0_attn_in['Wout_b'], 'L0_attn_hn_g': _L0_attn_in['hn_g'], 'L0_attn_hn_b': _L0_attn_in['hn_b'], 'L0_attn_head_w': _L0_attn_in['head_w'], 'L0_attn_ffn1_w': _L0_attn_in['ffn1_w'], 'L0_attn_ffn1_b': _L0_attn_in['ffn1_b'], 'L0_attn_ffn2_w': _L0_attn_in['ffn2_w'], 'L0_attn_ffn2_b': _L0_attn_in['ffn2_b'], 'L0_attn_proj_w': _L0_attn_in['proj_w'], 'L0_attn_proj_b': _L0_attn_in['proj_b'], 'L0_attn_norm_g': _L0_attn_in['norm_g'], 'L0_attn_norm_b': _L0_attn_in['norm_b'], 'L0_ffn_Wfc_s': _L0_ffn_in['Wfc_s'], 'L0_ffn_bfc_s': _L0_ffn_in['bfc_s'], 'L0_ffn_Wproj_s': _L0_ffn_in['Wproj_s'], 'L0_ffn_bproj_s': _L0_ffn_in['bproj_s'], 'L0_ffn_Wr': _L0_ffn_in['Wr'], 'L0_ffn_Wfc': _L0_ffn_in['Wfc'], 'L0_ffn_bfc': _L0_ffn_in['bfc'], 'L0_ffn_Wproj': _L0_ffn_in['Wproj'], 'L0_ffn_bproj': _L0_ffn_in['bproj'], 'L1_attn_Wq': _L1_attn_in['Wq'], 'L1_attn_bq': _L1_attn_in['bq'], 'L1_attn_Wk': _L1_attn_in['Wk'], 'L1_attn_bk': _L1_attn_in['bk'], 'L1_attn_Wv': _L1_attn_in['Wv'], 'L1_attn_bv': _L1_attn_in['bv'], 'L1_attn_Wo': _L1_attn_in['Wo'], 'L1_attn_bo': _L1_attn_in['bo'], 'L1_ffn_W1': _L1_ffn_in['W1'], 'L1_ffn_b1': _L1_ffn_in['b1'], 'L1_ffn_W2': _L1_ffn_in['W2'], 'L1_ffn_b2': _L1_ffn_in['b2']}
    _x0 = _d['L0_attn_emb']
    _d['L0_attn_emb'] = jax.random.normal(jax.random.fold_in(jax.random.key(seed), 1), (4, 1024, 128), dtype=_x0.dtype)
    del _x0
    return _d

def reference(L0_attn_emb, L0_attn_Wa_w, L0_attn_Wa_b, L0_attn_Wb_w, L0_attn_Wb_b, L0_attn_C_w, L0_attn_C_b, L0_attn_D_w, L0_attn_D_b, L0_attn_Wout_w, L0_attn_Wout_b, L0_attn_hn_g, L0_attn_hn_b, L0_attn_head_w, L0_attn_ffn1_w, L0_attn_ffn1_b, L0_attn_ffn2_w, L0_attn_ffn2_b, L0_attn_proj_w, L0_attn_proj_b, L0_attn_norm_g, L0_attn_norm_b, L0_ffn_Wfc_s, L0_ffn_bfc_s, L0_ffn_Wproj_s, L0_ffn_bproj_s, L0_ffn_Wr, L0_ffn_Wfc, L0_ffn_bfc, L0_ffn_Wproj, L0_ffn_bproj, L1_attn_Wq, L1_attn_bq, L1_attn_Wk, L1_attn_bk, L1_attn_Wv, L1_attn_bv, L1_attn_Wo, L1_attn_bo, L1_ffn_W1, L1_ffn_b1, L1_ffn_W2, L1_ffn_b2):

    def _L0_attn_ref(emb, Wa_w, Wa_b, Wb_w, Wb_b, C_w, C_b, D_w, D_b, Wout_w, Wout_b, hn_g, hn_b, head_w, ffn1_w, ffn1_b, ffn2_w, ffn2_b, proj_w, proj_b, norm_g, norm_b):
        import jax, jax.numpy as jnp
        import numpy as np
        B, L, E, D, H = (2, 256, 128, 128, 8)

        def _ln(x, g, b, eps=1e-05):
            m = jnp.mean(x, axis=-1, keepdims=True)
            v = jnp.mean((x - m) ** 2, axis=-1, keepdims=True)
            return (x - m) * jax.lax.rsqrt(v + eps) * g + b
        nH = head_w.shape[0]
        a = jnp.tanh(jnp.einsum('ble,hde->blhd', emb, Wa_w) + Wa_b)
        bg = jnp.einsum('ble,hde->blhd', emb, Wb_w) + Wb_b
        aT = jnp.moveaxis(a, 1, 0)
        bT = jnp.moveaxis(bg, 1, 0)

        def step(h, ab):
            at, bt = ab
            h = at * h + bt
            return (h, h)
        h0 = jnp.zeros_like(aT[0])
        _, hs = jax.lax.scan(step, h0, (aT, bT))
        hs = jnp.moveaxis(hs, 0, 1)
        Dx = emb @ D_w.T + D_b
        out = (jnp.einsum('blhd,hkd->blhk', hs, C_w) + C_b) * Dx[:, :, None, :]
        out = _ln(out, hn_g, hn_b)
        sum_heads = (Dx + jnp.einsum('h,blhd->bld', head_w, out)) / nH
        z = sum_heads @ Wout_w.T + Wout_b
        u = z + _ln(z, norm_g, norm_b)
        ffn = jax.nn.gelu(u @ ffn1_w.T + ffn1_b, approximate=False)
        h_out = u + (ffn @ ffn2_w.T + ffn2_b)
        return h_out @ proj_w.T + proj_b

    def _L0_ffn_ref(x, Wfc_s, bfc_s, Wproj_s, bproj_s, Wr, Wfc, bfc, Wproj, bproj):
        import jax, jax.numpy as jnp
        import numpy as np
        import math
        N_EMBD = 128
        HIDDEN = 4 * N_EMBD
        N_EXPERTS = 8
        TOP_K = 2
        B, T = (4, 256)

        def new_gelu(x):
            c = math.sqrt(2.0 / math.pi)
            return 0.5 * x * (1.0 + jnp.tanh(c * (x + 0.044715 * x * x * x)))

        def _moe_forward(x, Wfc_s, bfc_s, Wproj_s, bproj_s, Wr, Wfc, bfc, Wproj, bproj):
            Bb, Tt, C = x.shape
            xf = x.reshape(Bb * Tt, C)
            N = Bb * Tt
            shared = new_gelu(xf @ Wfc_s + bfc_s) @ Wproj_s + bproj_s
            logits = xf @ Wr
            probs = jax.nn.softmax(logits, axis=-1)
            topk_p, topk_i = jax.lax.top_k(probs, TOP_K)
            topk_p = topk_p / jnp.sum(topk_p, axis=-1, keepdims=True)
            gate = jnp.zeros((N, N_EXPERTS), dtype=xf.dtype)
            gate = gate.at[jnp.arange(N)[:, None], topk_i].add(topk_p)
            routed = jnp.zeros_like(xf)
            for e in range(N_EXPERTS):
                h = new_gelu(xf @ Wfc[e] + bfc[e]) @ Wproj[e] + bproj[e]
                routed = routed + h * gate[:, e:e + 1]
            return (shared + routed).reshape(Bb, Tt, C)
        return _moe_forward(x, Wfc_s, bfc_s, Wproj_s, bproj_s, Wr, Wfc, bfc, Wproj, bproj)

    def _L1_attn_ref(x, Wq, bq, Wk, bk, Wv, bv, Wo, bo):
        import jax, jax.numpy as jnp
        import numpy as np
        B, T, D, H = (2, 256, 128, 16)
        HD = D // H
        b, t, d = x.shape

        def split_heads(y):
            return y.reshape(b, t, H, HD).transpose(0, 2, 1, 3)
        Q = split_heads(x @ Wq.T + bq)
        K = split_heads(x @ Wk.T + bk)
        V = split_heads(x @ Wv.T + bv)
        Z = jnp.einsum('bhsp,bhsn->bhspn', V, K)
        Z_cum = jnp.cumsum(Z, axis=2)
        Y = jnp.einsum('bhtn,bhtpn->bhtp', Q, Z_cum)
        Y = Y.transpose(0, 2, 1, 3).reshape(b, t, d)
        return Y @ Wo.T + bo

    def _L1_ffn_ref(x, W1, b1, W2, b2):
        import jax, jax.numpy as jnp
        import numpy as np
        EPS = 1e-05

        def _quantize(W):
            gamma = jnp.mean(jnp.abs(W))
            return jnp.clip(jnp.round(W / (gamma + EPS)), -1.0, 1.0)
        Wq1 = _quantize(W1)
        Wq2 = _quantize(W2)
        h = jax.nn.relu(jnp.einsum('bsd,fd->bsf', x, Wq1) + b1)
        out = jnp.einsum('bsf,df->bsd', h, Wq2) + b2
        return out
    x = L0_attn_emb
    x = x + 0.5 * _L0_ffn_ref(_layernorm(x, axis=-1), L0_ffn_Wfc_s, L0_ffn_bfc_s, L0_ffn_Wproj_s, L0_ffn_bproj_s, L0_ffn_Wr, L0_ffn_Wfc, L0_ffn_bfc, L0_ffn_Wproj, L0_ffn_bproj)
    x = x + _L0_attn_ref(_layernorm(x, axis=-1), L0_attn_Wa_w, L0_attn_Wa_b, L0_attn_Wb_w, L0_attn_Wb_b, L0_attn_C_w, L0_attn_C_b, L0_attn_D_w, L0_attn_D_b, L0_attn_Wout_w, L0_attn_Wout_b, L0_attn_hn_g, L0_attn_hn_b, L0_attn_head_w, L0_attn_ffn1_w, L0_attn_ffn1_b, L0_attn_ffn2_w, L0_attn_ffn2_b, L0_attn_proj_w, L0_attn_proj_b, L0_attn_norm_g, L0_attn_norm_b)
    x = x + 0.5 * _L0_ffn_ref(_layernorm(x, axis=-1), L0_ffn_Wfc_s, L0_ffn_bfc_s, L0_ffn_Wproj_s, L0_ffn_bproj_s, L0_ffn_Wr, L0_ffn_Wfc, L0_ffn_bfc, L0_ffn_Wproj, L0_ffn_bproj)
    x = x + 0.5 * _L1_ffn_ref(_layernorm(x, axis=-1), L1_ffn_W1, L1_ffn_b1, L1_ffn_W2, L1_ffn_b2)
    x = x + _L1_attn_ref(_layernorm(x, axis=-1), L1_attn_Wq, L1_attn_bq, L1_attn_Wk, L1_attn_bk, L1_attn_Wv, L1_attn_bv, L1_attn_Wo, L1_attn_bo)
    x = x + 0.5 * _L1_ffn_ref(_layernorm(x, axis=-1), L1_ffn_W1, L1_ffn_b1, L1_ffn_W2, L1_ffn_b2)
    return x

_drawn_inputs = setup_inputs


def setup_inputs(seed=0):
    import zlib

    import numpy as np

    out = dict(_drawn_inputs(seed))
    spreads = {'L0_attn_Wa_b': (0.0, 0.8),
     'L0_attn_Wb_b': (0.0, 0.295),
     'L0_attn_C_b': (0.0, 0.1),
     'L0_attn_D_b': (0.0, 0.1),
     'L0_attn_Wout_b': (0.0, 0.1),
     'L0_attn_hn_g': (1.0, 0.2),
     'L0_attn_hn_b': (0.0, 0.357),
     'L0_attn_head_w': (1.0, 0.6),
     'L0_attn_ffn1_b': (0.0, 0.8),
     'L0_attn_ffn2_b': (0.0, 0.309),
     'L0_attn_proj_b': (0.0, 0.1),
     'L0_attn_norm_g': (1.0, 0.2),
     'L0_attn_norm_b': (0.0, 0.1),
     'L0_ffn_bfc_s': (0.0, 0.1),
     'L0_ffn_bproj_s': (0.0, 0.1),
     'L0_ffn_bfc': (0.0, 0.481),
     'L0_ffn_bproj': (0.0, 0.1)}
    factors = {'L0_attn_Wa_w': 3.632,
     'L0_attn_ffn1_w': 3.643,
     'L0_attn_ffn2_w': 3.416,
     'L1_attn_bo': 64.0,
     'L1_ffn_b1': 7.016,
     'L1_ffn_b2': 64.0}
    for name, (base, spread) in spreads.items():
        noise = np.random.default_rng([zlib.crc32(name.encode()), seed]).standard_normal(out[name].shape)
        drawn = base * np.exp(spread * noise) if base else spread * noise
        out[name] = jnp.asarray(drawn.astype(out[name].dtype))
    for name, factor in factors.items():
        out[name] = (out[name] * factor).astype(out[name].dtype)
    return out
```

```python
from contextlib import ExitStack

import concourse.bass as bass
from concourse import mybir

F32 = mybir.dt.float32
U32 = mybir.dt.uint32
ACT = mybir.ActivationFunctionType
ALU = mybir.AluOpType
AX_X = mybir.AxisListType.X

P = 128
EPS = 1e-5


class Steps:

    def __init__(self, eng, sem, apart):
        self.apart = apart
        self.eng, self.sem, self.total, self.turn, self.n = eng, sem, 0, 0, 0

    def done(self, ins):
        ins.then_inc(self.sem, 1)
        self.n += 1

    def wait(self):
        self.eng.wait_ge(self.sem, self.total + self.turn + self.n)

    def link(self, ins):
        self.done(ins)
        self.wait()

    def link_apart(self, ins):
        self.link(ins)
        self.eng.sem_inc(self.apart, 1)

    def enter(self, turn, per):
        self.total, self.n, self.turn, self.per = self.total + self.n, 0, turn * per, per

    def leave(self, turns):
        assert self.n == self.per, f"{self.n} steps a turn"
        self.total, self.turn, self.n = self.total + turns * self.per, 0, 0


def macaron_kernel(nc, t):
    E = P
    TOKENS, _ = t["x"].shape
    BATCHES = 4
    TB = 4
    TW = TB * P
    TILES = TOKENS // TW
    BLOCKS = TOKENS // P
    MLPS = t["w_up"].shape[1]
    EXPERTS = MLPS - 1
    HC = t["w_up"].shape[2] // P
    NH = t["wa"].shape[1]
    LH = 16
    HD = E // LH
    SEQ = TOKENS // BATCHES
    assert TW * TILES == TOKENS and SEQ == 2 * TW

    with ExitStack() as ctx:
        def sb(name, shape, dt=F32):
            return ctx.enter_context(nc.sbuf_tensor(name, shape, dt))

        def sem(name):
            return ctx.enter_context(nc.semaphore(name))

        def ring(tensor, n):
            return tensor[:, n]

        bank = [ctx.enter_context(nc.psum_tensor(f"bank{n}", [P, TW], F32)) for n in range(8)]

        X = sb("X", [P, BLOCKS + TB, E])
        w_up = sb("w_up_sb", [P, MLPS, HC * P])
        w_dn = sb("w_dn_sb", [P, MLPS, HC, E])
        wa = sb("wa_sb", [P, NH, P])
        wb = sb("wb_sb", [P, NH, P])
        cw = sb("cw_sb", [P, NH, P])
        squares = sb("squares_sb", [P, 7, P])
        dw, wout, proj, wq, wk, wv, wo = (squares[:, n] for n in range(7))
        wkv = squares[:, 4:6]
        f1 = sb("f1_sb", [P, HC * P])
        f2 = sb("f2_sb", [P, HC, E])
        t1 = sb("t1_sb", [P, HC * P])
        t2 = sb("t2_sb", [P, HC, E])
        COLS = t["cols"].shape[1]
        cols = sb("cols_sb", [P, COLS])
        at = [0]

        def col(n):
            at[0] += n
            return cols[:, at[0] - n:at[0]]

        b_up, b_dn, wr, ba, bb, cb, db = col(MLPS * HC), col(MLPS), col(EXPERTS), col(NH), col(NH), col(NH), col(1)
        hn_g, hn_b, f1b, f2b, bq, bk, b1, b2 = col(NH), col(NH), col(HC), col(1), col(1), col(1), col(HC), col(1)
        assert at[0] == COLS
        rows = sb("rows_sb", [P, t["rows"].shape[0]])
        woutb_row, projb_row, ng_row, nb_row, bk_row, bv_row, bo_row = (rows[:, P * n:P * n + P] for n in range(7))
        bkv_row = rows[:, 4 * P:6 * P]
        head_w = rows[:, 7 * P:7 * P + NH]

        ident = sb("ident", [P, P])
        ones = sb("ones", [P, P])
        causal = sb("causal", [P, P])
        same_head = sb("same_head", [P, P])
        head_of = sb("head_of", [P, 4])
        neg_half = sb("neg_half", [P, NH * TB])
        expert_no = sb("expert_no", [P, EXPERTS])
        keep = sb("keep", [P, TILES + 1])
        wz = sb("wz", [P, NH, P])
        zrow = sb("zrow", [P, P])

        stats = sb("stats", [P, TB, 6])
        mv = sb("mv", [P, TB, 2])
        var_eps = sb("var_eps", [P, TB])
        rstd = sb("rstd", [P, TB])
        xn = sb("xn", [P, TB, E])
        xT = sb("xT", [P, TW])
        hid = sb("hid", [P, 3 * HC, TW])
        acc = sb("acc", [P, TW])
        part = sb("part", [P, TW])
        gate_b = sb("gate_b", [P, 2, TW])

        c_dma = sem("weights_loaded")
        x_dma = sem("x_loaded")
        const_ready = sem("const_ready")
        phase_done = sem("phase_done")
        stored = sem("stored")
        dve_steps_sem, pool_steps_sem, act_steps_sem = sem("dve_step"), sem("pool_step"), sem("act_step")
        waits_apart = sem("waits_apart")
        setup_pe, setup_dve = sem("setup_pe"), sem("setup_dve")

        loads = [(squares, "squares"), (cols, "cols"), (w_up, "w_up"), (w_dn, "w_dn"), (wa, "wa"), (wb, "wb"), (cw, "cw"),
                 (f1, "f1"), (f2, "f2"), (t1, "w1"), (t2, "w2")]
        LOADED = 16 * (len(loads) + 1)

        def ln_sems(p):
            return {k: sem(f"{k}_{p}") for k in ("stats_ready", "rstd_ready", "xn_ready", "xn_turned", "xT_ready")}

        def ln_stats(dve, steps, s, i):
            for b in range(TB):
                ins = nc.vector.bn_stats(stats[:, b], X[:, bass.ds(i * TB + b, 1)])
            steps.link_apart(ins)
            for b in range(TB):
                ins = nc.vector.bn_aggr(mv[:, b], stats[:, b])
            ins.then_inc(s["stats_ready"], 1)

        def ln_rstd(pool, steps, s, i):
            pool.wait_ge(s["stats_ready"], i + 1)
            pool.sem_inc(waits_apart, 1)
            steps.link(nc.gpsimd.tensor_scalar(var_eps[:], mv[:, :, 1], EPS, None, ALU.add))
            nc.gpsimd.tensor_tensor(rstd[:], var_eps[:], neg_half[:, 0:TB], ALU.pow).then_inc(s["rstd_ready"], 1)

        def ln_apply(dve, steps, s, i, first=False):
            dve.wait_ge(s["stats_ready"], i + 1)
            dve.wait_ge(s["rstd_ready"], i + 1)
            if not first:
                dve.wait_ge(s["xn_turned"], i)
            for b in range(TB):
                ins = nc.vector.tensor_scalar(xn[:, b:b + 1], X[:, bass.ds(i * TB + b, 1)], mv[:, b, 0:1],
                                              rstd[:, b:b + 1], ALU.subtract, ALU.mult)
            ins.then_inc(s["xn_ready"], 1)

        def turn(pe, out, src):
            for b in range(TB):
                ins = nc.tensor.transpose(out[:, b * P:(b + 1) * P], src(b), ident[:])
            return ins

        def blk(ap, b):
            return ap[:, b * P:(b + 1) * P]

        logits = sb("logits", [P, TB, EXPERTS])
        top = sb("top", [P, TB, 8])
        top_at = sb("top_at", [P, TB, 8], U32)
        top_no = sb("top_no", [P, TB, 2])
        lead = sb("lead", [P, TB])
        half_tanh = sb("half_tanh", [P, TB])
        g2 = sb("g2", [P, 2, TB])
        pick = sb("pick", [P, 2, TB, EXPERTS])
        gates = sb("gates", [P, TB, EXPERTS])
        N = MLPS * HC

        def moe_sems(p):
            return ln_sems(p) | {k: sem(f"{k}_{p}") for k in (
                "logits_in", "lead_ready", "tanh_ready", "gates_ready", "up_done", "gelu_done", "gate_in", "gate_out",
                "down_done", "down_used", "acc_ready", "back_in", "tile_done")}

        UP_CREDIT, DOWN_CREDIT, USED_CREDIT, GATE_CREDIT = 3, 3, 2, 1

        def moe_pe(pe, s):
            def down(i, e):
                pe.wait_ge(s["down_used"], i * MLPS + e - 1 + USED_CREDIT)
                for c in range(HC):
                    n = e * HC + c
                    pe.wait_ge(s["gelu_done"], i * N + n + 1 + UP_CREDIT)
                    ins = nc.tensor.matmul(bank[3 + e % 2][:], w_dn[:, e, c], hid[:, n % (3 * HC)], start=(c == 0), stop=(c == HC - 1))
                ins.then_inc(s["down_done"], 1)

            with pe.Fori(0, TILES) as i:
                pe.wait_ge(s["xn_ready"], i + 1)
                pe.wait_ge(s["tile_done"], i + 1)
                turn(pe, bank[7], lambda b: xn[:, b]).then_inc(s["xn_turned"], 1)
                pe.wait_ge(s["xT_ready"], i + 1)
                for b in range(TB):
                    ins = nc.tensor.matmul(bank[6][:, b * EXPERTS:(b + 1) * EXPERTS], blk(xT, b), wr, start=True, stop=True)
                ins.then_inc(s["logits_in"], 1)
                for e in range(MLPS):
                    for c in range(HC):
                        n = e * HC + c
                        pe.wait_ge(s["gelu_done"], i * N + n - 2 + UP_CREDIT)
                        nc.tensor.matmul(bank[n % 3][:], w_up[:, e, c * P:(c + 1) * P], xT[:], start=True,
                                         stop=True).then_inc(s["up_done"], 1)
                    if e >= 1:
                        if e == 1:
                            pe.wait_ge(s["gates_ready"], i + 1)
                        pe.wait_ge(s["gate_out"], i * EXPERTS + e - 1 + GATE_CREDIT)
                        for b in range(TB):
                            ins = nc.tensor.matmul(blk(bank[5], b), gates[:, b, e - 1:e].broadcast_to([P, P]), ident[:],
                                                   start=True, stop=True)
                        ins.then_inc(s["gate_in"], 1)
                        down(i, e - 1)
                down(i, MLPS - 1)
                pe.wait_ge(s["acc_ready"], i + 1)
                turn(pe, bank[7], lambda b: blk(acc, b)).then_inc(s["back_in"], 1)

        def moe_act(act, steps, s):
            act.sem_inc(s["gelu_done"], UP_CREDIT)
            act.sem_inc(s["gate_out"], GATE_CREDIT)
            with act.Fori(0, TILES) as i:
                act.wait_ge(s["xn_turned"], i + 1)
                nc.scalar.copy(xT[:], bank[7][:]).then_inc(s["xT_ready"], 1)
                for e in range(MLPS):
                    act.wait_ge(s["down_done"], i * MLPS + e - 2 + DOWN_CREDIT)
                    for c in range(HC):
                        n = e * HC + c
                        act.wait_ge(s["up_done"], i * N + n + 1)
                        nc.scalar.activation(hid[:, n % (3 * HC)], bank[n % 3][:], ACT.Gelu_apprx_tanh,
                                             bias=b_up[:, n:n + 1]).then_inc(s["gelu_done"], 1)
                    if e == 0:
                        act.wait_ge(s["lead_ready"], i + 1)
                        nc.scalar.activation(half_tanh[:], lead[:], ACT.Tanh, scale=0.5).then_inc(s["tanh_ready"], 1)
                    else:
                        act.wait_ge(s["gate_in"], i * EXPERTS + e)
                        act.wait_ge(s["down_used"], i * MLPS + e - 1 + USED_CREDIT)
                        nc.scalar.copy(gate_b[:, e % 2], bank[5][:]).then_inc(s["gate_out"], 1)

        def moe_pool(pool, steps, s):
            ln_rstd(pool, steps, s, 0)
            steps_per = 1
            with pool.Fori(1, TILES + 1) as i:
                steps.enter(i - 1, steps_per)
                ln_rstd(pool, steps, s, i)
            steps.leave(TILES)

        def moe_dve(dve, steps, s):
            dve.sem_inc(s["down_used"], USED_CREDIT)
            dve.sem_inc(s["down_done"], DOWN_CREDIT)
            dve.sem_inc(s["tile_done"], 1)
            ln_stats(dve, steps, s, 0)
            ln_apply(dve, steps, s, 0, first=True)

            def route(i):
                dve.wait_ge(s["logits_in"], i + 1)
                steps.link_apart(nc.vector.tensor_copy(logits[:], bank[6][:, 0:TB * EXPERTS].rearrange("p (b e) -> p b e", b=TB)))
                for b in range(TB):
                    ins = nc.vector.max(top[:, b], logits[:, b])
                steps.link(ins)
                nc.vector.tensor_tensor(lead[:], top[:, :, 0], top[:, :, 1], ALU.subtract).then_inc(s["lead_ready"], 1)
                for b in range(TB):
                    ins = nc.vector.max_index(top_at[:, b], top[:, b], logits[:, b])
                steps.link(ins)
                steps.link(nc.vector.tensor_copy(top_no[:], top_at[:, :, 0:2]))
                for k in range(2):
                    ins = nc.vector.tensor_tensor(pick[:, k], expert_no[:].unsqueeze(1).broadcast_to([P, TB, EXPERTS]),
                                                  top_no[:, :, k:k + 1].broadcast_to([P, TB, EXPERTS]), ALU.is_equal)
                steps.done(ins)
                dve.wait_ge(s["tanh_ready"], i + 1)
                nc.vector.tensor_scalar(g2[:, 0], half_tanh[:], 0.5, 0.5, ALU.mult, ALU.add)
                steps.link(nc.vector.tensor_scalar(g2[:, 1], half_tanh[:], -0.5, 0.5, ALU.mult, ALU.add))
                for k in range(2):
                    ins = nc.vector.tensor_tensor(pick[:, k], pick[:, k],
                                                  g2[:, k].unsqueeze(2).broadcast_to([P, TB, EXPERTS]), ALU.mult)
                steps.link(ins)
                nc.vector.tensor_tensor(gates[:], pick[:, 0], pick[:, 1], ALU.add).then_inc(s["gates_ready"], 1)

            with dve.Fori(0, TILES) as i:
                steps.enter(i, MOE_STEPS)
                route(i)
                for e in range(MLPS):
                    dve.wait_ge(s["down_done"], i * MLPS + e + 1 + DOWN_CREDIT)
                    if e == 0:
                        ins = nc.vector.tensor_scalar(acc[:], bank[3][:], b_dn[:, 0:1], None, ALU.add)
                    else:
                        dve.wait_ge(s["gate_out"], i * EXPERTS + e + GATE_CREDIT)
                        ins = nc.vector.scalar_tensor_tensor(part[:], bank[3 + e % 2][:], b_dn[:, e:e + 1], gate_b[:, e % 2],
                                                             ALU.add, ALU.mult)
                    ins.then_inc(s["down_used"], 1)
                    dve.wait_ge(s["down_used"], i * MLPS + e + 1 + USED_CREDIT)
                    if e >= 1:
                        ins = nc.vector.tensor_tensor(acc[:], acc[:], part[:], ALU.add)
                        if e == MLPS - 1:
                            ins.then_inc(s["acc_ready"], 1)
                        else:
                            steps.link(ins)
                    if e == 3:
                        ln_stats(dve, steps, s, i + 1)
                    if e == 6:
                        ln_apply(dve, steps, s, i + 1)
                dve.wait_ge(s["back_in"], i + 1)
                tile = X[:, bass.ds(i * TB, TB)]
                nc.vector.scalar_tensor_tensor(tile.rearrange("p b e -> p (b e)"), bank[7][:], 0.5,
                                               tile.rearrange("p b e -> p (b e)"), ALU.mult, ALU.add).then_inc(s["tile_done"], 1)
            steps.leave(TILES)
            dve.wait_ge(s["tile_done"], TILES + 1)
            dve.sem_inc(phase_done, 1)

        MOE_STEPS = 15

        gain = sb("gain", [P, NH])
        head_bias = sb("head_bias", [P, 1])
        thr = sb("thr", [P, 4])
        mags = sb("mags", [P, 2])
        tern = sb("tern", [P, HC * P])
        zeros2 = sb("zeros2", [P, 2])

        def phase_setup_pool(pool, steps):
            pass

        def phase_setup_act(act, steps):
            pass

        def phase_setup_pe(pe):
            pe.wait_ge(setup_dve, 1)
            nc.tensor.matmul(bank[0][:, 0:2], ones[:], mags[:], start=True, stop=True).then_inc(setup_pe, 1)
            pe.wait_ge(setup_dve, 2)
            nc.tensor.matmul(bank[1][:, 0:P], head_bias[:].broadcast_to([P, P]), wout, start=True, stop=True).then_inc(setup_pe, 1)
            pe.wait_ge(setup_dve, 3)
            for h in range(NH):
                ins = nc.tensor.matmul(bank[2 + h // 4][:, (h % 4) * P:(h % 4 + 1) * P], ones[:], wz[:, h], start=True, stop=True)
            ins.then_inc(setup_pe, 1)

        def phase_setup_dve(dve, steps):
            v = nc.vector
            steps.link(v.tensor_scalar(tern[:], t1[:], -1.0, None, ALU.mult))
            steps.link(v.tensor_tensor(tern[:], tern[:], t1[:], ALU.max))
            steps.link(v.tensor_reduce(mags[:, 0:1], tern[:], AX_X, ALU.add))
            flat2 = t2[:].rearrange("p c e -> p (c e)")
            steps.link(v.tensor_scalar(tern[:], flat2, -1.0, None, ALU.mult))
            steps.link(v.tensor_tensor(tern[:], tern[:], flat2, ALU.max))
            v.tensor_reduce(mags[:, 1:2], tern[:], AX_X, ALU.add).then_inc(setup_dve, 1)
            dve.wait_ge(setup_pe, 1)
            steps.link(v.tensor_scalar(thr[:, 0:2], bank[0][:, 0:2], 1.0 / (HC * P), EPS, ALU.mult, ALU.add))
            steps.link(v.tensor_scalar(thr[:, 0:2], thr[:, 0:2], 0.5, None, ALU.mult))
            steps.link(v.tensor_scalar(thr[:, 2:4], thr[:, 0:2], -1.0, None, ALU.mult))
            for n, w in enumerate((t1[:], flat2)):
                steps.link(v.tensor_scalar(tern[:], w, thr[:, 2 + n:3 + n], None, ALU.is_lt))
                steps.link(v.scalar_tensor_tensor(w, w, thr[:, n:n + 1], tern[:], ALU.is_gt, ALU.subtract))
            steps.link(v.tensor_tensor(gain[:], hn_b, head_w, ALU.mult))
            steps.link(v.tensor_reduce(head_bias[:], gain[:], AX_X, ALU.add))
            steps.link(v.tensor_scalar(head_bias[:], head_bias[:], 1.0 / NH, None, ALU.mult))
            steps.link(v.tensor_tensor(gain[:], hn_g, head_w, ALU.mult))
            steps.link(v.tensor_scalar(gain[:], gain[:], 1.0 / NH, None, ALU.mult))
            dve.sem_inc(setup_dve, 1)
            dve.wait_ge(setup_pe, 2)
            steps.link(v.tensor_tensor(zrow[:], bank[1][:, 0:P], woutb_row, ALU.add))
            for h in range(NH):
                ins = v.tensor_scalar(wz[:, h], wout, gain[:, h:h + 1], None, ALU.mult)
            ins.then_inc(setup_dve, 1)
            dve.wait_ge(setup_pe, 3)
            for q in range(2):
                half = wz[:, 4 * q:4 * q + 4].rearrange("p h e -> p (h e)")
                v.tensor_tensor(half, half, bank[2 + q][:], ALU.subtract)
            steps.link(v.tensor_scalar(wout, wout, 1.0 / NH, None, ALU.mult))

        a_sb = sb("a_sb", [P, 2, TW])
        b_sb = sb("b_sb", [P, 2, TW])
        hs = sb("hs", [P, 2, TW])
        o_sb = sb("o_sb", [P, 2, TW])
        sq_sb = sb("sq_sb", [P, 2, TW])
        dx = sb("dx", [P, TW])
        carry = sb("carry", [P, NH])
        head_mean = sb("head_mean", [P, 2, TB])
        head_var = sb("head_var", [P, 2, TB])
        head_rstd = sb("head_rstd", [P, 2, TB])
        z = sb("z", [P, TB, P])
        u = sb("u", [P, TB, P])
        z_stats = sb("z_stats", [P, TB, 6])
        z_mv = sb("z_mv", [P, TB, 2])
        z_rstd = sb("z_rstd", [P, TB])
        z_var = sb("z_var", [P, TB])
        uT = sb("uT", [P, TW])
        hT = sb("hT", [P, TW])
        gelu_sb = hid

        def mix_sems():
            return ln_sems(1) | {k: sem(f"mix_{k}") for k in (
                "dx_in", "dx_ready", "ab_in", "ab_out", "hs_ready", "c_in", "o_ready", "sq_ready", "p_in", "var_ready",
                "head_rstd", "acc_done", "base_in", "base_out", "z_stats", "z_rstd", "u_ready", "u_in", "uT_ready", "f1_in", "f1_out",
                "f2_in", "hT_ready", "y_in", "tile_done")}

        def mix_pe(pe, s):
            def slot(i, n, heads, tail):
                j = i - 1
                if heads:
                    if n == 0:
                        pe.wait_ge(s["xn_ready"], i + 1)
                        turn(pe, bank[7], lambda b: xn[:, b]).then_inc(s["xn_turned"], 1)
                        pe.wait_ge(s["xT_ready"], i + 1)
                        nc.tensor.matmul(bank[6][:], dw, xT[:], start=True, stop=True).then_inc(s["dx_in"], 1)
                    if n < NH:
                        for k, w in enumerate((wa, wb)):
                            pe.wait_ge(s["ab_out"], i * 2 * NH + 2 * n + k - 1 + AB_CREDIT)
                            nc.tensor.matmul(bank[k][:], w[:, n], xT[:], start=True, stop=True).then_inc(s["ab_in"], 1)
                    if n == 1:
                        pe.wait_ge(s["dx_ready"], i + 1)
                        for b in range(TB):
                            ins = nc.tensor.matmul(blk(bank[6], b), blk(dx, b), wout, start=True, stop=True)
                        ins.then_inc(s["base_in"], 1)
                    if 1 <= n <= NH:
                        h = n - 1
                        pe.wait_ge(s["hs_ready"], i * NH + h + 1 + HS_CREDIT)
                        pe.wait_ge(s["o_ready"], i * NH + h + O_CREDIT)
                        nc.tensor.matmul(bank[2][:], cw[:, h], hs[:, h % 2], start=True, stop=True).then_inc(s["c_in"], 1)
                    if n >= 2:
                        h = n - 2
                        pe.wait_ge(s["sq_ready"], i * NH + h + 1)
                        pe.wait_ge(s["acc_done"], i * NH + h + ACC_CREDIT)
                        for b in range(TB):
                            nc.tensor.matmul(blk(bank[3], b), blk(o_sb[:, h % 2], b), wz[:, h], start=True, stop=True)
                            nc.tensor.matmul(bank[4 + h % 2][:, b:b + 1], blk(o_sb[:, h % 2], b), ones[:, 0:1], start=True, stop=True)
                            ins = nc.tensor.matmul(bank[4 + h % 2][:, TB + b:TB + b + 1], blk(sq_sb[:, h % 2], b), ones[:, 0:1],
                                                   start=True, stop=True)
                        ins.then_inc(s["p_in"], 1)
                if tail:
                    if n == 3:
                        pe.wait_ge(s["u_ready"], j + 1)
                        if heads:
                            pe.wait_ge(s["base_out"], i + 1)
                        turn(pe, bank[6], lambda b: u[:, b]).then_inc(s["u_in"], 1)
                    if n in (4, 5):
                        pe.wait_ge(s["uT_ready"], j + 1)
                        for c in (2 * n - 8, 2 * n - 7):
                            if c >= 2:
                                pe.wait_ge(s["f1_out"], j * HC + c - 1)
                            nc.tensor.matmul(bank[7 - c % 2][:], f1[:, c * P:(c + 1) * P], uT[:], start=True,
                                             stop=True).then_inc(s["f1_in"], 1)
                    if n == 6:
                        pe.wait_ge(s["f1_out"], (j + 1) * HC)
                        for c in range(HC):
                            ins = nc.tensor.matmul(bank[7][:], f2[:, c], gelu_sb[:, c], start=(c == 0), stop=(c == HC - 1))
                        ins.then_inc(s["f2_in"], 1)
                    if n == 8:
                        pe.wait_ge(s["hT_ready"], j + 1)
                        for b in range(TB):
                            ins = nc.tensor.matmul(blk(bank[6], b), blk(hT, b), proj, start=True, stop=True)
                        ins.then_inc(s["y_in"], 1)
                if n == 9 and tail:
                    pe.wait_ge(s["tile_done"], j + 1)

            def turn_of(i, heads, tail):
                for n in range(NH + 2):
                    slot(i, n, heads, tail)

            turn_of(0, True, False)
            with pe.Fori(1, TILES) as i:
                turn_of(i, True, True)
            turn_of(TILES, False, True)

        AB_CREDIT, O_CREDIT, ACC_CREDIT = 2, 1, 1

        def mix_act(act, steps, s):
            act.sem_inc(s["ab_out"], AB_CREDIT)

            def turn_of(i, heads, tail):
                j = i - 1
                for n in range(NH + 2):
                    if heads:
                        if n == 0:
                            act.wait_ge(s["xn_turned"], i + 1)
                            nc.scalar.copy(xT[:], bank[7][:]).then_inc(s["xT_ready"], 1)
                            act.wait_ge(s["dx_in"], i + 1)
                            nc.scalar.activation(dx[:], bank[6][:], ACT.Identity, bias=db).then_inc(s["dx_ready"], 1)
                        if n < NH:
                            act.wait_ge(s["hs_ready"], i * NH + n - 1 + HS_CREDIT)
                            act.wait_ge(s["ab_in"], i * 2 * NH + 2 * n + 1)
                            nc.scalar.activation(a_sb[:, n % 2], bank[0][:], ACT.Tanh, bias=ba[:, n:n + 1]).then_inc(s["ab_out"], 1)
                            act.wait_ge(s["ab_in"], i * 2 * NH + 2 * n + 2)
                            nc.scalar.activation(b_sb[:, n % 2], bank[1][:], ACT.Identity, bias=bb[:, n:n + 1]).then_inc(s["ab_out"], 1)
                        if 1 <= n <= NH:
                            h = n - 1
                            act.wait_ge(s["o_ready"], i * NH + h + 1 + O_CREDIT)
                            act.wait_ge(s["acc_done"], i * NH + h - 1 + ACC_CREDIT)
                            nc.scalar.activation(sq_sb[:, h % 2], o_sb[:, h % 2], ACT.Square).then_inc(s["sq_ready"], 1)
                    if tail:
                        if n == 3:
                            act.wait_ge(s["u_in"], j + 1)
                            nc.scalar.copy(uT[:], bank[6][:]).then_inc(s["uT_ready"], 1)
                        if n in (4, 5):
                            for c in (2 * n - 8, 2 * n - 7):
                                act.wait_ge(s["f1_in"], j * HC + c + 1)
                                nc.scalar.activation(gelu_sb[:, c], bank[7 - c % 2][:], ACT.Gelu, bias=f1b[:, c:c + 1])\
                                    .then_inc(s["f1_out"], 1)

            turn_of(0, True, False)
            with act.Fori(1, TILES) as i:
                turn_of(i, True, True)
            turn_of(TILES, False, True)

        HS_CREDIT = 1

        def mix_pool(pool, steps, s):
            def turn_of(i, heads, tail):
                j = i - 1
                for n in range(NH + 2):
                    if tail and n == 0:
                        pool.wait_ge(s["z_stats"], j + 1)
                        pool.sem_inc(waits_apart, 1)
                        steps.link(nc.gpsimd.tensor_scalar(z_var[:], z_mv[:, :, 1], EPS, None, ALU.add))
                        nc.gpsimd.tensor_tensor(z_rstd[:], z_var[:], neg_half[:, 0:TB], ALU.pow).then_inc(s["z_rstd"], 1)
                    if heads and n >= 2:
                        h = n - 2
                        pool.wait_ge(s["var_ready"], i * NH + h + 1)
                        nc.gpsimd.tensor_tensor(head_rstd[:, h % 2], head_var[:, h % 2], neg_half[:, 0:TB], ALU.pow)\
                            .then_inc(s["head_rstd"], 1)
                    if heads and n == 6:
                        ln_rstd(pool, steps, s, i + 1)

            ln_rstd(pool, steps, s, 0)
            turn_of(0, True, False)
            with pool.Fori(1, TILES) as i:
                steps.enter(i - 1, 2)
                turn_of(i, True, True)
            steps.leave(TILES - 1)
            turn_of(TILES, False, True)

        def mix_dve(dve, steps, s):
            v = nc.vector
            dve.sem_inc(s["hs_ready"], HS_CREDIT)
            dve.sem_inc(s["o_ready"], O_CREDIT)
            dve.sem_inc(s["acc_done"], ACC_CREDIT)
            steps.link(v.memset(carry[:], 0.0))
            ln_stats(dve, steps, s, 0)
            ln_apply(dve, steps, s, 0, first=True)

            def turn_of(i, heads, tail):
                j = i - 1
                for n in range(NH + 2):
                    if tail and n == 0:
                        for b in range(TB):
                            ins = v.bn_stats(z_stats[:, b], z[:, b])
                        steps.link_apart(ins)
                        for b in range(TB):
                            ins = v.bn_aggr(z_mv[:, b], z_stats[:, b])
                        ins.then_inc(s["z_stats"], 1)
                    if heads and n < NH:
                        dve.wait_ge(s["ab_out"], i * 2 * NH + 2 * n + 2 + AB_CREDIT)
                        if n >= 2:
                            pass
                        v.tensor_tensor_scan(hs[:, n % 2], a_sb[:, n % 2], b_sb[:, n % 2], carry[:, n:n + 1],
                                             ALU.mult, ALU.add).then_inc(s["hs_ready"], 1)
                        dve.wait_ge(s["hs_ready"], i * NH + n + 1 + HS_CREDIT)
                        steps.done(v.tensor_scalar(carry[:, n:n + 1], hs[:, n % 2, TW - 1:TW], keep[:, bass.ds(i + 1, 1)], None, ALU.mult))
                    if tail and n == 1:
                        dve.wait_ge(s["z_stats"], j + 1)
                        dve.wait_ge(s["z_rstd"], j + 1)
                        for b in range(TB):
                            ins = v.tensor_scalar(u[:, b], z[:, b], z_mv[:, b, 0:1], z_rstd[:, b:b + 1], ALU.subtract, ALU.mult)
                        steps.link(ins)
                        steps.link(v.tensor_tensor(u[:], u[:], ng_row.unsqueeze(1).broadcast_to([P, TB, P]), ALU.mult))
                        steps.link(v.tensor_tensor(u[:], u[:], nb_row.unsqueeze(1).broadcast_to([P, TB, P]), ALU.add))
                        v.tensor_tensor(u[:], u[:], z[:], ALU.add).then_inc(s["u_ready"], 1)
                    if heads:
                        if n == 1:
                            if tail:
                                dve.wait_ge(s["u_ready"], j + 1)
                            dve.wait_ge(s["base_in"], i + 1)
                            v.tensor_tensor(z[:], bank[6][:].rearrange("p (b e) -> p b e", b=TB),
                                            zrow[:].unsqueeze(1).broadcast_to([P, TB, P]), ALU.add).then_inc(s["base_out"], 1)
                        if 1 <= n <= NH:
                            h = n - 1
                            dve.wait_ge(s["c_in"], i * NH + h + 1)
                            if h >= 2:
                                dve.wait_ge(s["p_in"], i * NH + h - 1)
                            v.scalar_tensor_tensor(o_sb[:, h % 2], bank[2][:], cb[:, h:h + 1], dx[:], ALU.add, ALU.mult)\
                                .then_inc(s["o_ready"], 1)
                        if n >= 2:
                            h = n - 2
                            dve.wait_ge(s["p_in"], i * NH + h + 1)
                            steps.link(v.tensor_copy(head_mean[:, h % 2], bank[4 + h % 2][:, 0:TB]))
                            steps.link(v.tensor_tensor(head_var[:, h % 2], head_mean[:, h % 2], head_mean[:, h % 2], ALU.mult))
                            steps.link(v.tensor_tensor(head_var[:, h % 2], bank[4 + h % 2][:, TB:2 * TB], head_var[:, h % 2], ALU.subtract))
                            steps.link(v.tensor_scalar(head_var[:, h % 2], head_var[:, h % 2], 0.0, EPS, ALU.max, ALU.add))
                            dve.sem_inc(s["var_ready"], 1)
                            dve.wait_ge(s["head_rstd"], i * NH + h + 1)
                            if h == 0:
                                dve.wait_ge(s["base_out"], i + 1)
                            for b in range(TB):
                                ins = v.scalar_tensor_tensor(z[:, b], blk(bank[3], b), head_rstd[:, h % 2, b:b + 1], z[:, b],
                                                             ALU.mult, ALU.add)
                            ins.then_inc(s["acc_done"], 1)
                            dve.wait_ge(s["acc_done"], i * NH + h + 1 + ACC_CREDIT)
                        if n == 5:
                            ln_stats(dve, steps, s, i + 1)
                        if n == 7:
                            ln_apply(dve, steps, s, i + 1)
                    if tail and n == 7:
                        dve.wait_ge(s["f2_in"], j + 1)
                        v.scalar_tensor_tensor(hT[:], bank[7][:], f2b, uT[:], ALU.add, ALU.add).then_inc(s["hT_ready"], 1)
                    if tail and n == 9:
                        dve.wait_ge(s["y_in"], j + 1)
                        tile = X[:, bass.ds(j * TB, TB)]
                        steps.link(v.tensor_tensor(tile, tile, projb_row.unsqueeze(1).broadcast_to([P, TB, P]), ALU.add))
                        v.tensor_tensor(tile, bank[6][:].rearrange("p (b e) -> p b e", b=TB), tile, ALU.add).then_inc(s["tile_done"], 1)

            turn_of(0, True, False)
            with dve.Fori(1, TILES) as i:
                steps.enter(i - 1, MIX_STEPS)
                turn_of(i, True, True)
            steps.leave(TILES - 1)
            turn_of(TILES, False, True)
            dve.wait_ge(s["tile_done"], TILES)
            dve.sem_inc(phase_done, 1)

        MIX_STEPS = 46

        def tf_sems(p):
            return ln_sems(p) | {k: sem(f"{k}_{p}") for k in ("t_up_in", "t_up_out", "t_down_in", "t_down_out", "t_back_in", "tile_done")}

        relu_sb = hid[:, 0:HC]
        yT = acc

        def tf_pe(pe, s):
            def turn_of(i, up, down):
                j = i - 1
                if up:
                    pe.wait_ge(s["xn_ready"], i + 1)
                    turn(pe, bank[7], lambda b: xn[:, b]).then_inc(s["xn_turned"], 1)
                if down:
                    pe.wait_ge(s["t_up_out"], (j + 1) * HC)
                    for c in range(HC):
                        ins = nc.tensor.matmul(bank[4][:], t2[:, c], relu_sb[:, c], start=(c == 0), stop=(c == HC - 1))
                    ins.then_inc(s["t_down_in"], 1)
                if up:
                    pe.wait_ge(s["xT_ready"], i + 1)
                    for c in range(HC):
                        nc.tensor.matmul(bank[c][:], t1[:, c * P:(c + 1) * P], xT[:], start=True, stop=True).then_inc(s["t_up_in"], 1)
                if down:
                    pe.wait_ge(s["t_down_out"], j + 1)
                    pe.wait_ge(s["tile_done"], j + 1)
                    turn(pe, bank[6], lambda b: blk(yT, b)).then_inc(s["t_back_in"], 1)

            turn_of(0, True, False)
            with pe.Fori(1, TILES) as i:
                turn_of(i, True, True)
            turn_of(TILES, False, True)

        def tf_act(act, steps, s):
            def turn_of(i, up, down):
                j = i - 1
                if up:
                    act.wait_ge(s["xn_turned"], i + 1)
                    nc.scalar.copy(xT[:], bank[7][:]).then_inc(s["xT_ready"], 1)
                if down:
                    act.wait_ge(s["t_down_in"], j + 1)
                    act.wait_ge(s["tile_done"], j + 1)
                    nc.scalar.activation(yT[:], bank[4][:], ACT.Identity, bias=b2).then_inc(s["t_down_out"], 1)
                if up:
                    for c in range(HC):
                        act.wait_ge(s["t_up_in"], i * HC + c + 1)
                        nc.scalar.activation(relu_sb[:, c], bank[c][:], ACT.Relu, bias=b1[:, c:c + 1]).then_inc(s["t_up_out"], 1)

            turn_of(0, True, False)
            with act.Fori(1, TILES) as i:
                turn_of(i, True, True)
            turn_of(TILES, False, True)

        def tf_pool(pool, steps, s):
            moe_pool(pool, steps, s)

        def tf_dve(dve, steps, s):
            dve.sem_inc(s["tile_done"], 1)
            ln_stats(dve, steps, s, 0)
            ln_apply(dve, steps, s, 0, first=True)
            ln_stats(dve, steps, s, 1)
            ln_apply(dve, steps, s, 1)

            def turn_of(i, ahead=True):
                j = i - 1
                if ahead:
                    ln_stats(dve, steps, s, i + 1)
                    ln_apply(dve, steps, s, i + 1)
                dve.wait_ge(s["t_back_in"], j + 1)
                tile = X[:, bass.ds(j * TB, TB)].rearrange("p b e -> p (b e)")
                nc.vector.scalar_tensor_tensor(tile, bank[6][:], 0.5, tile, ALU.mult, ALU.add).then_inc(s["tile_done"], 1)

            with dve.Fori(1, TILES) as i:
                steps.enter(i - 1, 1)
                turn_of(i)
            steps.leave(TILES - 1)
            turn_of(TILES, ahead=False)
            dve.wait_ge(s["tile_done"], TILES + 1)
            dve.sem_inc(phase_done, 1)

        qT = sb("qT", [P, TW])
        kT = sb("kT", [P, TW])
        qm = sb("qm", [P, TB, 4, P])
        kv = sb("kv", [P, 2, 2 * P])
        scores = sb("scores", [P, 4, 4, P])
        state = sb("state", [P, P])
        y_tok = sb("y_tok", [P, P])
        y_turned = sb("y_turned", [P, P])

        def la_sems():
            return ln_sems(4) | {k: sem(f"la_{k}") for k in (
                "qk_in", "qk_out", "qm_ready", "kv_in", "kv_ready", "sc_in", "sc_out", "y_in", "y_out", "yt_in", "yt_out",
                "o_in", "o_out", "st_in", "st_ready")}

        TPS = SEQ // TW
        CH = TPS * TB
        SC_CREDIT = 2

        def la_pe(pe, s):
            with pe.Fori(0, BATCHES) as q:
                def finish_turn(c):
                    n = q * CH + c
                    pe.wait_ge(s["y_out"], n + 1)
                    nc.tensor.transpose(bank[1][:, 0:P], y_tok[:], ident[:]).then_inc(s["yt_in"], 1)

                def finish(c):
                    n = q * CH + c
                    pe.wait_ge(s["yt_out"], n + 1)
                    pe.wait_ge(s["o_out"], n + 1)
                    nc.tensor.matmul(bank[0][:, 0:P], y_turned[:], wo, start=True, stop=True).then_inc(s["o_in"], 1)

                for c in range(CH):
                    n = q * CH + c
                    b = c % TB
                    tile = q * TPS + c // TB
                    if b == 0:
                        pe.wait_ge(s["xn_ready"], tile + 1)
                        turn(pe, bank[7], lambda k: xn[:, k]).then_inc(s["xn_turned"], 1)
                        if c > 0:
                            finish_turn(c - 1)
                            finish(c - 1)
                        pe.wait_ge(s["xT_ready"], tile + 1)
                        pe.wait_ge(s["o_out"], n + 1)
                        nc.tensor.matmul(bank[0][:], wq, xT[:], start=True, stop=True).then_inc(s["qk_in"], 1)
                        nc.tensor.matmul(bank[1][:], wk, xT[:], start=True, stop=True).then_inc(s["qk_in"], 1)
                    nc.tensor.matmul(bank[2][:, 0:2 * P], blk(xT, b), wkv, start=True, stop=True).then_inc(s["kv_in"], 1)
                    pe.wait_ge(s["qm_ready"], tile + 1)
                    for g in range(4):
                        pe.wait_ge(s["sc_out"], n * 4 + g - 1 + SC_CREDIT)
                        nc.tensor.matmul(bank[3 + g % 2][:], kT[32 * g:32 * g + 32, b * P:(b + 1) * P],
                                         qm[32 * g:32 * g + 32, b].rearrange("p j t -> p (j t)"),
                                         start=True, stop=True).then_inc(s["sc_in"], 1)
                        if b > 0 and g == 1:
                            finish_turn(c - 1)
                        if b > 0 and g == 3:
                            finish(c - 1)
                    pe.wait_ge(s["st_ready"], n + 1)
                    nc.tensor.matmul(bank[5][:, 0:P], blk(qT, b), state[:], start=True, stop=False, skip_group_check=True)
                    pe.wait_ge(s["kv_ready"], n + 1)
                    for h in range(LH):
                        if h % 4 == 0:
                            pe.wait_ge(s["sc_out"], n * 4 + h // 4 + 1 + SC_CREDIT)
                        ins = nc.tensor.matmul(bank[5][:, h * HD:(h + 1) * HD], scores[:, h // 4, h % 4],
                                               kv[:, c % 2, P + h * HD:P + (h + 1) * HD], start=False, stop=(h == LH - 1),
                                               skip_group_check=True)
                    ins.then_inc(s["y_in"], 1)
                    nc.tensor.matmul(bank[6][:, 0:P], kv[:, c % 2, 0:P], kv[:, c % 2, P:2 * P], start=(c == 0), stop=(c == CH - 1),
                                     skip_group_check=True).then_inc(s["st_in"], 1)
                finish_turn(CH - 1)
                finish(CH - 1)

        def la_act(act, steps, s):
            with act.Fori(0, BATCHES) as q:
                for c in range(CH):
                    n = q * CH + c
                    tile = q * TPS + c // TB
                    if c % TB == 0:
                        act.wait_ge(s["xn_turned"], tile + 1)
                        nc.scalar.copy(xT[:], bank[7][:]).then_inc(s["xT_ready"], 1)
                        if c > 0:
                            act.wait_ge(s["yt_in"], n)
                            nc.scalar.copy(y_turned[:], bank[1][:, 0:P]).then_inc(s["yt_out"], 1)
                        act.wait_ge(s["qk_in"], 2 * tile + 1)
                        nc.scalar.activation(qT[:], bank[0][:], ACT.Identity, bias=bq).then_inc(s["qk_out"], 1)
                        act.wait_ge(s["qk_in"], 2 * tile + 2)
                        nc.scalar.activation(kT[:], bank[1][:], ACT.Identity, bias=bk).then_inc(s["qk_out"], 1)
                    elif c > 0:
                        act.wait_ge(s["yt_in"], n)
                        nc.scalar.copy(y_turned[:], bank[1][:, 0:P]).then_inc(s["yt_out"], 1)
                    act.wait_ge(s["y_in"], n + 1)
                    nc.scalar.copy(y_tok[:], bank[5][:, 0:P]).then_inc(s["y_out"], 1)
                act.wait_ge(s["yt_in"], q * CH + CH)
                nc.scalar.copy(y_turned[:], bank[1][:, 0:P]).then_inc(s["yt_out"], 1)

        def la_pool(pool, steps, s):
            moe_pool(pool, steps, s)

        def la_dve(dve, steps, s):
            v = nc.vector
            dve.sem_inc(s["sc_out"], SC_CREDIT)
            dve.sem_inc(s["o_out"], 1)
            ln_stats(dve, steps, s, 0)
            ln_apply(dve, steps, s, 0, first=True)
            with dve.Fori(0, BATCHES) as q:
                steps.enter(q, LA_STEPS)

                def finish(c):
                    x_block = X[:, bass.ds(q * CH + c, 1)].rearrange("p b e -> p (b e)")
                    dve.wait_ge(s["o_in"], q * CH + c + 1)
                    steps.link(v.tensor_tensor(x_block, bank[0][:, 0:P], x_block, ALU.add))
                    v.tensor_tensor(x_block, x_block, bo_row, ALU.add).then_inc(s["o_out"], 1)

                for c in range(CH):
                    n = q * CH + c
                    b = c % TB
                    tile = q * TPS + c // TB
                    if c == 0:
                        v.memset(state[:], 0.0).then_inc(s["st_ready"], 1)
                    if b == 0:
                        if c > 0:
                            finish(c - 1)
                        dve.wait_ge(s["qk_out"], 2 * tile + 1)
                        for j in range(4):
                            ins = v.tensor_scalar(qm[:, :, j], qT[:].rearrange("p (b t) -> p b t", b=TB), head_of[:, j:j + 1], None, ALU.mult)
                        dve.wait_ge(s["qk_out"], 2 * tile + 2)
                        steps.link(ins)
                        dve.sem_inc(s["qm_ready"], 1)
                    dve.wait_ge(s["kv_in"], n + 1)
                    v.tensor_tensor(kv[:, c % 2], bank[2][:, 0:2 * P], bkv_row, ALU.add).then_inc(s["kv_ready"], 1)
                    for g in range(4):
                        dve.wait_ge(s["sc_in"], n * 4 + g + 1)
                        v.tensor_tensor(scores[:, g], bank[3 + g % 2][:].rearrange("p (j t) -> p j t", j=4),
                                        causal[:].unsqueeze(1).broadcast_to([P, 4, P]), ALU.mult).then_inc(s["sc_out"], 1)
                    if b > 0:
                        finish(c - 1)
                    if b == 1:
                        ln_stats(dve, steps, s, tile + 1)
                    if b == 2:
                        ln_apply(dve, steps, s, tile + 1)
                    if c < CH - 1:
                        dve.wait_ge(s["st_in"], n + 1)
                        v.tensor_tensor(state[:], bank[6][:, 0:P], same_head[:], ALU.mult).then_inc(s["st_ready"], 1)
                finish(CH - 1)
            steps.leave(BATCHES)
            dve.wait_ge(s["o_out"], BLOCKS + 1)
            dve.sem_inc(phase_done, 1)

        LA_STEPS = 12

        moe_s = [moe_sems(0), moe_sems(2)]
        mix_s = [mix_sems()]
        tf_s = [tf_sems(3), tf_sems(5)]
        la_s = [la_sems()]
        block = ctx.enter_context(nc.Block())

        @block.sync
        def _(sp):
            sp.dma_start(X[:, 0:BLOCKS], t["x"].rearrange("(n p) d -> p n d", p=P)).then_inc(x_dma, 16)
            for dst, name in loads:
                sp.dma_start(dst[:], t[name]).then_inc(c_dma, 16)
            sp.dma_start(rows[:], t["rows"].partition_broadcast(P)).then_inc(c_dma, 16)
            sp.wait_ge(phase_done, 6)
            sp.dma_start(t["out"].rearrange("(n p) d -> p n d", p=P), X[:, 0:BLOCKS]).then_inc(stored, 16)
            sp.wait_ge(stored, 16)

        CONSTS = 10

        @block.gpsimd
        def _(pool):
            steps = Steps(pool, pool_steps_sem, waits_apart)
            g = nc.gpsimd
            g.memset(neg_half[:], -0.5).then_inc(const_ready, 1)
            g.memset(ones[:], 1.0 / P).then_inc(const_ready, 1)
            g.memset(X[:, BLOCKS:], 0.0).then_inc(const_ready, 1)
            g.iota(expert_no[:], [[1, EXPERTS]], base=0, channel_multiplier=0,
                   allow_small_or_imprecise_dtypes=True).then_inc(const_ready, 1)
            g.memset(ident[:], 0.0)
            g.memset(causal[:], 1.0)
            g.memset(same_head[:], 1.0)
            g.memset(head_of[:], 1.0)
            steps.link(g.memset(keep[:], 1.0))
            g.affine_select(ident[:], ident[:], [[-1, P]], ALU.not_equal, 1.0, base=0, channel_multiplier=1).then_inc(const_ready, 1)
            g.affine_select(causal[:], causal[:], [[1, P]], ALU.is_ge, 0.0, base=0, channel_multiplier=-1).then_inc(const_ready, 1)
            sh = same_head[:].rearrange("n (h d) -> n h d", d=HD)
            steps.link(g.affine_select(sh, sh, [[-HD, LH], [0, HD]], ALU.is_ge, 0.0, base=0, channel_multiplier=1))
            g.affine_select(sh, sh, [[HD, LH], [0, HD]], ALU.is_ge, 0.0, base=HD - 1, channel_multiplier=-1).then_inc(const_ready, 1)
            pool.wait_ge(const_ready, 7)
            g.tensor_tensor(head_of[:], same_head[:].rearrange("n (a j d) -> n a j d", j=4, d=HD)[:, 0, :, 0],
                            same_head[:].rearrange("n (a j d) -> n a j d", j=4, d=HD)[:, 1, :, 0], ALU.add).then_inc(const_ready, 1)
            pool.wait_ge(const_ready, 8)
            for a in range(2, 4):
                ins = g.tensor_tensor(head_of[:], head_of[:],
                                      same_head[:].rearrange("n (a j d) -> n a j d", j=4, d=HD)[:, a, :, 0], ALU.add)
                if a == 2:
                    steps.link(ins)
            ins.then_inc(const_ready, 1)
            g.memset(keep[:, 0:TILES:2], 0.0).then_inc(const_ready, 1)
            phase_setup_pool(pool, steps)
            moe_pool(pool, steps, moe_s[0])
            pool.wait_ge(phase_done, 1)
            mix_pool(pool, steps, mix_s[0])
            pool.wait_ge(phase_done, 2)
            moe_pool(pool, steps, moe_s[1])
            pool.wait_ge(phase_done, 3)
            tf_pool(pool, steps, tf_s[0])
            pool.wait_ge(phase_done, 4)
            la_pool(pool, steps, la_s[0])
            pool.wait_ge(phase_done, 5)
            tf_pool(pool, steps, tf_s[1])

        @block.tensor
        def _(pe):
            pe.wait_ge(const_ready, CONSTS)
            pe.wait_ge(c_dma, LOADED)
            phase_setup_pe(pe)
            moe_pe(pe, moe_s[0])
            pe.wait_ge(phase_done, 1)
            mix_pe(pe, mix_s[0])
            pe.wait_ge(phase_done, 2)
            moe_pe(pe, moe_s[1])
            pe.wait_ge(phase_done, 3)
            tf_pe(pe, tf_s[0])
            pe.wait_ge(phase_done, 4)
            la_pe(pe, la_s[0])
            pe.wait_ge(phase_done, 5)
            tf_pe(pe, tf_s[1])

        @block.scalar
        def _(act):
            steps = Steps(act, act_steps_sem, waits_apart)
            act.wait_ge(const_ready, CONSTS)
            act.wait_ge(c_dma, LOADED)
            phase_setup_act(act, steps)
            moe_act(act, steps, moe_s[0])
            act.wait_ge(phase_done, 1)
            mix_act(act, steps, mix_s[0])
            act.wait_ge(phase_done, 2)
            moe_act(act, steps, moe_s[1])
            act.wait_ge(phase_done, 3)
            tf_act(act, steps, tf_s[0])
            act.wait_ge(phase_done, 4)
            la_act(act, steps, la_s[0])
            act.wait_ge(phase_done, 5)
            tf_act(act, steps, tf_s[1])

        @block.vector
        def _(dve):
            steps = Steps(dve, dve_steps_sem, waits_apart)
            dve.wait_ge(const_ready, CONSTS)
            dve.wait_ge(c_dma, LOADED)
            dve.wait_ge(x_dma, 16)
            phase_setup_dve(dve, steps)
            moe_dve(dve, steps, moe_s[0])
            dve.wait_ge(phase_done, 1)
            mix_dve(dve, steps, mix_s[0])
            dve.wait_ge(phase_done, 2)
            moe_dve(dve, steps, moe_s[1])
            dve.wait_ge(phase_done, 3)
            tf_dve(dve, steps, tf_s[0])
            dve.wait_ge(phase_done, 4)
            la_dve(dve, steps, la_s[0])
            dve.wait_ge(phase_done, 5)
            tf_dve(dve, steps, tf_s[1])


def kernel(**inputs):
    import numpy as np
    from concourse.bacc import Bacc
    from concourse.bass_utils import run_bass_kernel_spmd

    a = {k: np.asarray(v) for k, v in inputs.items()}
    HC, W = a["L0_ffn_Wfc_s"].shape[1] // P, P
    att, ffn, la, tf = (lambda k: a["L0_attn_" + k]), (lambda k: a["L0_ffn_" + k]), (lambda k: a["L1_attn_" + k]), (lambda k: a["L1_ffn_" + k])
    mlps = lambda s, e: np.concatenate([s[None], e])
    chunked = lambda w: w.reshape(-1, HC, P, W)
    cols = [
        mlps(ffn("bfc_s"), ffn("bfc")).reshape(-1, P), mlps(ffn("bproj_s"), ffn("bproj")), ffn("Wr").T,
        att("Wa_b"), att("Wb_b"), att("C_b"), att("D_b")[None], att("hn_g"), att("hn_b"),
        att("ffn1_b").reshape(HC, P), att("ffn2_b")[None], la("bq")[None], la("bk")[None], tf("b1").reshape(HC, P), tf("b2")[None]]
    laid = {
        "x": a["L0_attn_emb"].reshape(-1, W),
        "w_up": mlps(ffn("Wfc_s"), ffn("Wfc")).transpose(1, 0, 2),
        "w_dn": chunked(mlps(ffn("Wproj_s"), ffn("Wproj"))).transpose(2, 0, 1, 3),
        "wa": att("Wa_w").transpose(2, 0, 1), "wb": att("Wb_w").transpose(2, 0, 1), "cw": att("C_w").transpose(2, 0, 1),
        "squares": np.stack([w.T for w in (att("D_w"), att("Wout_w"), att("proj_w"), la("Wq"), la("Wk"), la("Wv"), la("Wo"))], 1),
        "f1": att("ffn1_w").T, "f2": chunked(att("ffn2_w").T)[0].transpose(1, 0, 2),
        "w1": tf("W1").T, "w2": chunked(tf("W2").T)[0].transpose(1, 0, 2),
        "cols": np.concatenate(cols).T,
        "rows": np.concatenate([att("Wout_b"), att("proj_b"), att("norm_g"), att("norm_b"), la("bk"), la("bv"), la("bo"), att("head_w")]),
    }
    nc = Bacc("TRN2", target_bir_lowering=False, num_devices=1)
    arrays, t = {}, {}
    for name, v in laid.items():
        arrays["in_" + name] = np.ascontiguousarray(v)
        t[name] = nc.dram_tensor("in_" + name, v.shape, F32, kind="ExternalInput").ap()
    t["out"] = nc.dram_tensor("out_x", laid["x"].shape, F32, kind="ExternalOutput").ap()
    macaron_kernel(nc, t)
    got = run_bass_kernel_spmd(nc, [arrays], core_ids=[0]).results[0]["out_x"]
    return got.reshape(a["L0_attn_emb"].shape)
```

```python
from contextlib import ExitStack

import concourse.bass as bass
from concourse import mybir

F32 = mybir.dt.float32
F32R = mybir.dt.float32r
U32 = mybir.dt.uint32
ACT = mybir.ActivationFunctionType
ALU = mybir.AluOpType
AX_X = mybir.AxisListType.X

P = 128
EPS = 1e-5


class Steps:

    def __init__(self, eng, sem, apart):
        self.apart = apart
        self.eng, self.sem, self.total, self.turn, self.n = eng, sem, 0, 0, 0

    def done(self, ins):
        ins.then_inc(self.sem, 1)
        self.n += 1

    def wait(self):
        self.eng.wait_ge(self.sem, self.total + self.turn + self.n)

    def link(self, ins):
        self.done(ins)
        self.wait()

    def link_apart(self, ins):
        self.link(ins)
        self.eng.sem_inc(self.apart, 1)

    def enter(self, turn, per):
        self.total, self.n, self.turn, self.per = self.total + self.n, 0, turn * per, per

    def leave(self, turns):
        assert self.n == self.per, f"{self.n} steps a turn"
        self.total, self.turn, self.n = self.total + turns * self.per, 0, 0


def macaron_kernel(nc, t):
    E = P
    TOKENS, _ = t["x"].shape
    BATCHES = 4
    TB = 4
    TW = TB * P
    TILES = TOKENS // TW
    BLOCKS = TOKENS // P
    MLPS = t["w_mlp"].shape[0]
    EXPERTS = MLPS - 1
    HC = t["w_mlp"].shape[2] // (2 * P)
    NH = t["wa"].shape[1]
    LH = 16
    HD = E // LH
    SEQ = TOKENS // BATCHES
    assert TW * TILES == TOKENS and SEQ == 2 * TW

    with ExitStack() as ctx:
        def sb(name, shape, dt=F32):
            return ctx.enter_context(nc.sbuf_tensor(name, shape, dt))

        def sem(name):
            return ctx.enter_context(nc.semaphore(name))

        def ring(tensor, n):
            return tensor[:, n]

        bank = [ctx.enter_context(nc.psum_tensor(f"bank{n}", [P, TW], F32)) for n in range(8)]

        X = sb("X", [P, BLOCKS + TB, E])
        WM = 2 * HC * P
        STAGES = 4
        w_stage = sb("w_stage", [P, STAGES, WM])
        w_hi = sb("w_hi", [P, MLPS, WM], F32R)
        w_lo = sb("w_lo", [P, MLPS, WM], F32R)
        wa = sb("wa_sb", [P, NH, P])
        wb = sb("wb_sb", [P, NH, P])
        cw = sb("cw_sb", [P, NH, P])
        squares = sb("squares_sb", [P, 7, P])
        dw, wout, proj, wq, wk, wv, wo = (squares[:, n] for n in range(7))
        wkv = squares[:, 4:6]
        f1 = sb("f1_sb", [P, HC * P])
        f2 = sb("f2_sb", [P, HC, E])
        t1 = sb("t1_sb", [P, HC * P])
        t2 = sb("t2_sb", [P, HC, E])
        COLS = t["cols"].shape[1]
        cols = sb("cols_sb", [P, COLS])
        at = [0]

        def col(n):
            at[0] += n
            return cols[:, at[0] - n:at[0]]

        b_up, b_dn, wr, ba, bb, cb, db = col(MLPS * HC), col(MLPS), col(EXPERTS), col(NH), col(NH), col(NH), col(1)
        hn_g, hn_b, f1b, f2b, bq, bk, b1, b2 = col(NH), col(NH), col(HC), col(1), col(1), col(1), col(HC), col(1)
        bv = col(1)
        assert at[0] == COLS
        rows = sb("rows_sb", [P, t["rows"].shape[0]])
        woutb_row, projb_row, ng_row, nb_row, bk_row, bv_row, bo_row = (rows[:, P * n:P * n + P] for n in range(7))
        bkv_row = rows[:, 4 * P:6 * P]
        head_w = rows[:, 7 * P:7 * P + NH]

        ident = sb("ident", [P, P])
        ones = sb("ones", [P, P])
        causal = sb("causal", [P, P])
        same_head = sb("same_head", [P, P])
        head_of = sb("head_of", [P, 4])
        neg_half = sb("neg_half", [P, NH * TB])
        expert_no = sb("expert_no", [P, EXPERTS])
        keep = sb("keep", [P, TILES + 1])
        wz = sb("wz", [P, NH, P])
        zrow = sb("zrow", [P, P])

        stats = sb("stats", [P, TB, 6])
        mv = sb("mv", [P, TB, 2])
        var_eps = sb("var_eps", [P, TB])
        rstd = sb("rstd", [P, TB])
        xn = sb("xn", [P, TB, E])
        xT = sb("xT", [P, TW])
        hid = sb("hid", [P, HC, TW])
        hid_hi = sb("hid_hi", [P, 2 * HC, TW], F32R)
        hid_lo = sb("hid_lo", [P, 2 * HC, TW], F32R)
        x_hi = sb("x_hi", [P, TW], F32R)
        x_lo = sb("x_lo", [P, TW], F32R)
        ident_r = sb("ident_r", [P, P], F32R)
        acc = sb("acc", [P, TW])
        part = sb("part", [P, TW])
        gate_b = sb("gate_b", [P, 2, TW])

        c_dma = sem("weights_loaded")
        x_dma = sem("x_loaded")
        const_ready = sem("const_ready")
        phase_done = sem("phase_done")
        stored = sem("stored")
        dve_steps_sem, pool_steps_sem, act_steps_sem = sem("dve_step"), sem("pool_step"), sem("act_step")
        waits_apart = sem("waits_apart")
        setup_pe, setup_dve = sem("setup_pe"), sem("setup_dve")

        loads = [(squares, "squares"), (cols, "cols"), (wa, "wa"), (wb, "wb"), (cw, "cw"),
                 (f1, "f1"), (f2, "f2"), (t1, "w1"), (t2, "w2")]
        LOADED = 16 * (len(loads) + 1)

        def ln_sems(p):
            return {k: sem(f"{k}_{p}") for k in ("stats_ready", "rstd_ready", "xn_ready", "xn_turned", "xT_ready")}

        def ln_stats(dve, steps, s, i):
            for b in range(TB):
                ins = nc.vector.bn_stats(stats[:, b], X[:, bass.ds(i * TB + b, 1)])
            steps.link_apart(ins)
            for b in range(TB):
                ins = nc.vector.bn_aggr(mv[:, b], stats[:, b])
            ins.then_inc(s["stats_ready"], 1)

        def ln_rstd(pool, steps, s, i):
            pool.wait_ge(s["stats_ready"], i + 1)
            pool.sem_inc(waits_apart, 1)
            steps.link(nc.gpsimd.tensor_scalar(var_eps[:], mv[:, :, 1], EPS, None, ALU.add))
            nc.gpsimd.tensor_tensor(rstd[:], var_eps[:], neg_half[:, 0:TB], ALU.pow).then_inc(s["rstd_ready"], 1)

        def ln_apply(dve, steps, s, i, first=False):
            dve.wait_ge(s["stats_ready"], i + 1)
            dve.wait_ge(s["rstd_ready"], i + 1)
            if not first:
                dve.wait_ge(s["xn_turned"], i)
            for b in range(TB):
                ins = nc.vector.tensor_scalar(xn[:, b:b + 1], X[:, bass.ds(i * TB + b, 1)], mv[:, b, 0:1],
                                              rstd[:, b:b + 1], ALU.subtract, ALU.mult)
            ins.then_inc(s["xn_ready"], 1)

        def turn(pe, out, src):
            for b in range(TB):
                ins = nc.tensor.transpose(out[:, b * P:(b + 1) * P], src(b), ident[:])
            return ins

        def blk(ap, b):
            return ap[:, b * P:(b + 1) * P]

        logits = sb("logits", [P, TB, EXPERTS])
        top = sb("top", [P, TB, 8])
        top_at = sb("top_at", [P, TB, 8], U32)
        top_no = sb("top_no", [P, TB, 2])
        lead = sb("lead", [P, TB])
        half_tanh = sb("half_tanh", [P, TB])
        g2 = sb("g2", [P, 2, TB])
        pick = sb("pick", [P, 2, TB, EXPERTS])
        gates = sb("gates", [P, TB, EXPERTS])
        gates_hi = sb("gates_hi", [P, TB, EXPERTS], F32R)
        gates_lo = sb("gates_lo", [P, TB, EXPERTS], F32R)
        N = MLPS * HC
        w_in = [sem(f"w_in_{n}") for n in range(STAGES)]
        w_hi_ready, w_lo_ready = sem("w_hi_ready"), sem("w_lo_ready")

        def moe_sems(p):
            return ln_sems(p) | {k: sem(f"{k}_{p}") for k in (
                "x_hi_ready", "x_lo_ready", "logits_in", "lead_ready", "tanh_ready", "gates_ready", "up_done", "gelu_done", "lo_done",
                "gate_in", "gate_out", "down_done", "down_used", "acc_ready", "back_in", "tile_done")}

        GELU_CREDIT, DOWN_CREDIT, USED_CREDIT, GATE_CREDIT, LO_CREDIT = 3, 2, 2, 1, HC

        def slot_of(e, c):
            return (e % 2) * HC + c

        def moe_pe(pe, s):
            def take_tile(i):
                pe.wait_ge(s["xn_ready"], i + 1)
                turn(pe, bank[7], lambda b: xn[:, b]).then_inc(s["xn_turned"], 1)

            def back(i):
                pe.wait_ge(s["acc_ready"], i + 1)
                turn(pe, bank[7], lambda b: blk(acc, b)).then_inc(s["back_in"], 1)

            def up(i, e):
                for c in range(HC):
                    n = e * HC + c
                    pe.wait_ge(s["gelu_done"], i * N + n - 2 + GELU_CREDIT)
                    span = slice(c * P, (c + 1) * P)
                    nc.tensor.matmul(bank[n % 3][:], w_hi[:, e, span], x_hi[:], start=True, stop=False)
                    nc.tensor.matmul(bank[n % 3][:], w_lo[:, e, span], x_hi[:], start=False, stop=False)
                    nc.tensor.matmul(bank[n % 3][:], w_hi[:, e, span], x_lo[:], start=False, stop=True).then_inc(s["up_done"], 1)

            def down(i, e):
                pe.wait_ge(s["down_used"], i * MLPS + e - 1 + USED_CREDIT)
                for c in range(HC):
                    n = e * HC + c
                    pe.wait_ge(s["lo_done"], i * N + n + 1 + LO_CREDIT)
                    span, q = slice((HC + c) * P, (HC + c + 1) * P), slot_of(e, c)
                    nc.tensor.matmul(bank[3 + e % 2][:], w_hi[:, e, span], hid_hi[:, q], start=(c == 0), stop=False)
                    nc.tensor.matmul(bank[3 + e % 2][:], w_lo[:, e, span], hid_hi[:, q], start=False, stop=False)
                    ins = nc.tensor.matmul(bank[3 + e % 2][:], w_hi[:, e, span], hid_lo[:, q], start=False, stop=(c == HC - 1))
                ins.then_inc(s["down_done"], 1)

            def turn_of(i, first):
                pe.wait_ge(s["xT_ready"], i + 1)
                for b in range(TB):
                    ins = nc.tensor.matmul(bank[6][:, b * EXPERTS:(b + 1) * EXPERTS], blk(xT, b), wr, start=True, stop=True)
                ins.then_inc(s["logits_in"], 1)
                pe.wait_ge(s["x_lo_ready"], i + 1)
                for e in range(MLPS):
                    if first:
                        pe.wait_ge(w_lo_ready, e + 1)
                    up(i, e)
                    if e == 1 and not first:
                        back(i - 1)
                    if e >= 1:
                        if e == 1:
                            pe.wait_ge(s["gates_ready"], i + 1)
                        pe.wait_ge(s["gate_out"], i * EXPERTS + e - 1 + GATE_CREDIT)
                        for b in range(TB):
                            nc.tensor.matmul(blk(bank[5], b), gates_hi[:, b, e - 1:e].broadcast_to([P, P]), ident_r[:],
                                             start=True, stop=False)
                            ins = nc.tensor.matmul(blk(bank[5], b), gates_lo[:, b, e - 1:e].broadcast_to([P, P]), ident_r[:],
                                                   start=False, stop=True)
                        ins.then_inc(s["gate_in"], 1)
                        down(i, e - 1)
                pe.wait_ge(s["tile_done"], i + 1)
                take_tile(i + 1)
                down(i, MLPS - 1)

            take_tile(0)
            turn_of(0, True)
            with pe.Fori(1, TILES) as i:
                turn_of(i, False)
            back(TILES - 1)

        def split_weights_act(act):
            for e in range(MLPS):
                act.wait_ge(w_in[e % STAGES], 16 * (e // STAGES + 1))
                nc.scalar.copy(w_hi[:, e], w_stage[:, e % STAGES]).then_inc(w_hi_ready, 1)

        def split_weights_dve(dve):
            for e in range(MLPS):
                dve.wait_ge(w_in[e % STAGES], 16 * (e // STAGES + 1))
                dve.wait_ge(w_hi_ready, e + 1)
                nc.vector.tensor_tensor(w_lo[:, e], w_stage[:, e % STAGES], w_hi[:, e].bitcast(F32), ALU.subtract).then_inc(w_lo_ready, 1)

        def moe_act(act, steps, s):
            act.sem_inc(s["gelu_done"], GELU_CREDIT)
            act.sem_inc(s["gate_out"], GATE_CREDIT)

            def take_tile(i):
                act.wait_ge(s["xn_turned"], i + 1)
                nc.scalar.copy(x_hi[:], bank[7][:]).then_inc(s["x_hi_ready"], 1)
                nc.scalar.copy(xT[:], bank[7][:]).then_inc(s["xT_ready"], 1)

            take_tile(0)
            with act.Fori(0, TILES) as i:
                for e in range(MLPS):
                    act.wait_ge(s["down_done"], i * MLPS + e - 1 + DOWN_CREDIT)
                    for c in range(HC):
                        n = e * HC + c
                        act.wait_ge(s["up_done"], i * N + n + 1)
                        act.wait_ge(s["lo_done"], i * N + n - 3 + LO_CREDIT)
                        nc.scalar.activation(hid_hi[:, slot_of(e, c)], bank[n % 3][:], ACT.Gelu_apprx_tanh, bias=b_up[:, n:n + 1])
                        nc.scalar.activation(hid[:, c], bank[n % 3][:], ACT.Gelu_apprx_tanh,
                                             bias=b_up[:, n:n + 1]).then_inc(s["gelu_done"], 1)
                        if e == 0 and c == 1:
                            act.wait_ge(s["lead_ready"], i + 1)
                            nc.scalar.activation(half_tanh[:], lead[:], ACT.Tanh, scale=0.5).then_inc(s["tanh_ready"], 1)
                    if e >= 1:
                        act.wait_ge(s["gate_in"], i * EXPERTS + e)
                        act.wait_ge(s["down_used"], i * MLPS + e - 1 + USED_CREDIT)
                        nc.scalar.copy(gate_b[:, e % 2], bank[5][:]).then_inc(s["gate_out"], 1)
                take_tile(i + 1)

        def moe_pool(pool, steps, s):
            ln_rstd(pool, steps, s, 0)
            with pool.Fori(1, TILES + 1) as i:
                steps.enter(i - 1, 1)
                ln_rstd(pool, steps, s, i)
            steps.leave(TILES)

        def moe_dve(dve, steps, s):
            v = nc.vector
            dve.sem_inc(s["down_used"], USED_CREDIT)
            dve.sem_inc(s["down_done"], DOWN_CREDIT)
            dve.sem_inc(s["lo_done"], LO_CREDIT)
            dve.sem_inc(s["tile_done"], 1)

            def rest_of_x(i):
                dve.wait_ge(s["x_hi_ready"], i + 1)
                dve.wait_ge(s["xT_ready"], i + 1)
                v.tensor_tensor(x_lo[:], xT[:], x_hi[:].bitcast(F32), ALU.subtract).then_inc(s["x_lo_ready"], 1)

            def route(i):
                dve.wait_ge(s["logits_in"], i + 1)
                steps.link_apart(v.tensor_copy(logits[:], bank[6][:, 0:TB * EXPERTS].rearrange("p (b e) -> p b e", b=TB)))
                for b in range(TB):
                    ins = v.max(top[:, b], logits[:, b])
                steps.link(ins)
                v.tensor_tensor(lead[:], top[:, :, 0], top[:, :, 1], ALU.subtract).then_inc(s["lead_ready"], 1)
                for b in range(TB):
                    ins = v.max_index(top_at[:, b], top[:, b], logits[:, b])
                steps.link(ins)
                steps.link(v.tensor_copy(top_no[:], top_at[:, :, 0:2]))
                for k in range(2):
                    ins = v.tensor_tensor(pick[:, k], expert_no[:].unsqueeze(1).broadcast_to([P, TB, EXPERTS]),
                                          top_no[:, :, k:k + 1].broadcast_to([P, TB, EXPERTS]), ALU.is_equal)
                steps.done(ins)

            def share_out(i):
                dve.wait_ge(s["tanh_ready"], i + 1)
                v.tensor_scalar(g2[:, 0], half_tanh[:], 0.5, 0.5, ALU.mult, ALU.add)
                steps.link(v.tensor_scalar(g2[:, 1], half_tanh[:], -0.5, 0.5, ALU.mult, ALU.add))
                for k in range(2):
                    ins = v.tensor_tensor(pick[:, k], pick[:, k],
                                          g2[:, k].unsqueeze(2).broadcast_to([P, TB, EXPERTS]), ALU.mult)
                steps.link(ins)
                steps.link(v.tensor_tensor(gates[:], pick[:, 0], pick[:, 1], ALU.add))
                steps.link(v.tensor_copy(gates_hi[:], gates[:]))
                v.tensor_tensor(gates_lo[:], gates[:], gates_hi[:].bitcast(F32), ALU.subtract).then_inc(s["gates_ready"], 1)

            def rest_of_hidden(i, e, c):
                n = e * HC + c
                dve.wait_ge(s["gelu_done"], i * N + n + 1 + GELU_CREDIT)
                v.tensor_tensor(hid_lo[:, slot_of(e, c)], hid[:, c], hid_hi[:, slot_of(e, c)].bitcast(F32), ALU.subtract)\
                    .then_inc(s["lo_done"], 1)

            def gather(i, e):
                dve.wait_ge(s["down_done"], i * MLPS + e + 1 + DOWN_CREDIT)
                if e == 0:
                    ins = v.tensor_scalar(acc[:], bank[3][:], b_dn[:, 0:1], None, ALU.add)
                else:
                    dve.wait_ge(s["gate_out"], i * EXPERTS + e + GATE_CREDIT)
                    ins = v.scalar_tensor_tensor(part[:], bank[3 + e % 2][:], b_dn[:, e:e + 1], gate_b[:, e % 2], ALU.add, ALU.mult)
                ins.then_inc(s["down_used"], 1)
                dve.wait_ge(s["down_used"], i * MLPS + e + 1 + USED_CREDIT)
                if e >= 1:
                    ins = v.tensor_tensor(acc[:], acc[:], part[:], ALU.add)
                    if e == MLPS - 1:
                        ins.then_inc(s["acc_ready"], 1)
                    else:
                        steps.link(ins)

            def add_tile(i):
                dve.wait_ge(s["back_in"], i + 1)
                tile = X[:, bass.ds(i * TB, TB)].rearrange("p b e -> p (b e)")
                v.scalar_tensor_tensor(tile, bank[7][:], 0.5, tile, ALU.mult, ALU.add).then_inc(s["tile_done"], 1)

            def turn_of(i, first):
                route(i)
                for e in range(MLPS):
                    for c in range(HC):
                        rest_of_hidden(i, e, c)
                        if e == 0 and c == 3:
                            share_out(i)
                        if e == 1 and c == 3 and not first:
                            add_tile(i - 1)
                        if e >= 2 and c == 1:
                            gather(i, e - 2)
                    if e == 3:
                        ln_stats(dve, steps, s, i + 1)
                    if e == 5:
                        ln_apply(dve, steps, s, i + 1)
                gather(i, MLPS - 2)
                rest_of_x(i + 1)
                gather(i, MLPS - 1)

            ln_stats(dve, steps, s, 0)
            ln_apply(dve, steps, s, 0, first=True)
            rest_of_x(0)
            turn_of(0, True)
            with dve.Fori(1, TILES) as i:
                steps.enter(i - 1, MOE_STEPS)
                turn_of(i, False)
            steps.leave(TILES - 1)
            add_tile(TILES - 1)
            dve.wait_ge(s["tile_done"], TILES + 1)
            dve.sem_inc(phase_done, 1)

        MOE_STEPS = 17

        gain = sb("gain", [P, NH])
        head_bias = sb("head_bias", [P, 1])
        thr = sb("thr", [P, 4])
        mags = sb("mags", [P, 2])
        tern = sb("tern", [P, HC * P])
        t_r = sb("t_r", [P, 2, HC * P], F32R)
        
        def phase_setup_pool(pool, steps):
            pass

        def phase_setup_act(act, steps):
            pass

        def phase_setup_pe(pe):
            pe.wait_ge(setup_dve, 1)
            nc.tensor.matmul(bank[0][:, 0:2], ones[:], mags[:], start=True, stop=True).then_inc(setup_pe, 1)
            pe.wait_ge(setup_dve, 2)
            nc.tensor.matmul(bank[1][:, 0:P], head_bias[:].broadcast_to([P, P]), wout, start=True, stop=True).then_inc(setup_pe, 1)
            pe.wait_ge(setup_dve, 3)
            for h in range(NH):
                ins = nc.tensor.matmul(bank[2 + h // 4][:, (h % 4) * P:(h % 4 + 1) * P], ones[:], wz[:, h], start=True, stop=True)
            ins.then_inc(setup_pe, 1)

        def phase_setup_dve(dve, steps):
            v = nc.vector
            v.tensor_copy(ident_r[:], ident[:])
            steps.link(v.tensor_scalar(tern[:], t1[:], -1.0, None, ALU.mult))
            steps.link(v.tensor_tensor(tern[:], tern[:], t1[:], ALU.max))
            steps.link(v.tensor_reduce(mags[:, 0:1], tern[:], AX_X, ALU.add))
            flat2 = t2[:].rearrange("p c e -> p (c e)")
            steps.link(v.tensor_scalar(tern[:], flat2, -1.0, None, ALU.mult))
            steps.link(v.tensor_tensor(tern[:], tern[:], flat2, ALU.max))
            v.tensor_reduce(mags[:, 1:2], tern[:], AX_X, ALU.add).then_inc(setup_dve, 1)
            dve.wait_ge(setup_pe, 1)
            steps.link(v.tensor_scalar(thr[:, 0:2], bank[0][:, 0:2], 1.0 / (HC * P), EPS, ALU.mult, ALU.add))
            steps.link(v.tensor_scalar(thr[:, 0:2], thr[:, 0:2], 0.5, None, ALU.mult))
            steps.link(v.tensor_scalar(thr[:, 2:4], thr[:, 0:2], -1.0, None, ALU.mult))
            for n, w in enumerate((t1[:], flat2)):
                steps.link(v.tensor_scalar(tern[:], w, thr[:, 2 + n:3 + n], None, ALU.is_lt))
                steps.link(v.scalar_tensor_tensor(t_r[:, n], w, thr[:, n:n + 1], tern[:], ALU.is_gt, ALU.subtract))
            steps.link(v.tensor_tensor(gain[:], hn_b, head_w, ALU.mult))
            steps.link(v.tensor_reduce(head_bias[:], gain[:], AX_X, ALU.add))
            steps.link(v.tensor_scalar(head_bias[:], head_bias[:], 1.0 / NH, None, ALU.mult))
            steps.link(v.tensor_tensor(gain[:], hn_g, head_w, ALU.mult))
            steps.link(v.tensor_scalar(gain[:], gain[:], 1.0 / NH, None, ALU.mult))
            dve.sem_inc(setup_dve, 1)
            dve.wait_ge(setup_pe, 2)
            steps.link(v.tensor_tensor(zrow[:], bank[1][:, 0:P], woutb_row, ALU.add))
            for h in range(NH):
                ins = v.tensor_scalar(wz[:, h], wout, gain[:, h:h + 1], None, ALU.mult)
            ins.then_inc(setup_dve, 1)
            dve.wait_ge(setup_pe, 3)
            for q in range(2):
                half = wz[:, 4 * q:4 * q + 4].rearrange("p h e -> p (h e)")
                v.tensor_tensor(half, half, bank[2 + q][:], ALU.subtract)
            steps.link(v.tensor_scalar(wout, wout, 1.0 / NH, None, ALU.mult))

        spare = w_stage[:].rearrange("p a (n t) -> p (a n) t", t=TW)
        a_sb = spare[:, 0:2]
        b_sb = spare[:, 2:4]
        hs = spare[:, 4:6]
        o_sb = spare[:, 6:8]
        dx = part
        carry = sb("carry", [P, NH])
        o_stats = sb("o_stats", [P, TB, 6])
        o_mv = sb("o_mv", [P, 2, TB, 2])
        head_var = sb("head_var", [P, TB])
        head_rstd = sb("head_rstd", [P, 2, TB])
        share = gate_b[:].rearrange("p a (b e) -> p a b e", b=TB)
        z = t1[:].rearrange("p (b e) -> p b e", b=TB)
        u = t2
        z_stats = sb("z_stats", [P, TB, 6])
        z_mv = sb("z_mv", [P, TB, 2])
        z_rstd = sb("z_rstd", [P, TB])
        z_var = sb("z_var", [P, TB])
        uT = acc
        hT = tern
        gelu_sb = hid

        def mix_sems():
            return ln_sems(1) | {k: sem(f"mix_{k}") for k in (
                "dx_in", "dx_ready", "ab_in", "ab_out", "hs_ready", "c_in", "o_ready", "ot_in", "o_stats", "p_in",
                "head_rstd", "share_ready", "added", "base_in", "base_out", "z_stats", "z_rstd", "u_ready", "u_in", "uT_ready",
                "f1_in", "f1_out", "f2_in", "hT_ready", "y_in", "tile_done")}

        SLOTS = NH + 3
        AB_CREDIT, HS_CREDIT, O_CREDIT, SHARE_CREDIT, ADD_CREDIT, STATS_CREDIT = 2, 1, 1, 2, 2, 1

        def mix_pe(pe, s):
            def take_tile(i):
                pe.wait_ge(s["xn_ready"], i + 1)
                turn(pe, bank[7], lambda b: xn[:, b]).then_inc(s["xn_turned"], 1)

            def slot(i, n, heads, tail):
                j = i - 1
                if heads:
                    if n == 0:
                        pe.wait_ge(s["xT_ready"], i + 1)
                    if n < NH:
                        for k, w in enumerate((wa, wb)):
                            pe.wait_ge(s["ab_out"], i * 2 * NH + 2 * n + k - 1 + AB_CREDIT)
                            nc.tensor.matmul(bank[k][:], w[:, n], xT[:], start=True, stop=True).then_inc(s["ab_in"], 1)
                    if n == 0:
                        if tail:
                            pe.wait_ge(s["tile_done"], j)
                        nc.tensor.matmul(bank[6][:], dw, xT[:], start=True, stop=True).then_inc(s["dx_in"], 1)
                    if n == 1:
                        pe.wait_ge(s["dx_ready"], i + 1)
                        for b in range(TB):
                            ins = nc.tensor.matmul(blk(bank[6], b), blk(dx, b), wout, start=True, stop=True)
                        ins.then_inc(s["base_in"], 1)
                    if 1 <= n <= NH:
                        h = n - 1
                        pe.wait_ge(s["hs_ready"], i * NH + h + 1 + HS_CREDIT)
                        pe.wait_ge(s["o_ready"], i * NH + h + O_CREDIT)
                        nc.tensor.matmul(bank[2][:], cw[:, h], hs[:, h % 2], start=True, stop=True).then_inc(s["c_in"], 1)
                    if 2 <= n <= NH + 1:
                        h = n - 2
                        pe.wait_ge(s["o_ready"], i * NH + h + 1 + O_CREDIT)
                        pe.wait_ge(s["o_stats"], i * NH + h + STATS_CREDIT)
                        turn(pe, bank[5], lambda b: blk(o_sb[:, h % 2], b)).then_inc(s["ot_in"], 1)
                        pe.wait_ge(s["share_ready"], i * NH + h - 1 + SHARE_CREDIT)
                        for b in range(TB):
                            ins = nc.tensor.matmul(blk(bank[3 + h % 2], b), blk(o_sb[:, h % 2], b), wz[:, h], start=True, stop=True)
                        ins.then_inc(s["p_in"], 1)
                if tail:
                    if n == 3:
                        pe.wait_ge(s["u_ready"], j + 1)
                        if heads:
                            pe.wait_ge(s["base_out"], i + 1)
                        turn(pe, bank[6], lambda b: u[:, b]).then_inc(s["u_in"], 1)
                    if n in (4, 5):
                        pe.wait_ge(s["uT_ready"], j + 1)
                        for c in (2 * n - 8, 2 * n - 7):
                            if c >= 2:
                                pe.wait_ge(s["f1_out"], j * HC + c - 1)
                            nc.tensor.matmul(bank[7 - c % 2][:], f1[:, c * P:(c + 1) * P], uT[:], start=True,
                                             stop=True).then_inc(s["f1_in"], 1)
                    if n == 6:
                        pe.wait_ge(s["f1_out"], (j + 1) * HC)
                        for c in range(HC):
                            ins = nc.tensor.matmul(bank[7][:], f2[:, c], gelu_sb[:, c], start=(c == 0), stop=(c == HC - 1))
                        ins.then_inc(s["f2_in"], 1)
                    if n == 8:
                        pe.wait_ge(s["hT_ready"], j + 1)
                        for b in range(TB):
                            ins = nc.tensor.matmul(blk(bank[6], b), blk(hT, b), proj, start=True, stop=True)
                        ins.then_inc(s["y_in"], 1)
                if heads and n == 9:
                    take_tile(i + 1)

            def turn_of(i, heads, tail):
                for n in range(SLOTS):
                    slot(i, n, heads, tail)

            take_tile(0)
            turn_of(0, True, False)
            with pe.Fori(1, TILES) as i:
                turn_of(i, True, True)
            turn_of(TILES, False, True)

        def mix_act(act, steps, s):
            act.sem_inc(s["ab_out"], AB_CREDIT)
            act.sem_inc(s["share_ready"], SHARE_CREDIT)

            def take_tile(i):
                act.wait_ge(s["xn_turned"], i + 1)
                nc.scalar.copy(xT[:], bank[7][:]).then_inc(s["xT_ready"], 1)

            def turn_of(i, heads, tail):
                j = i - 1
                for n in range(SLOTS):
                    if heads:
                        if n < NH:
                            act.wait_ge(s["hs_ready"], i * NH + n - 1 + HS_CREDIT)
                            act.wait_ge(s["ab_in"], i * 2 * NH + 2 * n + 1)
                            nc.scalar.activation(a_sb[:, n % 2], bank[0][:], ACT.Tanh, bias=ba[:, n:n + 1]).then_inc(s["ab_out"], 1)
                            act.wait_ge(s["ab_in"], i * 2 * NH + 2 * n + 2)
                            nc.scalar.activation(b_sb[:, n % 2], bank[1][:], ACT.Identity, bias=bb[:, n:n + 1]).then_inc(s["ab_out"], 1)
                        if n == 0:
                            act.wait_ge(s["dx_in"], i + 1)
                            nc.scalar.activation(dx[:], bank[6][:], ACT.Identity, bias=db).then_inc(s["dx_ready"], 1)
                        if n >= 3:
                            h = n - 3
                            act.wait_ge(s["head_rstd"], i * NH + h + 1)
                            act.wait_ge(s["p_in"], i * NH + h + 1)
                            act.wait_ge(s["added"], i * NH + h - 1 + ADD_CREDIT)
                            for b in range(TB):
                                ins = nc.scalar.mul(share[:, h % 2, b], blk(bank[3 + h % 2], b), head_rstd[:, h % 2, b:b + 1])
                            ins.then_inc(s["share_ready"], 1)
                    if tail:
                        if n == 3:
                            act.wait_ge(s["u_in"], j + 1)
                            nc.scalar.copy(uT[:], bank[6][:]).then_inc(s["uT_ready"], 1)
                        if n in (4, 5):
                            for c in (2 * n - 8, 2 * n - 7):
                                act.wait_ge(s["f1_in"], j * HC + c + 1)
                                nc.scalar.activation(gelu_sb[:, c], bank[7 - c % 2][:], ACT.Gelu, bias=f1b[:, c:c + 1])\
                                    .then_inc(s["f1_out"], 1)
                    if heads and n == 9:
                        take_tile(i + 1)

            take_tile(0)
            turn_of(0, True, False)
            with act.Fori(1, TILES) as i:
                turn_of(i, True, True)
            turn_of(TILES, False, True)

        def mix_pool(pool, steps, s):
            pool.sem_inc(s["added"], ADD_CREDIT)

            def turn_of(i, heads, tail):
                j = i - 1
                for n in range(SLOTS):
                    if tail and n == 0:
                        pool.wait_ge(s["z_stats"], j + 1)
                        pool.sem_inc(waits_apart, 1)
                        steps.link(nc.gpsimd.tensor_scalar(z_var[:], z_mv[:, :, 1], EPS, None, ALU.add))
                        nc.gpsimd.tensor_tensor(z_rstd[:], z_var[:], neg_half[:, 0:TB], ALU.pow).then_inc(s["z_rstd"], 1)
                    if heads and 2 <= n <= NH + 1:
                        h = n - 2
                        if not (isinstance(i, int) and i * NH + h == 0):
                            pool.wait_ge(s["head_rstd"], i * NH + h)
                        pool.wait_ge(s["o_stats"], i * NH + h + 1 + STATS_CREDIT)
                        pool.sem_inc(waits_apart, 1)
                        steps.link(nc.gpsimd.tensor_scalar(head_var[:], o_mv[:, h % 2, :, 1], EPS, None, ALU.add))
                        nc.gpsimd.tensor_tensor(head_rstd[:, h % 2], head_var[:], neg_half[:, 0:TB], ALU.pow)\
                            .then_inc(s["head_rstd"], 1)
                    if heads and n >= 3:
                        h = n - 3
                        if h == 0:
                            pool.wait_ge(s["base_out"], i + 1)
                        pool.wait_ge(s["share_ready"], i * NH + h + 1 + SHARE_CREDIT)
                        nc.gpsimd.tensor_tensor(z, z, share[:, h % 2], ALU.add).then_inc(s["added"], 1)
                        pool.wait_ge(s["added"], i * NH + h + 1 + ADD_CREDIT)
                    if heads and n == 6:
                        ln_rstd(pool, steps, s, i + 1)

            ln_rstd(pool, steps, s, 0)
            turn_of(0, True, False)
            with pool.Fori(1, TILES) as i:
                steps.enter(i - 1, 2 + NH)
                turn_of(i, True, True)
            steps.leave(TILES - 1)
            turn_of(TILES, False, True)

        def mix_dve(dve, steps, s):
            v = nc.vector
            dve.sem_inc(s["hs_ready"], HS_CREDIT)
            dve.sem_inc(s["o_ready"], O_CREDIT)
            dve.sem_inc(s["o_stats"], STATS_CREDIT)
            steps.link(v.memset(carry[:], 0.0))
            ln_stats(dve, steps, s, 0)
            ln_apply(dve, steps, s, 0, first=True)

            def turn_of(i, heads, tail):
                j = i - 1
                for n in range(SLOTS):
                    if heads and n < NH:
                        dve.wait_ge(s["ab_out"], i * 2 * NH + 2 * n + 2 + AB_CREDIT)
                        v.tensor_tensor_scan(hs[:, n % 2], a_sb[:, n % 2], b_sb[:, n % 2], carry[:, n:n + 1],
                                             ALU.mult, ALU.add).then_inc(s["hs_ready"], 1)
                    if heads and 1 <= n <= NH:
                        h = n - 1
                        dve.wait_ge(s["c_in"], i * NH + h + 1)
                        if h >= 2:
                            dve.wait_ge(s["p_in"], i * NH + h - 1)
                        v.scalar_tensor_tensor(o_sb[:, h % 2], bank[2][:], cb[:, h:h + 1], dx[:], ALU.add, ALU.mult)\
                            .then_inc(s["o_ready"], 1)
                    if tail and n == 0:
                        dve.wait_ge(s["added"], i * NH + ADD_CREDIT)
                        dve.sem_inc(waits_apart, 1)
                        for b in range(TB):
                            ins = v.bn_stats(z_stats[:, b], z[:, b])
                        steps.link_apart(ins)
                        for b in range(TB):
                            ins = v.bn_aggr(z_mv[:, b], z_stats[:, b])
                        ins.then_inc(s["z_stats"], 1)
                    if tail and n == 1:
                        dve.wait_ge(s["z_stats"], j + 1)
                        dve.wait_ge(s["z_rstd"], j + 1)
                        for b in range(TB):
                            ins = v.tensor_scalar(u[:, b], z[:, b], z_mv[:, b, 0:1], z_rstd[:, b:b + 1], ALU.subtract, ALU.mult)
                        steps.link(ins)
                        steps.link(v.tensor_tensor(u[:], u[:], ng_row.unsqueeze(1).broadcast_to([P, TB, P]), ALU.mult))
                        steps.link(v.tensor_tensor(u[:], u[:], nb_row.unsqueeze(1).broadcast_to([P, TB, P]), ALU.add))
                        v.tensor_tensor(u[:], u[:], z, ALU.add).then_inc(s["u_ready"], 1)
                    if heads:
                        if n == 1:
                            if tail:
                                dve.wait_ge(s["u_ready"], j + 1)
                            dve.wait_ge(s["base_in"], i + 1)
                            v.tensor_tensor(z, bank[6][:].rearrange("p (b e) -> p b e", b=TB),
                                            zrow[:].unsqueeze(1).broadcast_to([P, TB, P]), ALU.add).then_inc(s["base_out"], 1)
                        if n < NH:
                            dve.wait_ge(s["hs_ready"], i * NH + n + 1 + HS_CREDIT)
                            steps.done(v.tensor_scalar(carry[:, n:n + 1], hs[:, n % 2, TW - 1:TW], keep[:, bass.ds(i + 1, 1)],
                                                       None, ALU.mult))
                        if 2 <= n <= NH + 1:
                            h = n - 2
                            dve.wait_ge(s["ot_in"], i * NH + h + 1)
                            dve.sem_inc(waits_apart, 1)
                            for b in range(TB):
                                ins = v.bn_stats(o_stats[:, b], blk(bank[5], b))
                            if h >= 2:
                                dve.wait_ge(s["head_rstd"], i * NH + h - 1)
                            steps.link_apart(ins)
                            for b in range(TB):
                                ins = v.bn_aggr(o_mv[:, h % 2, b], o_stats[:, b])
                            ins.then_inc(s["o_stats"], 1)
                        if n == 5:
                            ln_stats(dve, steps, s, i + 1)
                        if n == 7:
                            ln_apply(dve, steps, s, i + 1)
                    if tail and n == 7:
                        dve.wait_ge(s["f2_in"], j + 1)
                        v.scalar_tensor_tensor(hT[:], bank[7][:], f2b, uT[:], ALU.add, ALU.add).then_inc(s["hT_ready"], 1)
                    if tail and n == 9:
                        dve.wait_ge(s["y_in"], j + 1)
                        tile = X[:, bass.ds(j * TB, TB)]
                        steps.link(v.tensor_tensor(tile, tile, projb_row.unsqueeze(1).broadcast_to([P, TB, P]), ALU.add))
                        v.tensor_tensor(tile, bank[6][:].rearrange("p (b e) -> p b e", b=TB), tile, ALU.add).then_inc(s["tile_done"], 1)

            turn_of(0, True, False)
            with dve.Fori(1, TILES) as i:
                steps.enter(i - 1, MIX_STEPS)
                turn_of(i, True, True)
            steps.leave(TILES - 1)
            turn_of(TILES, False, True)
            dve.wait_ge(s["tile_done"], TILES)
            dve.sem_inc(phase_done, 1)

        MIX_STEPS = 22

        yT = acc

        def tf_sems(p):
            return ln_sems(p) | {k: sem(f"{k}_{p}") for k in ("t_x_hi", "t_x_lo", "t_up_in", "t_up_out", "t_hi_done", "t_lo_done", "t_down_in",
                                                                "t_down_out", "t_back_in", "tile_done")}

        def tf_pe(pe, s):
            def turn_of(i, up, down):
                j = i - 1
                if up:
                    pe.wait_ge(s["xn_ready"], i + 1)
                    turn(pe, bank[7], lambda b: xn[:, b]).then_inc(s["xn_turned"], 1)
                if down:
                    for c in range(HC):
                        pe.wait_ge(s["t_lo_done"], j * HC + c + 1)
                        for k, half in enumerate((hid_hi, hid_lo)):
                            ins = nc.tensor.matmul(bank[4][:], t_r[:, 1, c * P:(c + 1) * P], half[:, c], start=(c == 0 and k == 0),
                                                   stop=(c == HC - 1 and k == 1))
                    ins.then_inc(s["t_down_in"], 1)
                if up:
                    pe.wait_ge(s["t_x_lo"], i + 1)
                    for c in range(HC):
                        nc.tensor.matmul(bank[c][:], t_r[:, 0, c * P:(c + 1) * P], x_hi[:], start=True, stop=False)
                        nc.tensor.matmul(bank[c][:], t_r[:, 0, c * P:(c + 1) * P], x_lo[:], start=False, stop=True)\
                            .then_inc(s["t_up_in"], 1)
                if down:
                    pe.wait_ge(s["t_down_out"], j + 1)
                    pe.wait_ge(s["tile_done"], j + 1)
                    turn(pe, bank[6], lambda b: blk(yT, b)).then_inc(s["t_back_in"], 1)

            turn_of(0, True, False)
            with pe.Fori(1, TILES) as i:
                turn_of(i, True, True)
            turn_of(TILES, False, True)

        def tf_act(act, steps, s):
            def turn_of(i, up, down):
                j = i - 1
                if up:
                    act.wait_ge(s["xn_turned"], i + 1)
                    nc.scalar.copy(x_hi[:], bank[7][:]).then_inc(s["t_x_hi"], 1)
                    nc.scalar.copy(xT[:], bank[7][:]).then_inc(s["xT_ready"], 1)
                if down:
                    act.wait_ge(s["t_down_in"], j + 1)
                    act.wait_ge(s["tile_done"], j + 1)
                    nc.scalar.activation(yT[:], bank[4][:], ACT.Identity, bias=b2).then_inc(s["t_down_out"], 1)
                if up:
                    for c in range(HC):
                        act.wait_ge(s["t_up_in"], i * HC + c + 1)
                        if down:
                            act.wait_ge(s["t_lo_done"], j * HC + c + 1)
                        nc.scalar.activation(hid[:, c], bank[c][:], ACT.Relu, bias=b1[:, c:c + 1]).then_inc(s["t_up_out"], 1)

            turn_of(0, True, False)
            with act.Fori(1, TILES) as i:
                turn_of(i, True, True)
            turn_of(TILES, False, True)

        def tf_pool(pool, steps, s):
            def rest_of_hidden(i):
                for c in range(HC):
                    pool.wait_ge(s["t_hi_done"], i * HC + c + 1)
                    nc.gpsimd.tensor_tensor(hid_lo[:, c], hid[:, c], hid_hi[:, c].bitcast(F32), ALU.subtract).then_inc(s["t_lo_done"], 1)

            ln_rstd(pool, steps, s, 0)
            ln_rstd(pool, steps, s, 1)
            rest_of_hidden(0)
            with pool.Fori(1, TILES) as i:
                steps.enter(i - 1, 1)
                ln_rstd(pool, steps, s, i + 1)
                rest_of_hidden(i)
            steps.leave(TILES - 1)

        def tf_dve(dve, steps, s):
            v = nc.vector

            def rest_of_x(i):
                dve.wait_ge(s["t_x_hi"], i + 1)
                dve.wait_ge(s["xT_ready"], i + 1)
                v.tensor_tensor(x_lo[:], xT[:], x_hi[:].bitcast(F32), ALU.subtract).then_inc(s["t_x_lo"], 1)

            def rest_of_hidden(i):
                for c in range(HC):
                    dve.wait_ge(s["t_up_out"], i * HC + c + 1)
                    dve.sem_inc(waits_apart, 1)
                    v.tensor_copy(hid_hi[:, c], hid[:, c]).then_inc(s["t_hi_done"], 1)

            dve.sem_inc(s["tile_done"], 1)
            ln_stats(dve, steps, s, 0)
            ln_apply(dve, steps, s, 0, first=True)
            ln_stats(dve, steps, s, 1)
            rest_of_x(0)
            rest_of_hidden(0)
            ln_apply(dve, steps, s, 1)

            def turn_of(i, ahead=True):
                j = i - 1
                if ahead:
                    ln_stats(dve, steps, s, i + 1)
                    rest_of_x(i)
                    ln_apply(dve, steps, s, i + 1)
                    rest_of_hidden(i)
                dve.wait_ge(s["t_back_in"], j + 1)
                tile = X[:, bass.ds(j * TB, TB)].rearrange("p b e -> p (b e)")
                nc.vector.scalar_tensor_tensor(tile, bank[6][:], 0.5, tile, ALU.mult, ALU.add).then_inc(s["tile_done"], 1)

            with dve.Fori(1, TILES) as i:
                steps.enter(i - 1, 1)
                turn_of(i)
            steps.leave(TILES - 1)
            turn_of(TILES, ahead=False)
            dve.wait_ge(s["tile_done"], TILES + 1)
            dve.sem_inc(phase_done, 1)

        GROUPS = LH * HD * HD // P
        qkvT = spare[:, 0:3]
        qkv_hi = hid_hi[:, 0:6]
        qkv_lo = hid_lo[:, 0:6]
        pick_f32 = spare[:, 0:4].rearrange("p a t -> p (a t)")
        pick_kq = hid_hi[:, 6:8].rearrange("p a (g n) -> p (a g) n", n=P)
        pick_v = hid_lo[:, 6:8].rearrange("p a (g n) -> p (a g) n", n=P)
        gather_p = spare[:, 4:6].rearrange("p a (g n) -> p (a g) n", n=P)
        v_rep = gate_b
        kv_prod = acc
        kv_sum = hid[:, 0:2]
        qkv_sum = hid[:, 2:4]
        ones_row = spare[:, 6]
        la_carry = sb("la_carry", [P, GROUPS])
        yT_la = spare[:, 7]

        def la_sems():
            return ln_sems(4) | {k: sem(f"la_{k}") for k in (
                "picks", "picks_r", "qkv_in", "qkv_hi", "qkv_lo", "v_in", "k_in", "q_in", "v_out", "kv_out", "q_out",
                "summed", "y_out", "o_in", "tile_done")}

        TPS = SEQ // TW
        V_CREDIT, ONES_CREDIT = 2, 1

        def la_pe(pe, s):
            def take_tile(i):
                pe.wait_ge(s["xn_ready"], i + 1)
                turn(pe, bank[7], lambda b: xn[:, b]).then_inc(s["xn_turned"], 1)

            def project(i, k):
                pe.wait_ge(s["xT_ready"], i + 1) if k == 0 else pe.wait_ge(s["qkv_hi"], 3 * i + k)
                nc.tensor.matmul(bank[7][:], (wv, wk, wq)[k], xT[:], start=True, stop=True).then_inc(s["qkv_in"], 1)

            def tile_of(i, half):
                def onto(dst, pick_m, k):
                    nc.tensor.matmul(dst, pick_m, qkv_hi[:, 3 * half + k], start=True, stop=False)
                    return nc.tensor.matmul(dst, pick_m, qkv_lo[:, 3 * half + k], start=False, stop=True)

                def sums(g):
                    pe.wait_ge(s["q_out"], i * GROUPS + g + 1 + V_CREDIT)
                    nc.tensor.matmul(bank[6][:], gather_p[:, g], qkv_sum[:, g % 2], start=(g == 0), stop=(g == GROUPS - 1),
                                     skip_group_check=True).then_inc(s["summed"], 1)

                pe.wait_ge(s["qkv_lo"], 3 * i + 3)
                for g in range(GROUPS):
                    pe.wait_ge(s["v_out"], i * GROUPS + g - 1 + V_CREDIT)
                    onto(bank[g % 2][:], pick_v[:, g], 0).then_inc(s["v_in"], 1)
                    pe.wait_ge(s["kv_out"], i * GROUPS + g - 1 + V_CREDIT)
                    onto(bank[2 + g % 2][:], pick_kq[:, g], 1).then_inc(s["k_in"], 1)
                    pe.wait_ge(s["q_out"], i * GROUPS + g - 1 + V_CREDIT)
                    onto(bank[4 + g % 2][:], pick_kq[:, g], 2).then_inc(s["q_in"], 1)
                    if g == 2:
                        pe.wait_ge(s["tile_done"], i + ONES_CREDIT)
                    if g >= 2:
                        sums(g - 2)
                    if g == 3:
                        take_tile(i + 1)
                    if g >= 5:
                        project(i + 1, g - 5)
                sums(GROUPS - 2)
                sums(GROUPS - 1)
                pe.wait_ge(s["y_out"], i + 1)
                for b in range(TB):
                    ins = nc.tensor.matmul(blk(bank[6], b), blk(yT_la, b), wo, start=True, stop=True)
                ins.then_inc(s["o_in"], 1)

            take_tile(0)
            for k in range(3):
                project(0, k)
            pe.wait_ge(s["picks_r"], 2)
            with pe.Fori(0, BATCHES) as q:
                for half in range(TPS):
                    tile_of(q * TPS + half, half)

        def la_act(act, steps, s):
            act.sem_inc(s["v_out"], V_CREDIT)

            def take_tile(i):
                act.wait_ge(s["xn_turned"], i + 1)
                nc.scalar.copy(xT[:], bank[7][:]).then_inc(s["xT_ready"], 1)

            def split_projection(i, half, k):
                act.wait_ge(s["qkv_in"], 3 * i + k + 1)
                if not (isinstance(i, int) and i == 0):
                    act.wait_ge(s["qkv_lo"], 3 * i - 3 + k + 1)
                nc.scalar.activation(qkvT[:, k], bank[7][:], ACT.Identity, bias=(bv, bk, bq)[k])
                nc.scalar.activation(qkv_hi[:, 3 * half + k], bank[7][:], ACT.Identity, bias=(bv, bk, bq)[k]).then_inc(s["qkv_hi"], 1)

            def tile_of(i, half):
                for g in range(GROUPS):
                    act.wait_ge(s["v_in"], i * GROUPS + g + 1)
                    act.wait_ge(s["kv_out"], i * GROUPS + g - 1 + V_CREDIT)
                    nc.scalar.copy(v_rep[:, g % 2], bank[g % 2][:]).then_inc(s["v_out"], 1)
                    if g == 3:
                        take_tile(i + 1)
                    if g >= 5:
                        split_projection(i + 1, 1 - half, g - 5)
                act.wait_ge(s["summed"], (i + 1) * GROUPS)
                nc.scalar.copy(yT_la, bank[6][:]).then_inc(s["y_out"], 1)

            take_tile(0)
            act.wait_ge(s["picks_r"], 2)
            for k in range(3):
                split_projection(0, 0, k)
            with act.Fori(0, BATCHES) as q:
                for half in range(TPS):
                    tile_of(q * TPS + half, half)

        def la_pool(pool, steps, s):
            g = nc.gpsimd
            ln_rstd(pool, steps, s, 0)
            kq = pick_f32[:, 0:GROUPS * P]
            vv = pick_f32[:, GROUPS * P:2 * GROUPS * P]
            pool.wait_ge(w_lo_ready, MLPS)
            g.memset(ones_row, 1.0)
            g.memset(kq, 0.0)
            g.memset(vv, 0.0)
            steps.link(g.memset(gather_p, 1.0))
            g.affine_select(kq.rearrange("f (g h p n) -> f g h p n", g=GROUPS, h=2, p=HD), kq.rearrange("f (g h p n) -> f g h p n", g=GROUPS, h=2, p=HD),
                            [[-2 * HD, GROUPS], [-HD, 2], [0, HD], [-1, HD]], ALU.not_equal, 1.0, base=0, channel_multiplier=1)
            g.affine_select(vv.rearrange("f (g h p n) -> f g h p n", g=GROUPS, h=2, p=HD), vv.rearrange("f (g h p n) -> f g h p n", g=GROUPS, h=2, p=HD),
                            [[-2 * HD, GROUPS], [-HD, 2], [-1, HD], [0, HD]], ALU.not_equal, 1.0, base=0, channel_multiplier=1)\
                .then_inc(s["picks"], 1)
            steps.link(g.affine_select(gather_p, gather_p, [[2 * HD * HD, GROUPS], [-HD, P]], ALU.is_ge, 0.0, base=0, channel_multiplier=1))
            g.affine_select(gather_p, gather_p, [[-2 * HD * HD, GROUPS], [HD, P]], ALU.is_ge, 0.0, base=HD - 1, channel_multiplier=-1)\
                .then_inc(s["picks"], 1)
            with pool.Fori(1, TILES + 1) as i:
                steps.enter(i - 1, 1)
                ln_rstd(pool, steps, s, i)
            steps.leave(TILES)

        def la_dve(dve, steps, s):
            v = nc.vector
            dve.sem_inc(s["kv_out"], V_CREDIT)
            dve.sem_inc(s["q_out"], V_CREDIT)
            dve.sem_inc(s["tile_done"], ONES_CREDIT)
            steps.done(v.memset(la_carry[:], 0.0))

            def rest_of_projection(i, half, k):
                dve.wait_ge(s["qkv_hi"], 3 * i + k + 1)
                v.tensor_tensor(qkv_lo[:, 3 * half + k], qkvT[:, k], qkv_hi[:, 3 * half + k].bitcast(F32), ALU.subtract)\
                    .then_inc(s["qkv_lo"], 1)

            def tile_of(i, half):
                def through_q(g):
                    dve.wait_ge(s["q_in"], i * GROUPS + g + 1)
                    if g >= 2:
                        dve.wait_ge(s["summed"], i * GROUPS + g - 1)
                    v.tensor_tensor(qkv_sum[:, g % 2], bank[4 + g % 2][:], kv_sum[:, g % 2], ALU.mult).then_inc(s["q_out"], 1)

                for g in range(GROUPS):
                    dve.wait_ge(s["v_out"], i * GROUPS + g + 1 + V_CREDIT)
                    dve.wait_ge(s["k_in"], i * GROUPS + g + 1)
                    v.tensor_tensor(kv_prod[:], bank[2 + g % 2][:], v_rep[:, g % 2], ALU.mult).then_inc(s["kv_out"], 1)
                    if g >= 1:
                        through_q(g - 1)
                    dve.wait_ge(s["kv_out"], i * GROUPS + g + 1 + V_CREDIT)
                    steps.link(v.tensor_tensor_scan(kv_sum[:, g % 2], ones_row, kv_prod[:], la_carry[:, g:g + 1], ALU.mult, ALU.add))
                    steps.done(v.tensor_scalar(la_carry[:, g:g + 1], kv_sum[:, g % 2, TW - 1:TW], keep[:, bass.ds(i + 1, 1)], None, ALU.mult))
                    if g == 0:
                        ln_stats(dve, steps, s, i + 1)
                    if g == 2:
                        ln_apply(dve, steps, s, i + 1)
                    if g >= 6:
                        rest_of_projection(i + 1, 1 - half, g - 6)
                through_q(GROUPS - 1)
                rest_of_projection(i + 1, 1 - half, 2)
                dve.wait_ge(s["o_in"], i + 1)
                tile = X[:, bass.ds(i * TB, TB)]
                steps.link(v.tensor_tensor(tile, tile, bo_row.unsqueeze(1).broadcast_to([P, TB, P]), ALU.add))
                v.tensor_tensor(tile, bank[6][:].rearrange("p (b e) -> p b e", b=TB), tile, ALU.add).then_inc(s["tile_done"], 1)

            ln_stats(dve, steps, s, 0)
            ln_apply(dve, steps, s, 0, first=True)
            dve.wait_ge(s["picks"], 2)
            v.tensor_copy(hid_hi[:, 6:8].rearrange("p a t -> p (a t)"), pick_f32[:, 0:GROUPS * P]).then_inc(s["picks_r"], 1)
            v.tensor_copy(hid_lo[:, 6:8].rearrange("p a t -> p (a t)"), pick_f32[:, GROUPS * P:2 * GROUPS * P]).then_inc(s["picks_r"], 1)
            for k in range(3):
                rest_of_projection(0, 0, k)
            with dve.Fori(0, BATCHES) as q:
                steps.enter(q, TPS * LA_STEPS)
                for half in range(TPS):
                    tile_of(q * TPS + half, half)
            steps.leave(BATCHES)
            dve.wait_ge(s["tile_done"], TILES + ONES_CREDIT)
            dve.sem_inc(phase_done, 1)

        LA_STEPS = 18

        moe_s = [moe_sems(0), moe_sems(2)]
        mix_s = [mix_sems()]
        tf_s = [tf_sems(3), tf_sems(5)]
        la_s = [la_sems()]
        block = ctx.enter_context(nc.Block())

        @block.sync
        def _(sp):
            sp.dma_start(X[:, 0:BLOCKS], t["x"].rearrange("(n p) d -> p n d", p=P)).then_inc(x_dma, 16)
            for e in range(MLPS):
                if e >= STAGES:
                    sp.wait_ge(w_lo_ready, e - STAGES + 1)
                sp.dma_start(w_stage[:, e % STAGES], t["w_mlp"][e]).then_inc(w_in[e % STAGES], 16)
            for dst, name in loads:
                sp.dma_start(dst[:], t[name]).then_inc(c_dma, 16)
            sp.dma_start(rows[:], t["rows"].partition_broadcast(P)).then_inc(c_dma, 16)
            sp.wait_ge(phase_done, 6)
            sp.dma_start(t["out"].rearrange("(n p) d -> p n d", p=P), X[:, 0:BLOCKS]).then_inc(stored, 16)
            sp.wait_ge(stored, 16)

        CONSTS = 10

        @block.gpsimd
        def _(pool):
            steps = Steps(pool, pool_steps_sem, waits_apart)
            g = nc.gpsimd
            g.memset(neg_half[:], -0.5).then_inc(const_ready, 1)
            g.memset(ones[:], 1.0 / P).then_inc(const_ready, 1)
            g.memset(X[:, BLOCKS:], 0.0).then_inc(const_ready, 1)
            g.iota(expert_no[:], [[1, EXPERTS]], base=0, channel_multiplier=0,
                   allow_small_or_imprecise_dtypes=True).then_inc(const_ready, 1)
            g.memset(ident[:], 0.0)
            g.memset(causal[:], 1.0)
            g.memset(same_head[:], 1.0)
            g.memset(head_of[:], 1.0)
            steps.link(g.memset(keep[:], 1.0))
            g.affine_select(ident[:], ident[:], [[-1, P]], ALU.not_equal, 1.0, base=0, channel_multiplier=1).then_inc(const_ready, 1)
            g.affine_select(causal[:], causal[:], [[1, P]], ALU.is_ge, 0.0, base=0, channel_multiplier=-1).then_inc(const_ready, 1)
            sh = same_head[:].rearrange("n (h d) -> n h d", d=HD)
            steps.link(g.affine_select(sh, sh, [[-HD, LH], [0, HD]], ALU.is_ge, 0.0, base=0, channel_multiplier=1))
            g.affine_select(sh, sh, [[HD, LH], [0, HD]], ALU.is_ge, 0.0, base=HD - 1, channel_multiplier=-1).then_inc(const_ready, 1)
            pool.wait_ge(const_ready, 7)
            g.tensor_tensor(head_of[:], same_head[:].rearrange("n (a j d) -> n a j d", j=4, d=HD)[:, 0, :, 0],
                            same_head[:].rearrange("n (a j d) -> n a j d", j=4, d=HD)[:, 1, :, 0], ALU.add).then_inc(const_ready, 1)
            pool.wait_ge(const_ready, 8)
            for a in range(2, 4):
                ins = g.tensor_tensor(head_of[:], head_of[:],
                                      same_head[:].rearrange("n (a j d) -> n a j d", j=4, d=HD)[:, a, :, 0], ALU.add)
                if a == 2:
                    steps.link(ins)
            ins.then_inc(const_ready, 1)
            g.memset(keep[:, 0:TILES:2], 0.0).then_inc(const_ready, 1)
            phase_setup_pool(pool, steps)
            moe_pool(pool, steps, moe_s[0])
            pool.wait_ge(phase_done, 1)
            mix_pool(pool, steps, mix_s[0])
            pool.wait_ge(phase_done, 2)
            moe_pool(pool, steps, moe_s[1])
            pool.wait_ge(phase_done, 3)
            tf_pool(pool, steps, tf_s[0])
            pool.wait_ge(phase_done, 4)
            la_pool(pool, steps, la_s[0])
            pool.wait_ge(phase_done, 5)
            tf_pool(pool, steps, tf_s[1])

        @block.tensor
        def _(pe):
            pe.wait_ge(const_ready, CONSTS)
            pe.wait_ge(c_dma, LOADED)
            pe.wait_ge(setup_dve, 1)
            phase_setup_pe(pe)
            moe_pe(pe, moe_s[0])
            pe.wait_ge(phase_done, 1)
            mix_pe(pe, mix_s[0])
            pe.wait_ge(phase_done, 2)
            moe_pe(pe, moe_s[1])
            pe.wait_ge(phase_done, 3)
            tf_pe(pe, tf_s[0])
            pe.wait_ge(phase_done, 4)
            la_pe(pe, la_s[0])
            pe.wait_ge(phase_done, 5)
            tf_pe(pe, tf_s[1])

        @block.scalar
        def _(act):
            steps = Steps(act, act_steps_sem, waits_apart)
            act.wait_ge(const_ready, CONSTS)
            split_weights_act(act)
            act.wait_ge(c_dma, LOADED)
            phase_setup_act(act, steps)
            moe_act(act, steps, moe_s[0])
            act.wait_ge(phase_done, 1)
            mix_act(act, steps, mix_s[0])
            act.wait_ge(phase_done, 2)
            moe_act(act, steps, moe_s[1])
            act.wait_ge(phase_done, 3)
            tf_act(act, steps, tf_s[0])
            act.wait_ge(phase_done, 4)
            la_act(act, steps, la_s[0])
            act.wait_ge(phase_done, 5)
            tf_act(act, steps, tf_s[1])

        @block.vector
        def _(dve):
            steps = Steps(dve, dve_steps_sem, waits_apart)
            dve.wait_ge(const_ready, CONSTS)
            split_weights_dve(dve)
            dve.wait_ge(c_dma, LOADED)
            dve.wait_ge(x_dma, 16)
            phase_setup_dve(dve, steps)
            moe_dve(dve, steps, moe_s[0])
            dve.wait_ge(phase_done, 1)
            mix_dve(dve, steps, mix_s[0])
            dve.wait_ge(phase_done, 2)
            moe_dve(dve, steps, moe_s[1])
            dve.wait_ge(phase_done, 3)
            tf_dve(dve, steps, tf_s[0])
            dve.wait_ge(phase_done, 4)
            la_dve(dve, steps, la_s[0])
            dve.wait_ge(phase_done, 5)
            tf_dve(dve, steps, tf_s[1])


def kernel(**inputs):
    import numpy as np
    from concourse.bacc import Bacc
    from concourse.bass_utils import run_bass_kernel_spmd

    a = {k: np.asarray(v) for k, v in inputs.items()}
    HC, W = a["L0_ffn_Wfc_s"].shape[1] // P, P
    att, ffn, la, tf = (lambda k: a["L0_attn_" + k]), (lambda k: a["L0_ffn_" + k]), (lambda k: a["L1_attn_" + k]), (lambda k: a["L1_ffn_" + k])
    mlps = lambda s, e: np.concatenate([s[None], e])
    chunked = lambda w: w.reshape(-1, HC, P, W)
    cols = [
        mlps(ffn("bfc_s"), ffn("bfc")).reshape(-1, P), mlps(ffn("bproj_s"), ffn("bproj")), ffn("Wr").T,
        att("Wa_b"), att("Wb_b"), att("C_b"), att("D_b")[None], att("hn_g"), att("hn_b"),
        att("ffn1_b").reshape(HC, P), att("ffn2_b")[None], la("bq")[None], la("bk")[None], tf("b1").reshape(HC, P), tf("b2")[None], la("bv")[None]]
    laid = {
        "x": a["L0_attn_emb"].reshape(-1, W),
        "w_mlp": np.concatenate([mlps(ffn("Wfc_s"), ffn("Wfc")), chunked(mlps(ffn("Wproj_s"), ffn("Wproj"))).transpose(0, 2, 1, 3)
                                 .reshape(-1, P, HC * W)], 2),
        "wa": att("Wa_w").transpose(2, 0, 1), "wb": att("Wb_w").transpose(2, 0, 1), "cw": att("C_w").transpose(2, 0, 1),
        "squares": np.stack([w.T for w in (att("D_w"), att("Wout_w"), att("proj_w"), la("Wq"), la("Wk"), la("Wv"), la("Wo"))], 1),
        "f1": att("ffn1_w").T, "f2": chunked(att("ffn2_w").T)[0].transpose(1, 0, 2),
        "w1": tf("W1").T, "w2": chunked(tf("W2").T)[0].transpose(1, 0, 2),
        "cols": np.concatenate(cols).T,
        "rows": np.concatenate([att("Wout_b"), att("proj_b"), att("norm_g"), att("norm_b"), la("bk"), la("bv"), la("bo"), att("head_w")]),
    }
    nc = Bacc("TRN2", target_bir_lowering=False, num_devices=1)
    arrays, t = {}, {}
    for name, v in laid.items():
        arrays["in_" + name] = np.ascontiguousarray(v)
        t[name] = nc.dram_tensor("in_" + name, v.shape, F32, kind="ExternalInput").ap()
    t["out"] = nc.dram_tensor("out_x", laid["x"].shape, F32, kind="ExternalOutput").ap()
    macaron_kernel(nc, t)
    got = run_bass_kernel_spmd(nc, [arrays], core_ids=[0]).results[0]["out_x"]
    return got.reshape(a["L0_attn_emb"].shape)
```

```python
from contextlib import ExitStack

import concourse.bass as bass
from concourse import mybir

F32 = mybir.dt.float32
F32R = mybir.dt.float32r
U32 = mybir.dt.uint32
ACT = mybir.ActivationFunctionType
ALU = mybir.AluOpType
AX_X = mybir.AxisListType.X

P = 128
EPS = 1e-5


class Steps:

    def __init__(self, eng, sem, apart):
        self.apart = apart
        self.eng, self.sem, self.total, self.turn, self.n = eng, sem, 0, 0, 0

    def done(self, ins):
        ins.then_inc(self.sem, 1)
        self.n += 1

    def wait(self):
        self.eng.wait_ge(self.sem, self.total + self.turn + self.n)

    def link(self, ins):
        self.done(ins)
        self.wait()

    def link_apart(self, ins):
        self.link(ins)
        self.eng.sem_inc(self.apart, 1)

    def enter(self, turn, per):
        self.total, self.n, self.turn, self.per = self.total + self.n, 0, turn * per, per

    def leave(self, turns):
        assert self.n == self.per
        self.total, self.turn, self.n = self.total + turns * self.per, 0, 0


def macaron_kernel(nc, t):
    E = P
    TOKENS, _ = t["x"].shape
    BATCHES = 4
    TB = 4
    TW = TB * P
    TILES = TOKENS // TW
    BLOCKS = TOKENS // P
    MLPS = t["w_mlp"].shape[0]
    EXPERTS = MLPS - 1
    HC = t["w_mlp"].shape[2] // (2 * P)
    NH = t["wa"].shape[1]
    LH = 16
    HD = E // LH
    SEQ = TOKENS // BATCHES
    assert TW * TILES == TOKENS and SEQ == 2 * TW

    with ExitStack() as ctx:
        def sb(name, shape, dt=F32):
            return ctx.enter_context(nc.sbuf_tensor(name, shape, dt))

        def sem(name):
            return ctx.enter_context(nc.semaphore(name))

        bank = [ctx.enter_context(nc.psum_tensor(f"bank{n}", [P, TW], F32)) for n in range(8)]

        X_before = sb("X", [P, TB + BLOCKS + TB, E])
        X = X_before[:, TB:]
        WM = 2 * HC * P
        STAGES = 4
        w_stage = sb("w_stage", [P, STAGES, WM])
        w_hi = sb("w_hi", [P, MLPS, WM], F32R)
        w_lo = sb("w_lo", [P, MLPS, WM], F32R)
        wa = sb("wa_sb", [P, NH, P])
        wb = sb("wb_sb", [P, NH, P])
        cw = sb("cw_sb", [P, NH, P])
        squares = sb("squares_sb", [P, 7, P])
        dw, wout, proj, wq, wk, wv, wo = (squares[:, n] for n in range(7))
        wkv = squares[:, 4:6]
        f1 = sb("f1_sb", [P, HC * P])
        f2 = sb("f2_sb", [P, HC, E])
        t1 = sb("t1_sb", [P, HC * P])
        t2 = sb("t2_sb", [P, HC, E])
        COLS = t["cols"].shape[1]
        cols = sb("cols_sb", [P, COLS])
        at = [0]

        def col(n):
            at[0] += n
            return cols[:, at[0] - n:at[0]]

        b_up, b_dn, wr, ba, bb, cb, db = col(MLPS * HC), col(MLPS), col(EXPERTS), col(NH), col(NH), col(NH), col(1)
        hn_g, hn_b, f1b, f2b, bq, bk, b1, b2 = col(NH), col(NH), col(HC), col(1), col(1), col(1), col(HC), col(1)
        bv = col(1)
        assert at[0] == COLS
        rows = sb("rows_sb", [P, t["rows"].shape[0]])
        woutb_row, projb_row, ng_row, nb_row, bk_row, bv_row, bo_row = (rows[:, P * n:P * n + P] for n in range(7))
        bkv_row = rows[:, 4 * P:6 * P]
        head_w = rows[:, 7 * P:7 * P + NH]

        ident = sb("ident", [P, P])
        ones = sb("ones", [P, P])
        same_head = sb("same_head", [P, P])
        head_of = sb("head_of", [P, 4])
        neg_half = sb("neg_half", [P, NH * TB])
        expert_no = sb("expert_no", [P, EXPERTS])
        keep = sb("keep", [P, TILES + 1])
        wz = sb("wz", [P, NH, P])
        zrow = sb("zrow", [P, P])

        stats = sb("stats", [P, TB, 6])
        mv = sb("mv", [P, TB, 2])
        var_eps = sb("var_eps", [P, TB])
        rstd = sb("rstd", [P, TB])
        xn = sb("xn", [P, TB, E])
        xT = sb("xT", [P, TW])
        hid = sb("hid", [P, HC, TW])
        hid_hi = sb("hid_hi", [P, 2 * HC, TW], F32R)
        hid_lo = sb("hid_lo", [P, 2 * HC, TW], F32R)
        x_hi = sb("x_hi", [P, TW], F32R)
        x_lo = sb("x_lo", [P, TW], F32R)
        ident_r = sb("ident_r", [P, P], F32R)
        acc = sb("acc", [P, TW])
        part = sb("part", [P, TW])
        gate_b = sb("gate_b", [P, 2, TW])

        c_dma = sem("weights_loaded")
        x_first_dma, x_rest_dma = sem("first_tile_loaded"), sem("other_tiles_loaded")
        const_ready = sem("const_ready")
        phase_done = sem("phase_done")
        stored = sem("stored")
        dve_steps_sem, pool_steps_sem, act_steps_sem = sem("dve_step"), sem("pool_step"), sem("act_step")
        waits_apart = sem("waits_apart")
        setup_pe, setup_dve = sem("setup_pe"), sem("setup_dve")

        early_dma = sem("setup_weights_loaded")
        early_loads = [(cols, "cols"), (t1, "w1"), (t2, "w2"), (squares, "squares")]
        late_loads = [(wa, "wa"), (wb, "wb"), (cw, "cw"), (f1, "f1"), (f2, "f2")]
        EARLY, LATE = 16 * (len(early_loads) + 1), 16 * len(late_loads)

        def ln_sems(p):
            return {k: sem(f"{k}_{p}") for k in ("stats_ready", "rstd_ready", "xn_ready", "xn_turned", "xT_ready")}

        def ln_stats(dve, steps, s, i):
            for b in range(TB):
                ins = nc.vector.bn_stats(stats[:, b], X[:, bass.ds(i * TB + b, 1)])
            steps.link_apart(ins)
            for b in range(TB):
                ins = nc.vector.bn_aggr(mv[:, b], stats[:, b])
            ins.then_inc(s["stats_ready"], 1)

        def ln_rstd(pool, steps, s, i):
            pool.wait_ge(s["stats_ready"], i + 1)
            pool.sem_inc(waits_apart, 1)
            steps.link(nc.gpsimd.tensor_scalar(var_eps[:], mv[:, :, 1], EPS, None, ALU.add))
            nc.gpsimd.tensor_tensor(rstd[:], var_eps[:], neg_half[:, 0:TB], ALU.pow).then_inc(s["rstd_ready"], 1)

        def ln_apply(dve, steps, s, i, first=False):
            dve.wait_ge(s["stats_ready"], i + 1)
            dve.wait_ge(s["rstd_ready"], i + 1)
            if not first:
                dve.wait_ge(s["xn_turned"], i)
            for b in range(TB):
                ins = nc.vector.tensor_scalar(xn[:, b:b + 1], X[:, bass.ds(i * TB + b, 1)], mv[:, b, 0:1],
                                              rstd[:, b:b + 1], ALU.subtract, ALU.mult)
            ins.then_inc(s["xn_ready"], 1)

        def turn(pe, out, src):
            for b in range(TB):
                ins = nc.tensor.transpose(out[:, b * P:(b + 1) * P], src(b), ident[:])
            return ins

        def blk(ap, b):
            return ap[:, b * P:(b + 1) * P]

        logits = sb("logits", [P, TB, EXPERTS])
        top = sb("top", [P, TB, 8])
        top_at = sb("top_at", [P, TB, 8], U32)
        top_no = sb("top_no", [P, TB, 2])
        lead = sb("lead", [P, TB])
        half_tanh = sb("half_tanh", [P, TB])
        g2 = sb("g2", [P, 2, TB])
        pick = sb("pick", [P, 2, TB, EXPERTS])
        gates = sb("gates", [P, TB, EXPERTS])
        gates_split = sb("gates_split", [P, TB, 2 * EXPERTS], F32R)
        two_rows = sb("two_rows", [P, EXPERTS], F32R)
        N = MLPS * HC
        w_in = [sem(f"w_in_{n}") for n in range(STAGES)]
        w_hi_ready, w_lo_ready = sem("w_hi_ready"), sem("w_lo_ready")

        def moe_sems(p):
            return ln_sems(p) | {k: sem(f"{k}_{p}") for k in (
                "x_hi_ready", "x_lo_ready", "logits_in", "lead_ready", "tanh_ready", "gates_ready", "gates_turned", "gates_T",
                "up_done", "gelu_done", "lo_done", "gate_in", "gate_out", "down_done", "down_used", "acc_added",
                "back_in", "tile_done")}

        LAG = HC
        RING = 6
        assert N % RING == 0 and N % 3 == 0 and N % HC == 0 and MLPS % 2 == 1 and TILES % 2 == 0
        xs_hi, xs_lo = [x_hi[:], hid_hi[:, RING]], [x_lo[:], hid_lo[:, RING]]
        gates_T = hid_hi[0:2 * EXPERTS, RING + 1]
        GELU_CREDIT, DOWN_CREDIT, USED_CREDIT, GATE_CREDIT, LO_CREDIT, ACC_CREDIT = 3, RING, 2, 1, HC, 1
        BACK_AT, TURN_GATES_AT, TAKE_AT, LOGITS_AT = 8, 9, 30, 35

        def gate_step(e):
            return 12 if e == 1 else HC * e + 6

        def down_bank(par, e):
            return bank[3 + (par + e) % 2]

        def hi_by_dve(n):
            return n % HC == 1

        def moe_pe(pe, s):
            def take_tile(i):
                pe.wait_ge(s["xn_ready"], i + 1)
                turn(pe, bank[7], lambda b: xn[:, b]).then_inc(s["xn_turned"], 1)

            def find_logits(i):
                pe.wait_ge(s["xT_ready"], i + 1)
                for b in range(TB):
                    ins = nc.tensor.matmul(bank[6][:, b * EXPERTS:(b + 1) * EXPERTS], blk(xT, b), wr, start=True, stop=True)
                ins.then_inc(s["logits_in"], 1)

            def back(i):
                pe.wait_ge(s["acc_added"], (i + 1) * EXPERTS + ACC_CREDIT)
                turn(pe, bank[7], lambda b: blk(acc, b)).then_inc(s["back_in"], 1)

            def up(i, par, n):
                if n == 0:
                    pe.wait_ge(s["x_lo_ready"], i + 1)
                pe.wait_ge(s["gelu_done"], i * N + n - 2 + GELU_CREDIT)
                e, c, out = n // HC, n % HC, bank[n % 3]
                span = slice(c * P, (c + 1) * P)
                nc.tensor.matmul(out[:], w_hi[:, e, span], xs_hi[par], start=True, stop=False)
                nc.tensor.matmul(out[:], w_lo[:, e, span], xs_hi[par], start=False, stop=False)
                nc.tensor.matmul(out[:], w_hi[:, e, span], xs_lo[par], start=False, stop=True).then_inc(s["up_done"], 1)

            def down(i, par, n):
                e, c, out = n // HC, n % HC, down_bank(par, n // HC)
                if c == 0:
                    pe.wait_ge(s["down_used"], i * MLPS + e - 1 + USED_CREDIT)
                pe.wait_ge(s["lo_done"], i * N + n + 1 + LO_CREDIT)
                span, q = slice((HC + c) * P, (HC + c + 1) * P), n % RING
                nc.tensor.matmul(out[:], w_hi[:, e, span], hid_hi[:, q], start=(c == 0), stop=False)
                nc.tensor.matmul(out[:], w_lo[:, e, span], hid_hi[:, q], start=False, stop=False)
                nc.tensor.matmul(out[:], w_hi[:, e, span], hid_lo[:, q], start=False, stop=(c == HC - 1)).then_inc(s["down_done"], 1)

            def turn_of(i, par):
                for n in range(LAG, N + LAG):
                    if n < N:
                        if s is moe_s[0] and par == 0 and n % HC == 0:
                            pe.wait_ge(w_lo_ready, n // HC + 1)
                        up(i, par, n)
                    else:
                        up(i + 1, 1 - par, n - N)
                    down(i, par, n - LAG)
                    if n == BACK_AT:
                        back(i - 1)
                    if n == TURN_GATES_AT:
                        pe.wait_ge(s["gates_ready"], i + 1)
                        for b in range(TB):
                            ins = nc.tensor.matmul(blk(bank[6][0:2 * EXPERTS], b), gates_split[:, b], ident_r[:], start=True, stop=True)
                        ins.then_inc(s["gates_turned"], 1)
                    for e in range(1, MLPS):
                        if n == gate_step(e):
                            if e == 1:
                                pe.wait_ge(s["gates_T"], i + 1)
                            pe.wait_ge(s["gate_out"], i * EXPERTS + e - 1 + GATE_CREDIT)
                            nc.tensor.matmul(bank[5][:], two_rows[0:2 * EXPERTS, e - 1:e].broadcast_to([2 * EXPERTS, P]), gates_T,
                                             start=True, stop=True).then_inc(s["gate_in"], 1)
                    if n == TAKE_AT:
                        pe.wait_ge(s["tile_done"], i + 1)
                        take_tile(i + 1)
                    if n == LOGITS_AT:
                        find_logits(i + 1)

            take_tile(0)
            find_logits(0)
            if s is moe_s[0]:
                pe.wait_ge(w_lo_ready, 1)
            for n in range(LAG):
                up(0, 0, n)
            with pe.Fori(0, TILES // 2) as j:
                turn_of(j * 2, 0)
                turn_of(j * 2 + 1, 1)
            back(TILES - 1)

        def split_weights_act(act, mlps):
            for e in mlps:
                act.wait_ge(w_in[e % STAGES], 16 * (e // STAGES + 1))
                nc.scalar.copy(w_hi[:, e], w_stage[:, e % STAGES]).then_inc(w_hi_ready, 1)

        def split_weights_dve(dve, mlps):
            for e in mlps:
                dve.wait_ge(w_in[e % STAGES], 16 * (e // STAGES + 1))
                dve.wait_ge(w_hi_ready, e + 1)
                nc.vector.tensor_tensor(w_lo[:, e], w_stage[:, e % STAGES], w_hi[:, e].bitcast(F32), ALU.subtract).then_inc(w_lo_ready, 1)

        def moe_act(act, steps, s):
            act.sem_inc(s["gelu_done"], GELU_CREDIT)
            act.sem_inc(s["gate_out"], GATE_CREDIT)

            def take_tile(i, par):
                act.wait_ge(s["xn_turned"], i + 1)
                nc.scalar.copy(xs_hi[par], bank[7][:]).then_inc(s["x_hi_ready"], 1)
                nc.scalar.copy(xT[:], bank[7][:]).then_inc(s["xT_ready"], 1)

            def gelu(i, n):
                act.wait_ge(s["up_done"], i * N + n + 1)
                act.wait_ge(s["lo_done"], i * N + n - 3 + LO_CREDIT)
                act.wait_ge(s["down_done"], i * N + n - RING + 1 + DOWN_CREDIT)
                bias = b_up[:, n:n + 1]
                if not hi_by_dve(n):
                    nc.scalar.activation(hid_hi[:, n % RING], bank[n % 3][:], ACT.Gelu_apprx_tanh, bias=bias)
                nc.scalar.activation(hid[:, n % HC], bank[n % 3][:], ACT.Gelu_apprx_tanh, bias=bias).then_inc(s["gelu_done"], 1)

            def turn_of(i, par):
                for n in range(LAG, N + LAG):
                    if n < N:
                        gelu(i, n)
                    else:
                        gelu(i + 1, n - N)
                    if n == LAG:
                        act.wait_ge(s["lead_ready"], i + 1)
                        nc.scalar.activation(half_tanh[:], lead[:], ACT.Tanh, scale=0.5).then_inc(s["tanh_ready"], 1)
                    if n == TURN_GATES_AT + 1:
                        act.wait_ge(s["gates_turned"], i + 1)
                        nc.scalar.copy(gates_T, bank[6][0:2 * EXPERTS]).then_inc(s["gates_T"], 1)
                    for e in range(1, MLPS):
                        if n == gate_step(e) + 1:
                            act.wait_ge(s["gate_in"], i * EXPERTS + e)
                            act.wait_ge(s["down_used"], i * MLPS + e - 1 + USED_CREDIT)
                            nc.scalar.copy(gate_b[:, e % 2], bank[5][:]).then_inc(s["gate_out"], 1)
                    if n == TAKE_AT + 1:
                        take_tile(i + 1, 1 - par)

            if s is moe_s[0]:
                split_weights_act(act, range(2 * STAGES))
            take_tile(0, 0)
            for n in range(LAG):
                gelu(0, n)
            if s is moe_s[0]:
                split_weights_act(act, range(2 * STAGES, MLPS))
            with act.Fori(0, TILES // 2) as j:
                turn_of(j * 2, 0)
                turn_of(j * 2 + 1, 1)

        def moe_pool(pool, steps, s):
            def turn_of(i):
                for e in range(1, MLPS):
                    if e == 4:
                        ln_rstd(pool, steps, s, i + 1)
                    pool.wait_ge(s["down_used"], i * MLPS + e + 1 + USED_CREDIT)
                    pool.wait_ge(s["acc_added"], i * EXPERTS + e - 1 + ACC_CREDIT)
                    nc.gpsimd.tensor_tensor(acc[:], acc[:], part[:], ALU.add).then_inc(s["acc_added"], 1)

            ln_rstd(pool, steps, s, 0)
            with pool.Fori(0, TILES // 2) as j:
                steps.enter(j, 2)
                turn_of(j * 2)
                turn_of(j * 2 + 1)
            steps.leave(TILES // 2)

        def moe_dve(dve, steps, s):
            v = nc.vector

            def rest_of_x(i, par):
                dve.wait_ge(s["x_hi_ready"], i + 1)
                dve.wait_ge(s["xT_ready"], i + 1)
                v.tensor_tensor(xs_lo[par], xT[:], xs_hi[par].bitcast(F32), ALU.subtract).then_inc(s["x_lo_ready"], 1)

            def route(i):
                dve.wait_ge(s["logits_in"], i + 1)
                steps.link_apart(v.tensor_copy(logits[:], bank[6][:, 0:TB * EXPERTS].rearrange("p (b e) -> p b e", b=TB)))
                for b in range(TB):
                    ins = v.max(top[:, b], logits[:, b])
                steps.link(ins)
                v.tensor_tensor(lead[:], top[:, :, 0], top[:, :, 1], ALU.subtract).then_inc(s["lead_ready"], 1)
                for b in range(TB):
                    ins = v.max_index(top_at[:, b], top[:, b], logits[:, b])
                steps.link(ins)
                steps.link(v.tensor_copy(top_no[:], top_at[:, :, 0:2]))
                for k in range(2):
                    ins = v.tensor_tensor(pick[:, k], expert_no[:].unsqueeze(1).broadcast_to([P, TB, EXPERTS]),
                                          top_no[:, :, k:k + 1].broadcast_to([P, TB, EXPERTS]), ALU.is_equal)
                steps.done(ins)

            def share_out(i):
                dve.wait_ge(s["tanh_ready"], i + 1)
                v.tensor_scalar(g2[:, 0], half_tanh[:], 0.5, 0.5, ALU.mult, ALU.add)
                steps.link(v.tensor_scalar(g2[:, 1], half_tanh[:], -0.5, 0.5, ALU.mult, ALU.add))
                for k in range(2):
                    ins = v.tensor_tensor(pick[:, k], pick[:, k],
                                          g2[:, k].unsqueeze(2).broadcast_to([P, TB, EXPERTS]), ALU.mult)
                steps.link(ins)
                steps.link(v.tensor_tensor(gates[:], pick[:, 0], pick[:, 1], ALU.add))
                steps.link(v.tensor_copy(gates_split[:, :, 0:EXPERTS], gates[:]))
                v.tensor_tensor(gates_split[:, :, EXPERTS:], gates[:], gates_split[:, :, 0:EXPERTS].bitcast(F32), ALU.subtract)\
                    .then_inc(s["gates_ready"], 1)

            def split_hidden(i, n):
                dve.wait_ge(s["gelu_done"], i * N + n + 1 + GELU_CREDIT)
                q = n % RING
                if hi_by_dve(n):
                    steps.link(v.tensor_copy(hid_hi[:, q], hid[:, n % HC]))
                v.tensor_tensor(hid_lo[:, q], hid[:, n % HC], hid_hi[:, q].bitcast(F32), ALU.subtract).then_inc(s["lo_done"], 1)

            def gather(i, par, e):
                dve.wait_ge(s["down_done"], i * N + (e + 1) * HC + DOWN_CREDIT)
                if e == 0:
                    dve.wait_ge(s["back_in"], i + 1)
                    ins = v.tensor_scalar(acc[:], down_bank(par, e)[:], b_dn[:, 0:1], None, ALU.add)
                else:
                    dve.wait_ge(s["gate_out"], i * EXPERTS + e + GATE_CREDIT)
                    dve.wait_ge(s["acc_added"], i * EXPERTS + e - 1 + ACC_CREDIT)
                    ins = v.scalar_tensor_tensor(part[:], down_bank(par, e)[:], b_dn[:, e:e + 1], gate_b[:, e % 2], ALU.add, ALU.mult)
                ins.then_inc(s["down_used"], 1)

            def add_tile(i):
                dve.wait_ge(s["back_in"], i + 2)
                tile = X_before[:, bass.ds((i + 1) * TB, TB)].rearrange("p b e -> p (b e)")
                v.scalar_tensor_tensor(tile, bank[7][:], 0.5, tile, ALU.mult, ALU.add).then_inc(s["tile_done"], 1)

            def turn_of(i, par):
                for n in range(LAG, N + LAG):
                    if n < N:
                        split_hidden(i, n)
                    else:
                        split_hidden(i + 1, n - N)
                    if n == 6:
                        share_out(i)
                    for e in range(MLPS - 1):
                        if n == (14 if e == 1 else HC * e + 9):
                            gather(i, par, e)
                    if n == 10:
                        add_tile(i - 1)
                    if n == 22:
                        ln_stats(dve, steps, s, i + 1)
                    if n == 27:
                        ln_apply(dve, steps, s, i + 1)
                    if n == 32:
                        rest_of_x(i + 1, 1 - par)
                    if n == 36:
                        route(i + 1)
                gather(i, par, MLPS - 1)

            dve.sem_inc(s["down_used"], USED_CREDIT)
            dve.sem_inc(s["down_done"], DOWN_CREDIT)
            dve.sem_inc(s["lo_done"], LO_CREDIT)
            v.memset(acc[:], 0.0).then_inc(s["acc_added"], ACC_CREDIT)
            if s is moe_s[0]:
                dve.wait_ge(x_first_dma, 16)
            ln_stats(dve, steps, s, 0)
            ln_apply(dve, steps, s, 0, first=True)
            rest_of_x(0, 0)
            route(0)
            if s is moe_s[0]:
                split_weights_dve(dve, range(STAGES, 2 * STAGES))
            for n in range(LAG):
                split_hidden(0, n)
            if s is moe_s[0]:
                split_weights_dve(dve, range(2 * STAGES, MLPS))
                dve.wait_ge(x_rest_dma, 16)
            with dve.Fori(0, TILES // 2) as j:
                steps.enter(j, MOE_STEPS)
                turn_of(j * 2, 0)
                turn_of(j * 2 + 1, 1)
            steps.leave(TILES // 2)
            add_tile(TILES - 1)
            dve.wait_ge(s["tile_done"], TILES + 1)
            dve.sem_inc(phase_done, 1)

        MOE_STEPS = 38

        gain = sb("gain", [P, NH])
        head_bias = sb("head_bias", [P, 1])
        thr = sb("thr", [P, 4])
        mags = sb("mags", [P, NH])
        tern = sb("tern", [P, HC * P])
        t_r = sb("t_r", [P, 2, HC * P], F32R)
        
        def phase_setup_pe(pe):
            pe.wait_ge(setup_dve, 1)
            nc.tensor.matmul(bank[1][:, 0:P], head_bias[:].broadcast_to([P, P]), wout, start=True, stop=True).then_inc(setup_pe, 1)
            pe.wait_ge(setup_dve, 2)
            for h in range(NH):
                ins = nc.tensor.matmul(bank[2 + h // 4][:, (h % 4) * P:(h % 4 + 1) * P], ones[:], wz[:, h], start=True, stop=True)
            ins.then_inc(setup_pe, 1)
            pe.wait_ge(setup_dve, 3)
            nc.tensor.matmul(bank[0][:, 0:2], ones[:], mags[:, 0:2], start=True, stop=True).then_inc(setup_pe, 1)

        def phase_setup_dve(dve, steps):
            v = nc.vector
            v.tensor_copy(ident_r[:], ident[:])
            v.tensor_tensor(two_rows[0:2 * EXPERTS], ident[0:2 * EXPERTS, 0:EXPERTS], ident[0:2 * EXPERTS, EXPERTS:2 * EXPERTS], ALU.add)
            v.tensor_tensor(mags[:, 0:NH], hn_b, head_w, ALU.mult)
            steps.link(v.tensor_tensor(gain[:], hn_g, head_w, ALU.mult))
            v.tensor_scalar(gain[:], gain[:], 1.0 / NH, None, ALU.mult)
            steps.link(v.tensor_reduce(head_bias[:], mags[:, 0:NH], AX_X, ALU.add))
            v.tensor_scalar(head_bias[:], head_bias[:], 1.0 / NH, None, ALU.mult).then_inc(setup_dve, 1)
            dve.wait_ge(setup_dve, 1)
            for h in range(NH):
                ins = v.tensor_scalar(wz[:, h], wout, gain[:, h:h + 1], None, ALU.mult)
            ins.then_inc(setup_dve, 1)
            flat2 = t2[:].rearrange("p c e -> p (c e)")
            v.tensor_scalar(tern[:], t1[:], -1.0, None, ALU.mult)
            steps.link(v.tensor_scalar(part[:], flat2, -1.0, None, ALU.mult))
            v.tensor_tensor(tern[:], tern[:], t1[:], ALU.max)
            steps.link(v.tensor_tensor(part[:], part[:], flat2, ALU.max))
            v.tensor_reduce(mags[:, 0:1], tern[:], AX_X, ALU.add)
            v.tensor_reduce(mags[:, 1:2], part[:], AX_X, ALU.add).then_inc(setup_dve, 1)
            split_weights_dve(dve, range(STAGES))
            dve.wait_ge(setup_pe, 1)
            v.tensor_tensor(zrow[:], bank[1][:, 0:P], woutb_row, ALU.add)
            dve.wait_ge(setup_pe, 3)
            steps.link(v.tensor_scalar(thr[:, 0:2], bank[0][:, 0:2], 1.0 / (HC * P), EPS, ALU.mult, ALU.add))
            steps.link(v.tensor_scalar(thr[:, 0:2], thr[:, 0:2], 0.5, None, ALU.mult))
            steps.link(v.tensor_scalar(thr[:, 2:4], thr[:, 0:2], -1.0, None, ALU.mult))
            v.tensor_scalar(tern[:], t1[:], thr[:, 2:3], None, ALU.is_lt)
            steps.link(v.tensor_scalar(part[:], flat2, thr[:, 3:4], None, ALU.is_lt))
            v.scalar_tensor_tensor(t_r[:, 0], t1[:], thr[:, 0:1], tern[:], ALU.is_gt, ALU.subtract)
            v.scalar_tensor_tensor(t_r[:, 1], flat2, thr[:, 1:2], part[:], ALU.is_gt, ALU.subtract)
            for q in range(2):
                half = wz[:, 4 * q:4 * q + 4].rearrange("p h e -> p (h e)")
                v.tensor_tensor(half, half, bank[2 + q][:], ALU.subtract)
            steps.link(v.tensor_scalar(wout, wout, 1.0 / NH, None, ALU.mult))

        spare = w_stage[:].rearrange("p a (n t) -> p (a n) t", t=TW)
        a_sb = spare[:, 0:2]
        b_sb = spare[:, 2:4]
        hs = spare[:, 4:6]
        o_sb = spare[:, 6:8]
        dx = part
        carry = sb("carry", [P, NH])
        o_stats = sb("o_stats", [P, TB, 6])
        o_mv = sb("o_mv", [P, 2, TB, 2])
        head_var = sb("head_var", [P, TB])
        head_rstd = sb("head_rstd", [P, 2, TB])
        share = gate_b[:].rearrange("p a (b e) -> p a b e", b=TB)
        z = t1[:].rearrange("p (b e) -> p b e", b=TB)
        u = t2
        z_stats = sb("z_stats", [P, TB, 6])
        z_mv = sb("z_mv", [P, TB, 2])
        z_rstd = sb("z_rstd", [P, TB])
        z_var = sb("z_var", [P, TB])
        uT = acc
        hT = tern
        gelu_sb = hid
        as_heads = lambda ap: ap.rearrange("p a (g n) -> p (a g) n", n=P)
        wa_parts, wb_parts = ([as_heads(h[:, q:q + 2]) for h in (hid_hi, hid_lo)] for q in (0, 2))
        dw_parts = [h[:, 4, 0:P] for h in (hid_hi, hid_lo)]

        def mix_sems():
            return ln_sems(1) | {k: sem(f"mix_{k}") for k in (
                "w_hi_ready", "w_lo_ready", "x_hi_ready", "x_lo_ready",
                "dx_in", "dx_ready", "ab_in", "ab_out", "hs_ready", "c_in", "o_ready", "ot_in", "o_stats", "p_in",
                "head_rstd", "share_ready", "added", "base_in", "base_out", "z_stats", "z_rstd", "u_ready", "u_in", "uT_ready",
                "f1_in", "f1_out", "f2_in", "hT_ready", "y_in", "tile_done")}

        SLOTS = NH + 3
        AB_CREDIT, HS_CREDIT, O_CREDIT, SHARE_CREDIT, ADD_CREDIT, STATS_CREDIT = 2, 1, 1, 2, 2, 1

        def mix_pe(pe, s):
            def take_tile(i):
                pe.wait_ge(s["xn_ready"], i + 1)
                turn(pe, bank[7], lambda b: xn[:, b]).then_inc(s["xn_turned"], 1)

            def project(out, w, x_hi, x_lo):
                nc.tensor.matmul(out[:], w[0], x_hi, start=True, stop=False)
                nc.tensor.matmul(out[:], w[1], x_hi, start=False, stop=False)
                return nc.tensor.matmul(out[:], w[0], x_lo, start=False, stop=True)

            def slot(i, n, heads, tail):
                j = i - 1
                if heads:
                    if n == 0:
                        pe.wait_ge(s["x_lo_ready"], i + 1)
                    if n < NH:
                        for k, w in enumerate((wa_parts, wb_parts)):
                            pe.wait_ge(s["ab_out"], i * 2 * NH + 2 * n + k - 1 + AB_CREDIT)
                            project(bank[k], [half[:, n] for half in w], x_hi[:], x_lo[:]).then_inc(s["ab_in"], 1)
                    if n == 0:
                        if tail:
                            pe.wait_ge(s["tile_done"], j)
                        project(bank[6], dw_parts, x_hi[:], x_lo[:]).then_inc(s["dx_in"], 1)
                    if n == 1:
                        pe.wait_ge(s["dx_ready"], i + 1)
                        for b in range(TB):
                            ins = nc.tensor.matmul(blk(bank[6], b), blk(dx, b), wout, start=True, stop=True)
                        ins.then_inc(s["base_in"], 1)
                    if 1 <= n <= NH:
                        h = n - 1
                        pe.wait_ge(s["hs_ready"], i * NH + h + 1 + HS_CREDIT)
                        pe.wait_ge(s["o_ready"], i * NH + h + O_CREDIT)
                        nc.tensor.matmul(bank[2][:], cw[:, h], hs[:, h % 2], start=True, stop=True).then_inc(s["c_in"], 1)
                    if 2 <= n <= NH + 1:
                        h = n - 2
                        pe.wait_ge(s["o_ready"], i * NH + h + 1 + O_CREDIT)
                        pe.wait_ge(s["o_stats"], i * NH + h + STATS_CREDIT)
                        turn(pe, bank[5], lambda b: blk(o_sb[:, h % 2], b)).then_inc(s["ot_in"], 1)
                        pe.wait_ge(s["share_ready"], i * NH + h - 1 + SHARE_CREDIT)
                        for b in range(TB):
                            ins = nc.tensor.matmul(blk(bank[3 + h % 2], b), blk(o_sb[:, h % 2], b), wz[:, h], start=True, stop=True)
                        ins.then_inc(s["p_in"], 1)
                if tail:
                    if n == 3:
                        pe.wait_ge(s["u_ready"], j + 1)
                        if heads:
                            pe.wait_ge(s["base_out"], i + 1)
                        turn(pe, bank[6], lambda b: u[:, b]).then_inc(s["u_in"], 1)
                    if n in (4, 5):
                        pe.wait_ge(s["uT_ready"], j + 1)
                        for c in (2 * n - 8, 2 * n - 7):
                            if c >= 2:
                                pe.wait_ge(s["f1_out"], j * HC + c - 1)
                            nc.tensor.matmul(bank[7 - c % 2][:], f1[:, c * P:(c + 1) * P], uT[:], start=True,
                                             stop=True).then_inc(s["f1_in"], 1)
                    if n == 6:
                        pe.wait_ge(s["f1_out"], (j + 1) * HC)
                        for c in range(HC):
                            ins = nc.tensor.matmul(bank[7][:], f2[:, c], gelu_sb[:, c], start=(c == 0), stop=(c == HC - 1))
                        ins.then_inc(s["f2_in"], 1)
                    if n == 8:
                        pe.wait_ge(s["hT_ready"], j + 1)
                        for b in range(TB):
                            ins = nc.tensor.matmul(blk(bank[6], b), blk(hT, b), proj, start=True, stop=True)
                        ins.then_inc(s["y_in"], 1)
                if heads and n == 8:
                    take_tile(i + 1)

            def turn_of(i, heads, tail):
                for n in range(SLOTS):
                    slot(i, n, heads, tail)

            take_tile(0)
            pe.wait_ge(s["w_lo_ready"], 3)
            turn_of(0, True, False)
            with pe.Fori(1, TILES) as i:
                turn_of(i, True, True)
            turn_of(TILES, False, True)

        def mix_act(act, steps, s):
            act.sem_inc(s["ab_out"], AB_CREDIT)
            act.sem_inc(s["share_ready"], SHARE_CREDIT)

            def take_tile(i):
                act.wait_ge(s["xn_turned"], i + 1)
                nc.scalar.copy(x_hi[:], bank[7][:]).then_inc(s["x_hi_ready"], 1)

            def turn_of(i, heads, tail):
                j = i - 1
                for n in range(SLOTS):
                    if heads:
                        if n < NH:
                            act.wait_ge(s["hs_ready"], i * NH + n - 1 + HS_CREDIT)
                            act.wait_ge(s["ab_in"], i * 2 * NH + 2 * n + 1)
                            nc.scalar.activation(a_sb[:, n % 2], bank[0][:], ACT.Tanh, bias=ba[:, n:n + 1]).then_inc(s["ab_out"], 1)
                            act.wait_ge(s["ab_in"], i * 2 * NH + 2 * n + 2)
                            nc.scalar.activation(b_sb[:, n % 2], bank[1][:], ACT.Identity, bias=bb[:, n:n + 1]).then_inc(s["ab_out"], 1)
                        if n == 0:
                            act.wait_ge(s["dx_in"], i + 1)
                            nc.scalar.activation(dx[:], bank[6][:], ACT.Identity, bias=db).then_inc(s["dx_ready"], 1)
                        if n >= 3:
                            h = n - 3
                            act.wait_ge(s["head_rstd"], i * NH + h + 1)
                            act.wait_ge(s["p_in"], i * NH + h + 1)
                            act.wait_ge(s["added"], i * NH + h - 1 + ADD_CREDIT)
                            for b in range(TB):
                                ins = nc.scalar.mul(share[:, h % 2, b], blk(bank[3 + h % 2], b), head_rstd[:, h % 2, b:b + 1])
                            ins.then_inc(s["share_ready"], 1)
                    if tail:
                        if n == 3:
                            act.wait_ge(s["u_in"], j + 1)
                            nc.scalar.copy(uT[:], bank[6][:]).then_inc(s["uT_ready"], 1)
                        if n in (4, 5):
                            for c in (2 * n - 8, 2 * n - 7):
                                act.wait_ge(s["f1_in"], j * HC + c + 1)
                                nc.scalar.activation(gelu_sb[:, c], bank[7 - c % 2][:], ACT.Gelu, bias=f1b[:, c:c + 1])\
                                    .then_inc(s["f1_out"], 1)
                    if heads and n == 8:
                        take_tile(i + 1)

            for w, parts in ((wa[:], wa_parts), (wb[:], wb_parts), (dw, dw_parts)):
                nc.scalar.copy(parts[0], w).then_inc(s["w_hi_ready"], 1)
            take_tile(0)
            turn_of(0, True, False)
            with act.Fori(1, TILES) as i:
                turn_of(i, True, True)
            turn_of(TILES, False, True)

        def mix_pool(pool, steps, s):
            pool.sem_inc(s["added"], ADD_CREDIT)

            def turn_of(i, heads, tail):
                j = i - 1
                for n in range(SLOTS):
                    if tail and n == 0:
                        pool.wait_ge(s["z_stats"], j + 1)
                        pool.sem_inc(waits_apart, 1)
                        steps.link(nc.gpsimd.tensor_scalar(z_var[:], z_mv[:, :, 1], EPS, None, ALU.add))
                        nc.gpsimd.tensor_tensor(z_rstd[:], z_var[:], neg_half[:, 0:TB], ALU.pow).then_inc(s["z_rstd"], 1)
                    if heads and 2 <= n <= NH + 1:
                        h = n - 2
                        if not (isinstance(i, int) and i * NH + h == 0):
                            pool.wait_ge(s["head_rstd"], i * NH + h)
                        pool.wait_ge(s["o_stats"], i * NH + h + 1 + STATS_CREDIT)
                        pool.sem_inc(waits_apart, 1)
                        steps.link(nc.gpsimd.tensor_scalar(head_var[:], o_mv[:, h % 2, :, 1], EPS, None, ALU.add))
                        nc.gpsimd.tensor_tensor(head_rstd[:, h % 2], head_var[:], neg_half[:, 0:TB], ALU.pow)\
                            .then_inc(s["head_rstd"], 1)
                    if heads and n >= 3:
                        h = n - 3
                        if h == 0:
                            pool.wait_ge(s["base_out"], i + 1)
                        pool.wait_ge(s["share_ready"], i * NH + h + 1 + SHARE_CREDIT)
                        nc.gpsimd.tensor_tensor(z, z, share[:, h % 2], ALU.add).then_inc(s["added"], 1)
                        pool.wait_ge(s["added"], i * NH + h + 1 + ADD_CREDIT)
                    if heads and n == 6:
                        ln_rstd(pool, steps, s, i + 1)

            ln_rstd(pool, steps, s, 0)
            turn_of(0, True, False)
            with pool.Fori(1, TILES) as i:
                steps.enter(i - 1, 2 + NH)
                turn_of(i, True, True)
            steps.leave(TILES - 1)
            turn_of(TILES, False, True)

        def mix_dve(dve, steps, s):
            v = nc.vector
            dve.sem_inc(s["hs_ready"], HS_CREDIT)
            dve.sem_inc(s["o_ready"], O_CREDIT)
            dve.sem_inc(s["o_stats"], STATS_CREDIT)
            steps.link(v.memset(carry[:], 0.0))
            ln_stats(dve, steps, s, 0)
            dve.wait_ge(s["w_hi_ready"], 3)
            for n, (w, parts) in enumerate(((wa[:], wa_parts), (wb[:], wb_parts), (dw, dw_parts))):
                if n == 1:
                    ln_apply(dve, steps, s, 0, first=True)
                v.tensor_tensor(parts[1], w, parts[0].bitcast(F32), ALU.subtract).then_inc(s["w_lo_ready"], 1)

            def rest_of_x(i):
                dve.wait_ge(s["x_hi_ready"], i + 1)
                v.tensor_tensor(x_lo[:], bank[7][:], x_hi[:].bitcast(F32), ALU.subtract).then_inc(s["x_lo_ready"], 1)

            def turn_of(i, heads, tail):
                j = i - 1
                for n in range(SLOTS):
                    if heads and n < NH:
                        dve.wait_ge(s["ab_out"], i * 2 * NH + 2 * n + 2 + AB_CREDIT)
                        v.tensor_tensor_scan(hs[:, n % 2], a_sb[:, n % 2], b_sb[:, n % 2], carry[:, n:n + 1],
                                             ALU.mult, ALU.add).then_inc(s["hs_ready"], 1)
                    if heads and 1 <= n <= NH:
                        h = n - 1
                        dve.wait_ge(s["c_in"], i * NH + h + 1)
                        if h >= 2:
                            dve.wait_ge(s["p_in"], i * NH + h - 1)
                        v.scalar_tensor_tensor(o_sb[:, h % 2], bank[2][:], cb[:, h:h + 1], dx[:], ALU.add, ALU.mult)\
                            .then_inc(s["o_ready"], 1)
                    if tail and n == 0:
                        dve.wait_ge(s["added"], i * NH + ADD_CREDIT)
                        dve.sem_inc(waits_apart, 1)
                        for b in range(TB):
                            ins = v.bn_stats(z_stats[:, b], z[:, b])
                        steps.link_apart(ins)
                        for b in range(TB):
                            ins = v.bn_aggr(z_mv[:, b], z_stats[:, b])
                        ins.then_inc(s["z_stats"], 1)
                    if tail and n == 1:
                        dve.wait_ge(s["z_stats"], j + 1)
                        dve.wait_ge(s["z_rstd"], j + 1)
                        for b in range(TB):
                            ins = v.tensor_scalar(u[:, b], z[:, b], z_mv[:, b, 0:1], z_rstd[:, b:b + 1], ALU.subtract, ALU.mult)
                        steps.link(ins)
                        steps.link(v.tensor_tensor(u[:], u[:], ng_row.unsqueeze(1).broadcast_to([P, TB, P]), ALU.mult))
                        steps.link(v.tensor_tensor(u[:], u[:], nb_row.unsqueeze(1).broadcast_to([P, TB, P]), ALU.add))
                        v.tensor_tensor(u[:], u[:], z, ALU.add).then_inc(s["u_ready"], 1)
                    if heads:
                        if n == 1:
                            if tail:
                                dve.wait_ge(s["u_ready"], j + 1)
                            dve.wait_ge(s["base_in"], i + 1)
                            v.tensor_tensor(z, bank[6][:].rearrange("p (b e) -> p b e", b=TB),
                                            zrow[:].unsqueeze(1).broadcast_to([P, TB, P]), ALU.add).then_inc(s["base_out"], 1)
                        if n < NH:
                            dve.wait_ge(s["hs_ready"], i * NH + n + 1 + HS_CREDIT)
                            steps.done(v.tensor_scalar(carry[:, n:n + 1], hs[:, n % 2, TW - 1:TW], keep[:, bass.ds(i + 1, 1)],
                                                       None, ALU.mult))
                        if 2 <= n <= NH + 1:
                            h = n - 2
                            dve.wait_ge(s["ot_in"], i * NH + h + 1)
                            dve.sem_inc(waits_apart, 1)
                            for b in range(TB):
                                ins = v.bn_stats(o_stats[:, b], blk(bank[5], b))
                            if h >= 2:
                                dve.wait_ge(s["head_rstd"], i * NH + h - 1)
                            steps.link_apart(ins)
                            for b in range(TB):
                                ins = v.bn_aggr(o_mv[:, h % 2, b], o_stats[:, b])
                            ins.then_inc(s["o_stats"], 1)
                        if n == 5:
                            ln_stats(dve, steps, s, i + 1)
                        if n == 7:
                            ln_apply(dve, steps, s, i + 1)
                        if n == 9:
                            rest_of_x(i + 1)
                    if tail and n == 7:
                        dve.wait_ge(s["f2_in"], j + 1)
                        v.scalar_tensor_tensor(hT[:], bank[7][:], f2b, uT[:], ALU.add, ALU.add).then_inc(s["hT_ready"], 1)
                    if tail and n == 9:
                        dve.wait_ge(s["y_in"], j + 1)
                        tile = X[:, bass.ds(j * TB, TB)]
                        steps.link(v.tensor_tensor(tile, tile, projb_row.unsqueeze(1).broadcast_to([P, TB, P]), ALU.add))
                        v.tensor_tensor(tile, bank[6][:].rearrange("p (b e) -> p b e", b=TB), tile, ALU.add).then_inc(s["tile_done"], 1)

            rest_of_x(0)
            turn_of(0, True, False)
            with dve.Fori(1, TILES) as i:
                steps.enter(i - 1, MIX_STEPS)
                turn_of(i, True, True)
            steps.leave(TILES - 1)
            turn_of(TILES, False, True)
            dve.wait_ge(s["tile_done"], TILES)
            dve.sem_inc(phase_done, 1)

        MIX_STEPS = 22

        yT = acc

        def tf_sems(p):
            return ln_sems(p) | {k: sem(f"{k}_{p}") for k in ("t_x_hi", "t_x_lo", "t_up_in", "t_up_out", "t_hi_done", "t_lo_done", "t_down_in",
                                                                "t_down_out", "t_back_in", "tile_done")}

        def tf_pe(pe, s):
            def turn_of(i, up, down):
                j = i - 1
                if up:
                    pe.wait_ge(s["xn_ready"], i + 1)
                    turn(pe, bank[7], lambda b: xn[:, b]).then_inc(s["xn_turned"], 1)
                if down:
                    for c in range(HC):
                        pe.wait_ge(s["t_lo_done"], j * HC + c + 1)
                        for k, half in enumerate((hid_hi, hid_lo)):
                            ins = nc.tensor.matmul(bank[4][:], t_r[:, 1, c * P:(c + 1) * P], half[:, c], start=(c == 0 and k == 0),
                                                   stop=(c == HC - 1 and k == 1))
                    ins.then_inc(s["t_down_in"], 1)
                if up:
                    pe.wait_ge(s["t_x_lo"], i + 1)
                    for c in range(HC):
                        nc.tensor.matmul(bank[c][:], t_r[:, 0, c * P:(c + 1) * P], x_hi[:], start=True, stop=False)
                        nc.tensor.matmul(bank[c][:], t_r[:, 0, c * P:(c + 1) * P], x_lo[:], start=False, stop=True)\
                            .then_inc(s["t_up_in"], 1)
                if down:
                    pe.wait_ge(s["t_down_out"], j + 1)
                    pe.wait_ge(s["tile_done"], j + 1)
                    turn(pe, bank[6], lambda b: blk(yT, b)).then_inc(s["t_back_in"], 1)

            turn_of(0, True, False)
            with pe.Fori(1, TILES) as i:
                turn_of(i, True, True)
            turn_of(TILES, False, True)

        def tf_act(act, steps, s):
            def turn_of(i, up, down):
                j = i - 1
                if up:
                    act.wait_ge(s["xn_turned"], i + 1)
                    nc.scalar.copy(x_hi[:], bank[7][:]).then_inc(s["t_x_hi"], 1)
                    nc.scalar.copy(xT[:], bank[7][:]).then_inc(s["xT_ready"], 1)
                if down:
                    act.wait_ge(s["t_down_in"], j + 1)
                    act.wait_ge(s["tile_done"], j + 1)
                    nc.scalar.activation(yT[:], bank[4][:], ACT.Identity, bias=b2).then_inc(s["t_down_out"], 1)
                if up:
                    for c in range(HC):
                        act.wait_ge(s["t_up_in"], i * HC + c + 1)
                        if down:
                            act.wait_ge(s["t_lo_done"], j * HC + c + 1)
                        nc.scalar.activation(hid[:, c], bank[c][:], ACT.Relu, bias=b1[:, c:c + 1]).then_inc(s["t_up_out"], 1)

            turn_of(0, True, False)
            with act.Fori(1, TILES) as i:
                turn_of(i, True, True)
            turn_of(TILES, False, True)

        def tf_pool(pool, steps, s):
            def rest_of_hidden(i):
                for c in range(HC):
                    pool.wait_ge(s["t_hi_done"], i * HC + c + 1)
                    nc.gpsimd.tensor_tensor(hid_lo[:, c], hid[:, c], hid_hi[:, c].bitcast(F32), ALU.subtract).then_inc(s["t_lo_done"], 1)

            ln_rstd(pool, steps, s, 0)
            ln_rstd(pool, steps, s, 1)
            rest_of_hidden(0)
            with pool.Fori(1, TILES) as i:
                steps.enter(i - 1, 1)
                ln_rstd(pool, steps, s, i + 1)
                rest_of_hidden(i)
            steps.leave(TILES - 1)

        def tf_dve(dve, steps, s):
            v = nc.vector

            def rest_of_x(i):
                dve.wait_ge(s["t_x_hi"], i + 1)
                dve.wait_ge(s["xT_ready"], i + 1)
                v.tensor_tensor(x_lo[:], xT[:], x_hi[:].bitcast(F32), ALU.subtract).then_inc(s["t_x_lo"], 1)

            def rest_of_hidden(i):
                for c in range(HC):
                    dve.wait_ge(s["t_up_out"], i * HC + c + 1)
                    dve.sem_inc(waits_apart, 1)
                    v.tensor_copy(hid_hi[:, c], hid[:, c]).then_inc(s["t_hi_done"], 1)

            dve.sem_inc(s["tile_done"], 1)
            ln_stats(dve, steps, s, 0)
            ln_apply(dve, steps, s, 0, first=True)
            ln_stats(dve, steps, s, 1)
            rest_of_x(0)
            rest_of_hidden(0)
            ln_apply(dve, steps, s, 1)

            def turn_of(i, ahead=True):
                j = i - 1
                if ahead:
                    ln_stats(dve, steps, s, i + 1)
                    rest_of_x(i)
                    ln_apply(dve, steps, s, i + 1)
                    rest_of_hidden(i)
                dve.wait_ge(s["t_back_in"], j + 1)
                tile = X[:, bass.ds(j * TB, TB)].rearrange("p b e -> p (b e)")
                nc.vector.scalar_tensor_tensor(tile, bank[6][:], 0.5, tile, ALU.mult, ALU.add).then_inc(s["tile_done"], 1)

            with dve.Fori(1, TILES) as i:
                steps.enter(i - 1, 1)
                turn_of(i)
            steps.leave(TILES - 1)
            turn_of(TILES, ahead=False)
            dve.wait_ge(s["tile_done"], TILES + 1)
            dve.sem_inc(phase_done, 1)

        GROUPS = LH * HD * HD // P
        qkvT = spare[:, 0:3]
        qkv_hi = hid_hi[:, 0:6]
        qkv_lo = hid_lo[:, 0:6]
        pick_f32 = spare[:, 0:4].rearrange("p a t -> p (a t)")
        pick_kq = hid_hi[:, 6:8].rearrange("p a (g n) -> p (a g) n", n=P)
        pick_v = hid_lo[:, 6:8].rearrange("p a (g n) -> p (a g) n", n=P)
        gather_p = spare[:, 4:6].rearrange("p a (g n) -> p (a g) n", n=P)
        v_rep = gate_b
        kv_prod = acc
        kv_sum = hid[:, 0:2]
        qkv_sum = hid[:, 2:4]
        ones_row = spare[:, 6]
        la_carry = sb("la_carry", [P, GROUPS])
        yT_la = spare[:, 7]

        def la_sems():
            return ln_sems(4) | {k: sem(f"la_{k}") for k in (
                "picks", "picks_r", "qkv_in", "qkv_hi", "qkv_lo", "v_in", "k_in", "q_in", "v_out", "kv_out", "q_out",
                "summed", "y_out", "o_in", "tile_done")}

        TPS = SEQ // TW
        V_CREDIT, ONES_CREDIT = 2, 1

        def la_pe(pe, s):
            def take_tile(i):
                pe.wait_ge(s["xn_ready"], i + 1)
                turn(pe, bank[7], lambda b: xn[:, b]).then_inc(s["xn_turned"], 1)

            def project(i, k):
                pe.wait_ge(s["xT_ready"], i + 1) if k == 0 else pe.wait_ge(s["qkv_hi"], 3 * i + k)
                nc.tensor.matmul(bank[7][:], (wv, wk, wq)[k], xT[:], start=True, stop=True).then_inc(s["qkv_in"], 1)

            def tile_of(i, half):
                def onto(dst, pick_m, k):
                    nc.tensor.matmul(dst, pick_m, qkv_hi[:, 3 * half + k], start=True, stop=False)
                    return nc.tensor.matmul(dst, pick_m, qkv_lo[:, 3 * half + k], start=False, stop=True)

                def sums(g):
                    pe.wait_ge(s["q_out"], i * GROUPS + g + 1 + V_CREDIT)
                    nc.tensor.matmul(bank[6][:], gather_p[:, g], qkv_sum[:, g % 2], start=(g == 0), stop=(g == GROUPS - 1),
                                     skip_group_check=True).then_inc(s["summed"], 1)

                pe.wait_ge(s["qkv_lo"], 3 * i + 3)
                for g in range(GROUPS):
                    pe.wait_ge(s["v_out"], i * GROUPS + g - 1 + V_CREDIT)
                    onto(bank[g % 2][:], pick_v[:, g], 0).then_inc(s["v_in"], 1)
                    pe.wait_ge(s["kv_out"], i * GROUPS + g - 1 + V_CREDIT)
                    onto(bank[2 + g % 2][:], pick_kq[:, g], 1).then_inc(s["k_in"], 1)
                    pe.wait_ge(s["q_out"], i * GROUPS + g - 1 + V_CREDIT)
                    onto(bank[4 + g % 2][:], pick_kq[:, g], 2).then_inc(s["q_in"], 1)
                    if g == 2:
                        pe.wait_ge(s["tile_done"], i + ONES_CREDIT)
                    if g >= 2:
                        sums(g - 2)
                    if g == 3:
                        take_tile(i + 1)
                    if g >= 5:
                        project(i + 1, g - 5)
                sums(GROUPS - 2)
                sums(GROUPS - 1)
                pe.wait_ge(s["y_out"], i + 1)
                for b in range(TB):
                    ins = nc.tensor.matmul(blk(bank[6], b), blk(yT_la, b), wo, start=True, stop=True)
                ins.then_inc(s["o_in"], 1)

            take_tile(0)
            for k in range(3):
                project(0, k)
            pe.wait_ge(s["picks_r"], 2)
            with pe.Fori(0, BATCHES) as q:
                for half in range(TPS):
                    tile_of(q * TPS + half, half)

        def la_act(act, steps, s):
            act.sem_inc(s["v_out"], V_CREDIT)

            def take_tile(i):
                act.wait_ge(s["xn_turned"], i + 1)
                nc.scalar.copy(xT[:], bank[7][:]).then_inc(s["xT_ready"], 1)

            def split_projection(i, half, k):
                act.wait_ge(s["qkv_in"], 3 * i + k + 1)
                if not (isinstance(i, int) and i == 0):
                    act.wait_ge(s["qkv_lo"], 3 * i - 3 + k + 1)
                nc.scalar.activation(qkvT[:, k], bank[7][:], ACT.Identity, bias=(bv, bk, bq)[k])
                nc.scalar.activation(qkv_hi[:, 3 * half + k], bank[7][:], ACT.Identity, bias=(bv, bk, bq)[k]).then_inc(s["qkv_hi"], 1)

            def tile_of(i, half):
                for g in range(GROUPS):
                    act.wait_ge(s["v_in"], i * GROUPS + g + 1)
                    act.wait_ge(s["kv_out"], i * GROUPS + g - 1 + V_CREDIT)
                    nc.scalar.copy(v_rep[:, g % 2], bank[g % 2][:]).then_inc(s["v_out"], 1)
                    if g == 3:
                        take_tile(i + 1)
                    if g >= 5:
                        split_projection(i + 1, 1 - half, g - 5)
                act.wait_ge(s["summed"], (i + 1) * GROUPS)
                nc.scalar.copy(yT_la, bank[6][:]).then_inc(s["y_out"], 1)

            take_tile(0)
            act.wait_ge(s["picks_r"], 2)
            for k in range(3):
                split_projection(0, 0, k)
            with act.Fori(0, BATCHES) as q:
                for half in range(TPS):
                    tile_of(q * TPS + half, half)

        def la_pool(pool, steps, s):
            g = nc.gpsimd
            ln_rstd(pool, steps, s, 0)
            kq = pick_f32[:, 0:GROUPS * P]
            vv = pick_f32[:, GROUPS * P:2 * GROUPS * P]
            pool.wait_ge(w_lo_ready, MLPS)
            g.memset(ones_row, 1.0)
            g.memset(kq, 0.0)
            g.memset(vv, 0.0)
            steps.link(g.memset(gather_p, 1.0))
            g.affine_select(kq.rearrange("f (g h p n) -> f g h p n", g=GROUPS, h=2, p=HD), kq.rearrange("f (g h p n) -> f g h p n", g=GROUPS, h=2, p=HD),
                            [[-2 * HD, GROUPS], [-HD, 2], [0, HD], [-1, HD]], ALU.not_equal, 1.0, base=0, channel_multiplier=1)
            g.affine_select(vv.rearrange("f (g h p n) -> f g h p n", g=GROUPS, h=2, p=HD), vv.rearrange("f (g h p n) -> f g h p n", g=GROUPS, h=2, p=HD),
                            [[-2 * HD, GROUPS], [-HD, 2], [-1, HD], [0, HD]], ALU.not_equal, 1.0, base=0, channel_multiplier=1)\
                .then_inc(s["picks"], 1)
            steps.link(g.affine_select(gather_p, gather_p, [[2 * HD * HD, GROUPS], [-HD, P]], ALU.is_ge, 0.0, base=0, channel_multiplier=1))
            g.affine_select(gather_p, gather_p, [[-2 * HD * HD, GROUPS], [HD, P]], ALU.is_ge, 0.0, base=HD - 1, channel_multiplier=-1)\
                .then_inc(s["picks"], 1)
            with pool.Fori(1, TILES + 1) as i:
                steps.enter(i - 1, 1)
                ln_rstd(pool, steps, s, i)
            steps.leave(TILES)

        def la_dve(dve, steps, s):
            v = nc.vector
            dve.sem_inc(s["kv_out"], V_CREDIT)
            dve.sem_inc(s["q_out"], V_CREDIT)
            dve.sem_inc(s["tile_done"], ONES_CREDIT)
            steps.done(v.memset(la_carry[:], 0.0))

            def rest_of_projection(i, half, k):
                dve.wait_ge(s["qkv_hi"], 3 * i + k + 1)
                v.tensor_tensor(qkv_lo[:, 3 * half + k], qkvT[:, k], qkv_hi[:, 3 * half + k].bitcast(F32), ALU.subtract)\
                    .then_inc(s["qkv_lo"], 1)

            def tile_of(i, half):
                def through_q(g):
                    dve.wait_ge(s["q_in"], i * GROUPS + g + 1)
                    if g >= 2:
                        dve.wait_ge(s["summed"], i * GROUPS + g - 1)
                    v.tensor_tensor(qkv_sum[:, g % 2], bank[4 + g % 2][:], kv_sum[:, g % 2], ALU.mult).then_inc(s["q_out"], 1)

                for g in range(GROUPS):
                    dve.wait_ge(s["v_out"], i * GROUPS + g + 1 + V_CREDIT)
                    dve.wait_ge(s["k_in"], i * GROUPS + g + 1)
                    v.tensor_tensor(kv_prod[:], bank[2 + g % 2][:], v_rep[:, g % 2], ALU.mult).then_inc(s["kv_out"], 1)
                    if g >= 1:
                        through_q(g - 1)
                    dve.wait_ge(s["kv_out"], i * GROUPS + g + 1 + V_CREDIT)
                    steps.link(v.tensor_tensor_scan(kv_sum[:, g % 2], ones_row, kv_prod[:], la_carry[:, g:g + 1], ALU.mult, ALU.add))
                    steps.done(v.tensor_scalar(la_carry[:, g:g + 1], kv_sum[:, g % 2, TW - 1:TW], keep[:, bass.ds(i + 1, 1)], None, ALU.mult))
                    if g == 0:
                        ln_stats(dve, steps, s, i + 1)
                    if g == 2:
                        ln_apply(dve, steps, s, i + 1)
                    if g >= 6:
                        rest_of_projection(i + 1, 1 - half, g - 6)
                through_q(GROUPS - 1)
                rest_of_projection(i + 1, 1 - half, 2)
                dve.wait_ge(s["o_in"], i + 1)
                tile = X[:, bass.ds(i * TB, TB)]
                steps.link(v.tensor_tensor(tile, tile, bo_row.unsqueeze(1).broadcast_to([P, TB, P]), ALU.add))
                v.tensor_tensor(tile, bank[6][:].rearrange("p (b e) -> p b e", b=TB), tile, ALU.add).then_inc(s["tile_done"], 1)

            ln_stats(dve, steps, s, 0)
            ln_apply(dve, steps, s, 0, first=True)
            dve.wait_ge(s["picks"], 2)
            v.tensor_copy(hid_hi[:, 6:8].rearrange("p a t -> p (a t)"), pick_f32[:, 0:GROUPS * P]).then_inc(s["picks_r"], 1)
            v.tensor_copy(hid_lo[:, 6:8].rearrange("p a t -> p (a t)"), pick_f32[:, GROUPS * P:2 * GROUPS * P]).then_inc(s["picks_r"], 1)
            for k in range(3):
                rest_of_projection(0, 0, k)
            with dve.Fori(0, BATCHES) as q:
                steps.enter(q, TPS * LA_STEPS)
                for half in range(TPS):
                    tile_of(q * TPS + half, half)
            steps.leave(BATCHES)
            dve.wait_ge(s["tile_done"], TILES + ONES_CREDIT)
            dve.sem_inc(phase_done, 1)

        LA_STEPS = 18

        moe_s = [moe_sems(0), moe_sems(2)]
        mix_s = [mix_sems()]
        tf_s = [tf_sems(3), tf_sems(5)]
        la_s = [la_sems()]
        block = ctx.enter_context(nc.Block())

        @block.sync
        def _(sp):
            x_in = t["x"].rearrange("(n p) d -> p n d", p=P)
            sp.dma_start(cols[:], t["cols"]).then_inc(early_dma, 16)
            sp.dma_start(rows[:], t["rows"].partition_broadcast(P)).then_inc(early_dma, 16)
            for dst, name in early_loads[1:]:
                sp.dma_start(dst[:], t[name]).then_inc(early_dma, 16)
            sp.dma_start(X[:, 0:TB], x_in[:, 0:TB]).then_inc(x_first_dma, 16)
            for e in range(MLPS):
                if e == STAGES:
                    sp.dma_start(X[:, TB:BLOCKS], x_in[:, TB:]).then_inc(x_rest_dma, 16)
                if e >= STAGES:
                    sp.wait_ge(w_lo_ready, e - STAGES + 1)
                sp.dma_start(w_stage[:, e % STAGES], t["w_mlp"][e]).then_inc(w_in[e % STAGES], 16)
            for dst, name in late_loads:
                sp.dma_start(dst[:], t[name]).then_inc(c_dma, 16)
            sp.wait_ge(phase_done, 6)
            sp.dma_start(t["out"].rearrange("(n p) d -> p n d", p=P), X[:, 0:BLOCKS]).then_inc(stored, 16)
            sp.wait_ge(stored, 16)

        CONSTS = 9

        @block.gpsimd
        def _(pool):
            steps = Steps(pool, pool_steps_sem, waits_apart)
            g = nc.gpsimd
            g.memset(neg_half[:], -0.5).then_inc(const_ready, 1)
            g.memset(ones[:], 1.0 / P).then_inc(const_ready, 1)
            g.memset(X_before[:, 0:TB], 0.0)
            g.memset(X[:, BLOCKS:], 0.0).then_inc(const_ready, 1)
            g.iota(expert_no[:], [[1, EXPERTS]], base=0, channel_multiplier=0,
                   allow_small_or_imprecise_dtypes=True).then_inc(const_ready, 1)
            g.memset(ident[:], 0.0)
            g.memset(same_head[:], 1.0)
            g.memset(head_of[:], 1.0)
            steps.link(g.memset(keep[:], 1.0))
            g.affine_select(ident[:], ident[:], [[-1, P]], ALU.not_equal, 1.0, base=0, channel_multiplier=1).then_inc(const_ready, 1)
            sh = same_head[:].rearrange("n (h d) -> n h d", d=HD)
            steps.link(g.affine_select(sh, sh, [[-HD, LH], [0, HD]], ALU.is_ge, 0.0, base=0, channel_multiplier=1))
            g.affine_select(sh, sh, [[HD, LH], [0, HD]], ALU.is_ge, 0.0, base=HD - 1, channel_multiplier=-1).then_inc(const_ready, 1)
            pool.wait_ge(const_ready, 6)
            g.tensor_tensor(head_of[:], same_head[:].rearrange("n (a j d) -> n a j d", j=4, d=HD)[:, 0, :, 0],
                            same_head[:].rearrange("n (a j d) -> n a j d", j=4, d=HD)[:, 1, :, 0], ALU.add).then_inc(const_ready, 1)
            pool.wait_ge(const_ready, 7)
            for a in range(2, 4):
                ins = g.tensor_tensor(head_of[:], head_of[:],
                                      same_head[:].rearrange("n (a j d) -> n a j d", j=4, d=HD)[:, a, :, 0], ALU.add)
                if a == 2:
                    steps.link(ins)
            ins.then_inc(const_ready, 1)
            g.memset(keep[:, 0:TILES:2], 0.0).then_inc(const_ready, 1)
            moe_pool(pool, steps, moe_s[0])
            pool.wait_ge(phase_done, 1)
            mix_pool(pool, steps, mix_s[0])
            pool.wait_ge(phase_done, 2)
            moe_pool(pool, steps, moe_s[1])
            pool.wait_ge(phase_done, 3)
            tf_pool(pool, steps, tf_s[0])
            pool.wait_ge(phase_done, 4)
            la_pool(pool, steps, la_s[0])
            pool.wait_ge(phase_done, 5)
            tf_pool(pool, steps, tf_s[1])

        @block.tensor
        def _(pe):
            pe.wait_ge(const_ready, CONSTS)
            pe.wait_ge(early_dma, EARLY)
            phase_setup_pe(pe)
            moe_pe(pe, moe_s[0])
            pe.wait_ge(phase_done, 1)
            pe.wait_ge(c_dma, LATE)
            mix_pe(pe, mix_s[0])
            pe.wait_ge(phase_done, 2)
            moe_pe(pe, moe_s[1])
            pe.wait_ge(phase_done, 3)
            tf_pe(pe, tf_s[0])
            pe.wait_ge(phase_done, 4)
            la_pe(pe, la_s[0])
            pe.wait_ge(phase_done, 5)
            tf_pe(pe, tf_s[1])

        @block.scalar
        def _(act):
            steps = Steps(act, act_steps_sem, waits_apart)
            act.wait_ge(const_ready, CONSTS)
            act.wait_ge(early_dma, EARLY)
            moe_act(act, steps, moe_s[0])
            act.wait_ge(phase_done, 1)
            act.wait_ge(c_dma, LATE)
            mix_act(act, steps, mix_s[0])
            act.wait_ge(phase_done, 2)
            moe_act(act, steps, moe_s[1])
            act.wait_ge(phase_done, 3)
            tf_act(act, steps, tf_s[0])
            act.wait_ge(phase_done, 4)
            la_act(act, steps, la_s[0])
            act.wait_ge(phase_done, 5)
            tf_act(act, steps, tf_s[1])

        @block.vector
        def _(dve):
            steps = Steps(dve, dve_steps_sem, waits_apart)
            dve.wait_ge(const_ready, CONSTS)
            dve.wait_ge(early_dma, EARLY)
            phase_setup_dve(dve, steps)
            moe_dve(dve, steps, moe_s[0])
            dve.wait_ge(phase_done, 1)
            dve.wait_ge(c_dma, LATE)
            mix_dve(dve, steps, mix_s[0])
            dve.wait_ge(phase_done, 2)
            moe_dve(dve, steps, moe_s[1])
            dve.wait_ge(phase_done, 3)
            tf_dve(dve, steps, tf_s[0])
            dve.wait_ge(phase_done, 4)
            la_dve(dve, steps, la_s[0])
            dve.wait_ge(phase_done, 5)
            tf_dve(dve, steps, tf_s[1])


def kernel(**inputs):
    import numpy as np
    from concourse.bacc import Bacc
    from concourse.bass_utils import run_bass_kernel_spmd

    a = {k: np.asarray(v) for k, v in inputs.items()}
    HC, W = a["L0_ffn_Wfc_s"].shape[1] // P, P
    att, ffn, la, tf = (lambda k: a["L0_attn_" + k]), (lambda k: a["L0_ffn_" + k]), (lambda k: a["L1_attn_" + k]), (lambda k: a["L1_ffn_" + k])
    mlps = lambda s, e: np.concatenate([s[None], e])
    chunked = lambda w: w.reshape(-1, HC, P, W)
    cols = [
        mlps(ffn("bfc_s"), ffn("bfc")).reshape(-1, P), mlps(ffn("bproj_s"), ffn("bproj")), ffn("Wr").T,
        att("Wa_b"), att("Wb_b"), att("C_b"), att("D_b")[None], att("hn_g"), att("hn_b"),
        att("ffn1_b").reshape(HC, P), att("ffn2_b")[None], la("bq")[None], la("bk")[None], tf("b1").reshape(HC, P), tf("b2")[None], la("bv")[None]]
    laid = {
        "x": a["L0_attn_emb"].reshape(-1, W),
        "w_mlp": np.concatenate([mlps(ffn("Wfc_s"), ffn("Wfc")), chunked(mlps(ffn("Wproj_s"), ffn("Wproj"))).transpose(0, 2, 1, 3)
                                 .reshape(-1, P, HC * W)], 2),
        "wa": att("Wa_w").transpose(2, 0, 1), "wb": att("Wb_w").transpose(2, 0, 1), "cw": att("C_w").transpose(2, 0, 1),
        "squares": np.stack([w.T for w in (att("D_w"), att("Wout_w"), att("proj_w"), la("Wq"), la("Wk"), la("Wv"), la("Wo"))], 1),
        "f1": att("ffn1_w").T, "f2": chunked(att("ffn2_w").T)[0].transpose(1, 0, 2),
        "w1": tf("W1").T, "w2": chunked(tf("W2").T)[0].transpose(1, 0, 2),
        "cols": np.concatenate(cols).T,
        "rows": np.concatenate([att("Wout_b"), att("proj_b"), att("norm_g"), att("norm_b"), la("bk"), la("bv"), la("bo"), att("head_w")]),
    }
    nc = Bacc("TRN2", target_bir_lowering=False, num_devices=1)
    arrays, t = {}, {}
    for name, v in laid.items():
        arrays["in_" + name] = np.ascontiguousarray(v)
        t[name] = nc.dram_tensor("in_" + name, v.shape, F32, kind="ExternalInput").ap()
    t["out"] = nc.dram_tensor("out_x", laid["x"].shape, F32, kind="ExternalOutput").ap()
    macaron_kernel(nc, t)
    got = run_bass_kernel_spmd(nc, [arrays], core_ids=[0]).results[0]["out_x"]
    return got.reshape(a["L0_attn_emb"].shape)
```
